# Optimizing a Trainium2 kernel written in Bass

```python
import numpy as np
import jax
import jax.numpy as jnp

def _softmax(x, axis=-1):
    return jax.nn.softmax(x, axis=axis)

def _gelu(x):
    return jax.nn.gelu(x, approximate=True)

def _silu(x):
    return jax.nn.silu(x)

def _sigmoid(x):
    return jax.nn.sigmoid(x)

def _layernorm(x, axis=-1, eps=1e-05):
    m = jnp.mean(x, axis=axis, keepdims=True)
    v = jnp.var(x, axis=axis, keepdims=True)
    return (x - m) / jnp.sqrt(v + eps)

def _scatter_add(tgt, idx, src, axis=0):
    return tgt.at[idx].add(src)

def _segment_sum(src, seg, n):
    return jax.ops.segment_sum(src, seg, n)
kernel_name = 'mk_gnn_resnorm_d4_gnn_r32_2c5299'

def setup_inputs(seed: int=0):
    np.random.seed(seed)
    _w = jnp.asarray

    def _rec_inputs():
        import jax
        import jax.numpy as jnp
        _gk = jax.random.key(seed)
        x = -0.0003713 + 1 * jax.random.normal(jax.random.fold_in(_gk, 1), (3125, 128), jnp.float32)
        src = jax.random.randint(jax.random.fold_in(_gk, 2), (50000,), 0, 3125, jnp.int32)
        dst = jax.random.randint(jax.random.fold_in(_gk, 3), (50000,), 0, 3125, jnp.int32)
        _o = jnp.argsort(dst, stable=True)
        src = src[_o]
        dst = dst[_o]
        edge_attr_32 = 0.000283511 + 1.00007 * jax.random.normal(jax.random.fold_in(_gk, 11), (50000, 32), jnp.float32)
        edge_weight1 = jax.random.uniform(jax.random.fold_in(_gk, 13), (50000, 1), jnp.float32, 0.0, 0.999998)
        return (x, src, dst, edge_attr_32, edge_weight1)
    x, src, dst, edge_attr_32, edge_weight1 = _rec_inputs()

    def _L0_gnn_setup():
        import jax, jax.numpy as jnp
        import numpy as np
        N, E, D, H = (3125, 50000, 128, 2)
        NEG_SLOPE = 0.2
        EPS = 1e-16

        def _segment_softmax(alpha, seg, num_segments):
            m = jax.ops.segment_max(alpha, seg, num_segments=num_segments)
            a = jnp.exp(alpha - m[seg])
            z = jax.ops.segment_sum(a, seg, num_segments=num_segments)
            return a / (z[seg] + EPS)
        key = jax.random.key(seed)
        ks = jax.random.split(key, 12)
        s = 1.0 / np.sqrt(D)
        return {'x': jax.random.normal(ks[0], (N, D), jnp.float32), 'edge_index': jax.random.randint(ks[1], (2, E), 0, N, jnp.int64), 'gamma': jnp.ones((D,), jnp.float32), 'beta': jnp.zeros((D,), jnp.float32), 'Wl': jax.random.normal(ks[2], (D, H * D), jnp.float32) * s, 'bl': jnp.zeros((H * D,), jnp.float32), 'Wr': jax.random.normal(ks[3], (D, H * D), jnp.float32) * s, 'br': jnp.zeros((H * D,), jnp.float32), 'att': jax.random.normal(ks[4], (H, D), jnp.float32) * s, 'res_W': jax.random.normal(ks[5], (D, D), jnp.float32) * s, 'bias': jnp.zeros((D,), jnp.float32)}
    _L0_gnn_all = _L0_gnn_setup()
    _L0_gnn_in = {k: v for k, v in _L0_gnn_all.items() if k in ('gamma', 'beta', 'Wl', 'bl', 'Wr', 'br', 'att', 'res_W', 'bias')}
    del _L0_gnn_all

    def _L1_gnn_setup():
        import jax, jax.numpy as jnp
        import numpy as np
        N_NODES = 50000
        N_EDGES = 20000
        D = 128
        BN_EPS = 1e-05
        NEG_SLOPE = 0.2

        def _gatv2(x, edge_index, edge_attr, Wl, bl, Wr, br, We, att, bias_out):
            src, dst = (edge_index[0], edge_index[1])
            xl = x @ Wl + bl
            xr = x @ Wr + br
            e = edge_attr @ We
            m = xl[src] + xr[dst] + e
            m = jax.nn.leaky_relu(m, NEG_SLOPE)
            logits = m @ att
            n = x.shape[0]
            mx = jax.ops.segment_max(logits, dst, num_segments=n)
            ex = jnp.exp(logits - mx[dst])
            den = jax.ops.segment_sum(ex, dst, num_segments=n)
            alpha = ex / (den[dst] + 1e-16)
            out = jax.ops.segment_sum(xl[src] * alpha[:, None], dst, num_segments=n)
            return out + bias_out
        key = jax.random.key(seed)
        ks = jax.random.split(key, 8)
        s = 1.0 / np.sqrt(D)
        x = jax.random.normal(ks[0], (N_NODES, D), dtype=jnp.float32)
        edge_index = jax.random.randint(ks[1], (2, N_EDGES), 0, N_NODES, dtype=jnp.int32)
        edge_attr = jax.random.uniform(ks[2], (N_EDGES, 1), dtype=jnp.float32)
        Wl = jax.random.normal(ks[3], (D, D), dtype=jnp.float32) * s
        Wr = jax.random.normal(ks[4], (D, D), dtype=jnp.float32) * s
        We = jax.random.normal(ks[5], (1, D), dtype=jnp.float32) * s
        att = jax.random.normal(ks[6], (D,), dtype=jnp.float32) * s
        return {'x': x, 'edge_index': edge_index, 'edge_attr': edge_attr, 'Wl': Wl, 'bl': jnp.zeros((D,), jnp.float32), 'Wr': Wr, 'br': jnp.zeros((D,), jnp.float32), 'We': We, 'att': att, 'bias_out': jnp.zeros((D,), jnp.float32), 'bn_gamma': jnp.ones((D,), jnp.float32), 'bn_beta': jnp.zeros((D,), jnp.float32)}
    _L1_gnn_all = _L1_gnn_setup()
    _L1_gnn_in = {k: v for k, v in _L1_gnn_all.items() if k in ('Wl', 'bl', 'Wr', 'br', 'We', 'att', 'bias_out', 'bn_gamma', 'bn_beta')}
    del _L1_gnn_all

    def _L2_gnn_setup():
        import jax, jax.numpy as jnp
        import numpy as np
        N_NODES = 50000
        N_EDGES = 18750
        D = 128
        EDGE_D = 32
        N_LAYERS = 3
        BN_EPS = 1e-05
        key = jax.random.key(seed)
        ks = jax.random.split(key, 8)
        x = jax.random.normal(ks[0], (N_NODES, D), dtype=jnp.float32)
        edge_index = jax.random.randint(ks[1], (2, N_EDGES), 0, N_NODES, dtype=jnp.int64)
        edge_attr = jax.random.normal(ks[2], (N_EDGES, EDGE_D), dtype=jnp.float32)
        W_lin = jax.random.normal(ks[3], (N_LAYERS, EDGE_D, D), dtype=jnp.float32) * 0.05
        b_lin = jnp.zeros((N_LAYERS, D), dtype=jnp.float32)
        W1 = jax.random.normal(ks[4], (N_LAYERS, D, D), dtype=jnp.float32) * 0.05
        b1 = jnp.zeros((N_LAYERS, D), dtype=jnp.float32)
        W2 = jax.random.normal(ks[5], (N_LAYERS, D, D), dtype=jnp.float32) * 0.05
        b2 = jnp.zeros((N_LAYERS, D), dtype=jnp.float32)
        gamma = jnp.ones((N_LAYERS, D), dtype=jnp.float32)
        beta = jnp.zeros((N_LAYERS, D), dtype=jnp.float32)
        return {'x': x, 'edge_index': edge_index, 'edge_attr': edge_attr, 'W_lin': W_lin, 'b_lin': b_lin, 'W1': W1, 'b1': b1, 'W2': W2, 'b2': b2, 'gamma': gamma, 'beta': beta}
    _L2_gnn_all = _L2_gnn_setup()
    _L2_gnn_in = {k: v for k, v in _L2_gnn_all.items() if k in ('W_lin', 'b_lin', 'W1', 'b1', 'W2', 'b2', 'gamma', 'beta')}
    del _L2_gnn_all

    def _L3_gnn_setup():
        import jax, jax.numpy as jnp
        import numpy as np
        N, E = (50000, 25000)
        ND, ED, HD = (128, 32, 256)
        LN_EPS = 1e-05
        key = jax.random.key(seed)
        ks = jax.random.split(key, 16)
        s = lambda d: 1.0 / np.sqrt(d)
        return {'x': jax.random.normal(ks[0], (N, ND), dtype=jnp.float32), 'edge_index': jax.random.randint(ks[1], (2, E), 0, N, dtype=jnp.int64), 'edge_attr': jax.random.normal(ks[2], (E, ED), dtype=jnp.float32), 'W1': jax.random.normal(ks[3], (2 * ND + ED, HD), dtype=jnp.float32) * s(2 * ND + ED), 'b1': jnp.zeros((HD,), dtype=jnp.float32), 'W2': jax.random.normal(ks[4], (HD, HD), dtype=jnp.float32) * s(HD), 'b2': jnp.zeros((HD,), dtype=jnp.float32), 'W3': jax.random.normal(ks[5], (HD, ND), dtype=jnp.float32) * s(HD), 'b3': jnp.zeros((ND,), dtype=jnp.float32), 'Wn1': jax.random.normal(ks[6], (2 * ND, HD), dtype=jnp.float32) * s(2 * ND), 'bn1': jnp.zeros((HD,), dtype=jnp.float32), 'Wn2': jax.random.normal(ks[7], (HD, ND), dtype=jnp.float32) * s(HD), 'bn2': jnp.zeros((ND,), dtype=jnp.float32), 'gamma': jnp.ones((ND,), dtype=jnp.float32), 'beta': jnp.zeros((ND,), dtype=jnp.float32)}
    _L3_gnn_all = _L3_gnn_setup()
    _L3_gnn_in = {k: v for k, v in _L3_gnn_all.items() if k in ('W1', 'b1', 'W2', 'b2', 'W3', 'b3', 'Wn1', 'bn1', 'Wn2', 'bn2', 'gamma', 'beta')}
    del _L3_gnn_all
    return {'x': x, 'src': src, 'dst': dst, 'edge_attr_32': edge_attr_32, 'edge_weight1': edge_weight1, 'L0_gnn_gamma': _L0_gnn_in['gamma'], 'L0_gnn_beta': _L0_gnn_in['beta'], 'L0_gnn_Wl': _L0_gnn_in['Wl'], 'L0_gnn_bl': _L0_gnn_in['bl'], 'L0_gnn_Wr': _L0_gnn_in['Wr'], 'L0_gnn_br': _L0_gnn_in['br'], 'L0_gnn_att': _L0_gnn_in['att'], 'L0_gnn_res_W': _L0_gnn_in['res_W'], 'L0_gnn_bias': _L0_gnn_in['bias'], 'L1_gnn_Wl': _L1_gnn_in['Wl'], 'L1_gnn_bl': _L1_gnn_in['bl'], 'L1_gnn_Wr': _L1_gnn_in['Wr'], 'L1_gnn_br': _L1_gnn_in['br'], 'L1_gnn_We': _L1_gnn_in['We'], 'L1_gnn_att': _L1_gnn_in['att'], 'L1_gnn_bias_out': _L1_gnn_in['bias_out'], 'L1_gnn_bn_gamma': _L1_gnn_in['bn_gamma'], 'L1_gnn_bn_beta': _L1_gnn_in['bn_beta'], 'L2_gnn_W_lin': _L2_gnn_in['W_lin'], 'L2_gnn_b_lin': _L2_gnn_in['b_lin'], 'L2_gnn_W1': _L2_gnn_in['W1'], 'L2_gnn_b1': _L2_gnn_in['b1'], 'L2_gnn_W2': _L2_gnn_in['W2'], 'L2_gnn_b2': _L2_gnn_in['b2'], 'L2_gnn_gamma': _L2_gnn_in['gamma'], 'L2_gnn_beta': _L2_gnn_in['beta'], 'L3_gnn_W1': _L3_gnn_in['W1'], 'L3_gnn_b1': _L3_gnn_in['b1'], 'L3_gnn_W2': _L3_gnn_in['W2'], 'L3_gnn_b2': _L3_gnn_in['b2'], 'L3_gnn_W3': _L3_gnn_in['W3'], 'L3_gnn_b3': _L3_gnn_in['b3'], 'L3_gnn_Wn1': _L3_gnn_in['Wn1'], 'L3_gnn_bn1': _L3_gnn_in['bn1'], 'L3_gnn_Wn2': _L3_gnn_in['Wn2'], 'L3_gnn_bn2': _L3_gnn_in['bn2'], 'L3_gnn_gamma': _L3_gnn_in['gamma'], 'L3_gnn_beta': _L3_gnn_in['beta']}

def reference(x, src, dst, edge_attr_32, edge_weight1, L0_gnn_gamma, L0_gnn_beta, L0_gnn_Wl, L0_gnn_bl, L0_gnn_Wr, L0_gnn_br, L0_gnn_att, L0_gnn_res_W, L0_gnn_bias, L1_gnn_Wl, L1_gnn_bl, L1_gnn_Wr, L1_gnn_br, L1_gnn_We, L1_gnn_att, L1_gnn_bias_out, L1_gnn_bn_gamma, L1_gnn_bn_beta, L2_gnn_W_lin, L2_gnn_b_lin, L2_gnn_W1, L2_gnn_b1, L2_gnn_W2, L2_gnn_b2, L2_gnn_gamma, L2_gnn_beta, L3_gnn_W1, L3_gnn_b1, L3_gnn_W2, L3_gnn_b2, L3_gnn_W3, L3_gnn_b3, L3_gnn_Wn1, L3_gnn_bn1, L3_gnn_Wn2, L3_gnn_bn2, L3_gnn_gamma, L3_gnn_beta):
    import jax
    import jax.numpy as jnp

    def _L0_gnn_ref(x, edge_index, gamma, beta, Wl, bl, Wr, br, att, res_W, bias):
        import jax, jax.numpy as jnp
        import numpy as np
        N, E, D, H = (3125, 50000, 128, 2)
        NEG_SLOPE = 0.2
        EPS = 1e-16

        def _segment_softmax(alpha, seg, num_segments):
            m = jax.ops.segment_max(alpha, seg, num_segments=num_segments)
            a = jnp.exp(alpha - m[seg])
            z = jax.ops.segment_sum(a, seg, num_segments=num_segments)
            return a / (z[seg] + EPS)
        n = x.shape[0]
        residual = x
        mu = x.mean(-1, keepdims=True)
        var = ((x - mu) ** 2).mean(-1, keepdims=True)
        h = (x - mu) * jax.lax.rsqrt(var + 1e-05) * gamma + beta
        h = jax.nn.relu(h)
        xl = (h @ Wl + bl).reshape(n, H, D)
        xr = (h @ Wr + br).reshape(n, H, D)
        src, dst = (edge_index[0], edge_index[1])
        e = jax.nn.leaky_relu(xl[src] + xr[dst], NEG_SLOPE)
        alpha = jnp.einsum('ehd,hd->eh', e, att)
        alpha = _segment_softmax(alpha, dst, n)
        msg = xl[src] * alpha[..., None]
        out = jax.ops.segment_sum(msg, dst, num_segments=n)
        out = out.mean(axis=1)
        out = out + h @ res_W + bias
        return residual + out

    def _L1_gnn_ref(x, edge_index, edge_attr, Wl, bl, Wr, br, We, att, bias_out, bn_gamma, bn_beta):
        import jax, jax.numpy as jnp
        import numpy as np
        N_NODES = 50000
        N_EDGES = 20000
        D = 128
        BN_EPS = 1e-05
        NEG_SLOPE = 0.2

        def _gatv2(x, edge_index, edge_attr, Wl, bl, Wr, br, We, att, bias_out):
            src, dst = (edge_index[0], edge_index[1])
            xl = x @ Wl + bl
            xr = x @ Wr + br
            e = edge_attr @ We
            m = xl[src] + xr[dst] + e
            m = jax.nn.leaky_relu(m, NEG_SLOPE)
            logits = m @ att
            n = x.shape[0]
            mx = jax.ops.segment_max(logits, dst, num_segments=n)
            ex = jnp.exp(logits - mx[dst])
            den = jax.ops.segment_sum(ex, dst, num_segments=n)
            alpha = ex / (den[dst] + 1e-16)
            out = jax.ops.segment_sum(xl[src] * alpha[:, None], dst, num_segments=n)
            return out + bias_out
        h = x + _gatv2(x, edge_index, edge_attr, Wl, bl, Wr, br, We, att, bias_out)
        h = jax.nn.gelu(h, approximate=False)
        mean = jnp.mean(h, axis=0)
        var = jnp.mean((h - mean) ** 2, axis=0)
        h = (h - mean) * jax.lax.rsqrt(var + BN_EPS) * bn_gamma + bn_beta
        return h

    def _L2_gnn_ref(x, edge_index, edge_attr, W_lin, b_lin, W1, b1, W2, b2, gamma, beta):
        import jax, jax.numpy as jnp
        import numpy as np
        N_NODES = 50000
        N_EDGES = 18750
        D = 128
        EDGE_D = 32
        N_LAYERS = 3
        BN_EPS = 1e-05
        src, dst = (edge_index[0], edge_index[1])
        n = x.shape[0]
        for l in range(W1.shape[0]):
            e = edge_attr @ W_lin[l] + b_lin[l]
            msg = jax.nn.relu(x[src] + e)
            agg = jax.ops.segment_sum(msg, dst, num_segments=n)
            h = x + agg
            h = jax.nn.relu(h @ W1[l] + b1[l]) @ W2[l] + b2[l]
            mu = jnp.mean(h, axis=0)
            var = jnp.var(h, axis=0)
            h = (h - mu) * jax.lax.rsqrt(var + BN_EPS) * gamma[l] + beta[l]
            x = jax.nn.relu(h)
        return x

    def _L3_gnn_ref(x, edge_index, edge_attr, W1, b1, W2, b2, W3, b3, Wn1, bn1, Wn2, bn2, gamma, beta):
        import jax, jax.numpy as jnp
        import numpy as np
        N, E = (50000, 25000)
        ND, ED, HD = (128, 32, 256)
        LN_EPS = 1e-05
        row, col = (edge_index[0], edge_index[1])
        ef = jnp.concatenate([x[row], x[col], edge_attr], axis=-1)
        h = jax.nn.relu(ef @ W1 + b1)
        h = jax.nn.relu(h @ W2 + b2)
        edge_out = h @ W3 + b3
        aggr = jax.ops.segment_sum(edge_out, col, num_segments=x.shape[0])
        nf = jnp.concatenate([x, aggr], axis=-1)
        node_out = jax.nn.relu(nf @ Wn1 + bn1) @ Wn2 + bn2
        y = x + node_out
        mean = jnp.mean(y, axis=-1, keepdims=True)
        var = jnp.mean(jnp.square(y - mean), axis=-1, keepdims=True)
        return (y - mean) * jax.lax.rsqrt(var + LN_EPS) * gamma + beta
    edge_index = jnp.stack([src, dst])
    x = _layernorm(x + _L0_gnn_ref(x, edge_index, L0_gnn_gamma, L0_gnn_beta, L0_gnn_Wl, L0_gnn_bl, L0_gnn_Wr, L0_gnn_br, L0_gnn_att, L0_gnn_res_W, L0_gnn_bias), axis=-1)
    x = _layernorm(x + _L1_gnn_ref(x, edge_index, edge_weight1, L1_gnn_Wl, L1_gnn_bl, L1_gnn_Wr, L1_gnn_br, L1_gnn_We, L1_gnn_att, L1_gnn_bias_out, L1_gnn_bn_gamma, L1_gnn_bn_beta), axis=-1)
    x = _layernorm(x + _L2_gnn_ref(x, edge_index, edge_attr_32, L2_gnn_W_lin, L2_gnn_b_lin, L2_gnn_W1, L2_gnn_b1, L2_gnn_W2, L2_gnn_b2, L2_gnn_gamma, L2_gnn_beta), axis=-1)
    x = _layernorm(x + _L3_gnn_ref(x, edge_index, edge_attr_32, L3_gnn_W1, L3_gnn_b1, L3_gnn_W2, L3_gnn_b2, L3_gnn_W3, L3_gnn_b3, L3_gnn_Wn1, L3_gnn_bn1, L3_gnn_Wn2, L3_gnn_bn2, L3_gnn_gamma, L3_gnn_beta), axis=-1)
    return x

_drawn_inputs = setup_inputs


def setup_inputs(seed=0):
    import zlib

    import numpy as np

    out = dict(_drawn_inputs(seed))
    spreads = {'L0_gnn_gamma': (1.0, 0.2),
     'L0_gnn_beta': (0.0, 0.1),
     'L0_gnn_bl': (0.0, 0.332),
     'L0_gnn_br': (0.0, 2.0),
     'L0_gnn_bias': (0.0, 0.1),
     'L1_gnn_bl': (0.0, 0.28),
     'L1_gnn_br': (0.0, 0.8),
     'L1_gnn_bias_out': (0.0, 0.359),
     'L1_gnn_bn_gamma': (1.0, 0.2),
     'L1_gnn_bn_beta': (0.0, 0.1),
     'L2_gnn_b_lin': (0.0, 0.1),
     'L2_gnn_b1': (0.0, 0.4),
     'L2_gnn_b2': (0.0, 2.0),
     'L2_gnn_gamma': (1.0, 0.2),
     'L2_gnn_beta': (0.0, 0.1),
     'L3_gnn_b1': (0.0, 0.1),
     'L3_gnn_b2': (0.0, 0.1),
     'L3_gnn_b3': (0.0, 0.1),
     'L3_gnn_bn1': (0.0, 0.654),
     'L3_gnn_bn2': (0.0, 0.411),
     'L3_gnn_gamma': (1.0, 0.2),
     'L3_gnn_beta': (0.0, 0.1)}
    factors = {'edge_weight1': 8.0, 'L0_gnn_Wr': 6.311, 'L0_gnn_att': 2.849, 'L1_gnn_We': 8.0}
    for name, (base, spread) in spreads.items():
        noise = np.random.default_rng([zlib.crc32(name.encode()), seed]).standard_normal(out[name].shape)
        drawn = base * np.exp(spread * noise) if base else spread * noise
        out[name] = jnp.asarray(drawn.astype(out[name].dtype))
    for name, factor in factors.items():
        out[name] = (out[name] * factor).astype(out[name].dtype)
    return out
```

```python
from contextlib import ExitStack

import numpy as np
import concourse.bass as bass
from concourse import mybir

F32 = mybir.dt.float32
BF16 = mybir.dt.bfloat16
I32 = mybir.dt.int32
ALU = mybir.AluOpType
ACT = mybir.ActivationFunctionType
AX = mybir.AxisListType.X

P = 128
NODES, EDGES, D = 3125, 50000, 128
EDGE_D, HID, HEADS, GINE_LAYERS = 32, 256, 2, 3
NODE_BLOCKS = -(-NODES // P)
NPAD = NODE_BLOCKS * P
SUBS = 4
GROUP_EDGES = SUBS * P
GROUPS = -(-EDGES // GROUP_EDGES)
ITEMS = GROUPS + NODE_BLOCKS - 1
PAIRS = ITEMS // 2
assert ITEMS % 2 == 0 and ITEMS <= P
SPLIT = 3
MASKED = -1e30
FLOOR = -1e20

C_IDENT, C_IOTA, C_ROW = 0, P, 2 * P
C_WIDTH = 2 * P + 1
BIASES = [("L0_gnn_gamma", D), ("L0_gnn_beta", D), ("L0_gnn_bl", 2 * D), ("L0_gnn_br", 2 * D),
          ("L0_gnn_bias", D), ("L1_gnn_bl", D), ("L1_gnn_br", D), ("L1_gnn_bias_out", D),
          ("L3_gnn_b1", HID), ("L3_gnn_b2", HID), ("L3_gnn_b3", D), ("L3_gnn_gamma", D),
          ("L3_gnn_beta", D)]
BIAS_AT, at = {}, 0
for _name, _n in BIASES:
    BIAS_AT[_name] = (at, _n)
    at += _n
BIAS_WIDTH = at
COLS = ["att0", "att1", "att2", "bn_gamma", "bn_beta", "bn1a", "bn1b", "bn2"]
GINE_COLS = 4
WEIGHTS = [("L0_gnn_Wl", 2 * D), ("L0_gnn_Wr", 2 * D), ("L0_gnn_res_W", D), ("L1_gnn_Wl", D),
           ("L1_gnn_Wr", D), ("L3_gnn_W1a", HID), ("L3_gnn_W1b", HID), ("L3_gnn_W2a", HID),
           ("L3_gnn_W2b", HID), ("L3_gnn_W3a", D), ("L3_gnn_W3b", D), ("L3_gnn_Wn1a", HID),
           ("L3_gnn_Wn1b", HID), ("L3_gnn_Wn2a", D), ("L3_gnn_Wn2b", D)]
WEIGHT_AT, at = {}, 0
for _name, _n in WEIGHTS:
    WEIGHT_AT[_name] = (at, _n)
    at += _n
WEIGHT_WIDTH = at


def build(nc, t):
    with ExitStack() as ctx:
        def sb(name, shape, dt=F32):
            return ctx.enter_context(nc.sbuf_tensor(name, shape, dt))

        def sem(name):
            return ctx.enter_context(nc.semaphore(name))

        def scratch(name, shape, dt=F32):
            return nc.dram_tensor(name, shape, dt, kind="Internal").ap()

        table = scratch("source_rows", (NPAD, 2 * D))
        table1 = scratch("source_rows_narrow", (NPAD, D))
        rel_rows = scratch("rel_rows", (ITEMS, GROUP_EDGES), BF16)
        weight_rows = scratch("weight_rows", (ITEMS, GROUP_EDGES))
        group_block = scratch("group_block", (ITEMS, 2), I32)

        consts = sb("consts", [P, C_WIDTH])
        ident = consts[:, C_IDENT:C_IDENT + P]
        iota = consts[:, C_IOTA:C_IOTA + P]
        row = consts[:, C_ROW:C_ROW + 1]
        bias_all = sb("bias_all", [P, BIAS_WIDTH])
        weight_all = sb("weight_all", [P, WEIGHT_WIDTH])
        cols = sb("cols", [P, len(COLS)])
        gine_cols = sb("gine_cols", [P, GINE_COLS])
        gine_w = sb("gine_w", [P, 2, D])
        gine_lin = sb("gine_lin", [EDGE_D, D])
        gine_blin = sb("gine_blin", [P, D])
        edge_w1 = sb("edge_w1", [EDGE_D, HID])
        we_row = sb("we_row", [1, D])
        att_b = sb("att_b", [P, 3, P])
        X = sb("X", [P, NODE_BLOCKS, D])
        Y = sb("Y", [P, NODE_BLOCKS, D])
        XT = sb("XT", [P, NPAD])
        TMP = sb("TMP", [P, NODE_BLOCKS, D])
        ACC = sb("ACC", [P, NODE_BLOCKS * 2 * D])
        XR = sb("XR", [P, NODE_BLOCKS, SPLIT, 2 * D], BF16)
        stage = sb("stage", [P, 4, 2 * D])
        stage_r = sb("stage_r", [P, 4, 2 * D])
        zsum = sb("zsum", [P, NODE_BLOCKS, 2])
        mmax = sb("mmax", [P, NODE_BLOCKS, 2])
        stat = sb("stat", [P, 4, NODE_BLOCKS])
        groups_blocks = sb("groups_blocks", [1, ITEMS, 2], I32)
        idx_all = sb("idx_all", [P, ITEMS, SUBS], I32)
        rel_all = sb("rel_all", [P, ITEMS, SUBS])
        idx = sb("idx", [P, 2, SUBS], I32)
        rel = sb("rel", [P, 2, GROUP_EDGES], BF16)
        wrow = sb("wrow", [1, 2, GROUP_EDGES])
        gath = sb("gath", [P, 2, SUBS, 2 * D])
        hot_t = sb("hot_t", [P, 2, GROUP_EDGES], BF16)
        hot = sb("hot", [P, 2, SUBS, P])
        neg = sb("neg", [P, 2, GROUP_EDGES], BF16)
        ea = sb("ea", [EDGE_D, 2, GROUP_EDGES])
        vs = sb("vs", [P, 2, GROUP_EDGES])
        lk = sb("lk", [P, 2, GROUP_EDGES])
        sm = sb("sm", [P, 2, GROUP_EDGES])
        pm = sb("pm", [P, 2, GROUP_EDGES])
        pt = sb("pt", [P, 2, SUBS, P])
        small = sb("small", [P, 8, 2])
        MI, MNEW, NEGM, DM, SCL, ZI = (small[:, k, :] for k in range(6))

        psum = ctx.enter_context(nc.psum_tensor("psum", [P, 8, 512], F32))

        consts_in = sem("consts_in")

        def wait(e, s, value):
            if not (isinstance(value, int) and value <= 0):
                e.wait_ge(s, value)

        def hold(e, *waits):
            waits = [(s, v if isinstance(v, int) else e.snap(e.to_reg(v))) for s, v in waits]
            e.wait_ge(consts_in, 16)
            for s, v in waits:
                wait(e, s, v)

        def pairs(e, body):
            body(0, 0, 0)
            body(1, 1, 0)
            with e.Fori(1, PAIRS) as k:
                body(2 * k, 0, k)
                body(2 * k + 1, 1, k)

        def bias(name):
            a, n = BIAS_AT[name]
            return bias_all[:, a:a + n]

        def weight(name):
            a, n = WEIGHT_AT[name]
            return weight_all[:, a:a + n]

        def col(name):
            k = COLS.index(name)
            return cols[:, k:k + 1]

        def over_blocks(v):
            return v.unsqueeze(1).broadcast_to([P, NODE_BLOCKS, v.shape[1]])

        def over_features(v):
            return v.unsqueeze(2).broadcast_to([P, NODE_BLOCKS, D])

        def setup():
            loads = sem("setup_loads")
            last_in = sem("last_in")
            dve = sem("setup_dve")
            tables_out = sem("tables_out")
            rows_in = sem("rows_in")
            pe = sem("setup_pe")
            copied = sem("setup_copied")
            with ExitStack() as mine:
                def tmp(name, shape, dt=F32):
                    return mine.enter_context(nc.sbuf_tensor(name, shape, dt))
                last_i = tmp("last_i", [ITEMS, GROUPS], I32)
                last_f = tmp("last_f", [ITEMS, GROUPS])
                gb_f = tmp("gb_f", [ITEMS, 4])
                gb_i = tmp("gb_i", [ITEMS, 2], I32)
                dst_i = tmp("dst_i", [ITEMS, GROUP_EDGES], I32)
                src_i = tmp("src_i", [ITEMS, GROUP_EDGES], I32)
                ew_i = tmp("ew_i", [ITEMS, GROUP_EDGES])
                with nc.Block() as block:
                    @block.sync
                    def _(sp):
                        sp.dma_start(consts[:, :], t["consts"]).then_inc(consts_in, 16)
                        sp.dma_start(last_i[:, :], t["dst_last"].broadcast_to([ITEMS, GROUPS])).then_inc(last_in, 16)
                        sp.dma_start(X[:, :, :], t["x"].rearrange("(b p) d -> p b d", p=P)).then_inc(loads, 16)
                        sp.dma_start(bias_all[:, :], t["biases"]).then_inc(loads, 16)
                        sp.dma_start(weight_all[:, :], t["weights"]).then_inc(loads, 16)
                        sp.dma_start(cols[:, :], t["cols"]).then_inc(loads, 16)
                        sp.dma_start(edge_w1[:, :], t["edge_w1"]).then_inc(loads, 16)
                        sp.dma_start(we_row[:, :], t["we"]).then_inc(loads, 16)
                        sp.wait_ge(dve, 8)
                        sp.dma_start(group_block, gb_i[:, :]).then_inc(tables_out, 16)
                        sp.wait_ge(tables_out, 16)
                        sp.dma_start(groups_blocks[:, :, :], group_block.unsqueeze(0)).then_inc(loads, 16)
                        sp.wait_ge(dve, 12)
                        sp.dma_start(rel_rows, rel_b[:, :]).then_inc(tables_out, 16)
                        sp.wait_ge(rows_in, 48)
                        sp.dma_start(weight_rows, ew_i[:, :]).then_inc(tables_out, 16)
                        sp.wait_ge(tables_out, 48)
                        sp.wait_ge(loads, 7 * 16)

                    @block.gpsimd
                    def _(pool):
                        pool.wait_ge(dve, 8)
                        for rows, out in ((t["dst"], dst_i), (t["src"], src_i), (t["edge_weight"], ew_i)):
                            pool.indirect_dma_start(
                                out=out[:, :], out_offset=None, in_=rows,
                                in_offset=bass.IndirectOffsetOnAxis(ap=gb_i[:, 0:1], axis=0)).then_inc(rows_in, 16)
                        pool.wait_ge(rows_in, 48)

                    @block.vector
                    def _(v):
                        n = [0]

                        def step(ins):
                            n[0] += 1
                            ins.then_inc(dve, 1)
                            v.wait_ge(dve, n[0])

                        v.wait_ge(last_in, 16)
                        v.wait_ge(consts_in, 16)
                        step(v.tensor_scalar(last_i[:, :], last_i[:, :], 7, None, ALU.arith_shift_right))
                        step(v.tensor_copy(last_f[:, :], last_i[:, :]))
                        step(v.scalar_tensor_tensor(last_f[:, :], last_f[:, :], float(NODE_BLOCKS - 1),
                                                    iota[0:ITEMS, 0:GROUPS], ALU.min, ALU.add))
                        step(v.tensor_scalar(last_f[:, :], last_f[:, :], row[0:ITEMS, :], None, ALU.is_lt))
                        step(v.tensor_reduce(gb_f[:, 0:1], last_f[:, :], AX, ALU.add))
                        step(v.tensor_tensor(gb_f[:, 1:2], row[0:ITEMS, :], gb_f[:, 0:1], ALU.subtract))
                        step(v.tensor_copy(gb_i[:, :], gb_f[:, 0:2]))
                        step(v.tensor_scalar(gb_f[:, 2:3], gb_f[:, 1:2], float(P), None, ALU.mult))
                        v.wait_ge(rows_in, 48)
                        step(v.tensor_copy(dst_f[:, :], dst_i[:, :]))
                        step(v.tensor_scalar(dst_f[:, :], dst_f[:, :], gb_f[:, 2:3], -1.0, ALU.subtract, ALU.max))
                        step(v.tensor_scalar(dst_f[:, :], dst_f[:, :], float(P), None, ALU.min))
                        step(v.tensor_copy(rel_b[:, :], dst_f[:, :]))
                        step(v.tensor_copy(src_f[:, :], src_i[:, :]))
                        v.wait_ge(pe, 1)
                        v.tensor_copy(rel_all[:, :, :].rearrange("p i j -> p j i"), psum[:, 0, :].rearrange("p (j i) -> p j i", j=SUBS)[:, :, 0:ITEMS])
                        v.tensor_copy(idx_all[:, :, :].rearrange("p i j -> p j i"), psum[:, 1, :].rearrange("p (j i) -> p j i", j=SUBS)[:, :, 0:ITEMS])
                        v.wait_ge(loads, 7 * 16)
                        for k in range(3):
                            v.tensor_copy(att_b[:, k, :], cols[:, k:k + 1].broadcast_to([P, P]))

                    @block.tensor
                    def _(e):
                        e.wait_ge(consts_in, 16)
                        e.wait_ge(dve, 13)
                        for k, rows in enumerate((dst_f, src_f)):
                            for j in range(SUBS):
                                last = e.transpose(psum[:, k, j * P:j * P + ITEMS], rows[:, j * P:(j + 1) * P],
                                                   ident[0:ITEMS, 0:ITEMS])
                        last.then_inc(pe, 1)

        dst_f = sm[0:ITEMS, 0, :]
        src_f = sm[0:ITEMS, 1, :]
        rel_b = rel[0:ITEMS, 0, :]
        setup()

        def layernorm(name, src, dst, gamma=None, beta=None, relu=False, prep=None, prep_steps=0):
            dve, act = sem(name + "_dve"), sem(name + "_act")
            with nc.Block() as block:
                @block.vector
                def _(v):
                    n = [0]

                    def step(ins):
                        n[0] += 1
                        ins.then_inc(dve, 1)
                        v.wait_ge(dve, n[0])

                    if prep is not None:
                        prep(v, step)
                    assert n[0] == prep_steps
                    step(v.tensor_reduce(stat[:, 0, :], src, AX, ALU.add))
                    step(v.tensor_scalar(stat[:, 0, :], stat[:, 0, :], 1.0 / D, None, ALU.mult))
                    step(v.tensor_tensor(dst, src, over_features(stat[:, 0, :]), ALU.subtract))
                    v.wait_ge(act, 1)
                    step(v.tensor_reduce(stat[:, 1, :], TMP[:, :, :], AX, ALU.add))
                    step(v.tensor_scalar(stat[:, 1, :], stat[:, 1, :], 1.0 / D, 1e-5, ALU.mult, ALU.add))
                    v.wait_ge(act, 2)
                    step(v.reciprocal(stat[:, 3, :], stat[:, 2, :]))
                    step(v.tensor_tensor(dst, dst, over_features(stat[:, 3, :]), ALU.mult))
                    if gamma is not None:
                        step(v.tensor_tensor(dst, dst, over_blocks(gamma), ALU.mult))
                        step(v.tensor_tensor(dst, dst, over_blocks(beta), ALU.add))
                    if relu:
                        step(v.tensor_scalar(dst, dst, 0.0, None, ALU.max))

                @block.scalar
                def _(a):
                    a.wait_ge(dve, prep_steps + 3)
                    a.activation(TMP[:, :, :], dst, ACT.Square).then_inc(act, 1)
                    a.wait_ge(dve, prep_steps + 5)
                    a.activation(stat[:, 2, :], stat[:, 1, :], ACT.Sqrt).then_inc(act, 1)

        def turn_blocks(name, src, dst, to_feature_major=True, rounds=None):
            turned, taken = rounds or (sem(name + "_turned"), sem(name + "_taken"))[0:2]
            return turned, taken

        CH = 5
        def transposes(turned, taken, src, dst, base=0):
            with nc.Block() as block:
                @block.tensor
                def _(e):
                    for c in range(NODE_BLOCKS // CH):
                        if c >= 2:
                            hold(e, (taken, base + c - 1))
                        for k in range(CH):
                            b = c * CH + k
                            o = psum[:, 2 * (c % 2) + k // 4, (k % 4) * P:(k % 4 + 1) * P]
                            last = e.transpose(o, src[:, b * P:(b + 1) * P], ident)
                        last.then_inc(turned, 1)

                @block.scalar
                def _(a):
                    for c in range(NODE_BLOCKS // CH):
                        wait(a, turned, base + c + 1)
                        half = psum[:, 2 * (c % 2):2 * (c % 2) + 2, :].rearrange("p a n -> p (a n)")
                        a.activation(dst[:, c * CH * P:(c + 1) * CH * P], half[:, 0:CH * P], ACT.Copy).then_inc(taken, 1)

        def flat(buf):
            return buf[:, :, :].rearrange("p b d -> p (b d)")

        CB = 4
        CHUNKS = -(-NODE_BLOCKS // CB)

        def tables(name, width, w_src, b_src, w_dst, b_dst, dram, extra=None):
            made, staged, split_a, split_v, stored, eb = (sem(f"{name}_{k}") for k in (
                "made", "staged", "split_a", "split_v", "stored", "extra"))
            rows = dram.rearrange("(b p) d -> p b d", p=P)
            per = 512 // width
            STG = 2 if extra is None else 3

            def place(bank0, k):
                return psum[:, bank0 + k // per, (k % per) * width:(k % per + 1) * width]

            def banks(bank0, n):
                v = psum[:, bank0:bank0 + CB // per, :].rearrange("p a (k w) -> p (a k) w", w=width)
                return v[:, 0:n, :]

            def bias_of(b, n):
                return b.unsqueeze(1).broadcast_to([P, n, b.shape[1]])

            with nc.Block() as block:
                @block.tensor
                def _(e):
                    for c in range(CHUNKS):
                        wait(e, staged, STG * c)
                        for k in range(min(CB, NODE_BLOCKS - c * CB)):
                            b = c * CB + k
                            xt = XT[:, b * P:(b + 1) * P]
                            e.matmul(place(0, k), xt, w_src, start=True, stop=True)
                            last = e.matmul(place(2, k), xt, w_dst, start=True, stop=True)
                            if extra is not None:
                                last = e.matmul(psum[:, 4, k * D:(k + 1) * D], xt, extra[0], start=True, stop=True)
                        last.then_inc(made, 1)

                @block.vector
                def _(v):
                    for c in range(CHUNKS):
                        n = min(CB, NODE_BLOCKS - c * CB)
                        v.wait_ge(made, c + 1)
                        wait(v, stored, 16 * c)
                        v.tensor_tensor(stage[:, 0:n, 0:width], banks(0, n), bias_of(b_src, n), ALU.add).then_inc(staged, 1)
                        wait(v, split_v, 2 * c)
                        v.tensor_tensor(stage_r[:, 0:n, 0:width], banks(2, n), bias_of(b_dst, n), ALU.add).then_inc(staged, 1)
                        if extra is not None:
                            y = Y[:, c * CB:c * CB + n, :]
                            v.tensor_tensor(y, psum[:, 4, 0:n * D].rearrange("p (k d) -> p k d", d=D), bias_of(extra[1], n), ALU.add).then_inc(eb, 1)
                            v.wait_ge(eb, c + 1)
                            v.scalar_tensor_tensor(y, X[:, c * CB:c * CB + n, :], 2.0, y, ALU.mult, ALU.add).then_inc(staged, 1)
                        r = stage_r[:, 0:n, 0:width]
                        x = XR[:, c * CB:c * CB + n, :, 0:width]
                        v.wait_ge(split_a, 2 * c + 1)
                        v.tensor_tensor(r, r, x[:, :, 0, :], ALU.subtract).then_inc(split_v, 1)
                        v.wait_ge(split_a, 2 * c + 2)
                        v.wait_ge(split_v, 2 * c + 1)
                        v.tensor_tensor(x[:, :, 2, :], r, x[:, :, 1, :], ALU.subtract).then_inc(split_v, 1)

                @block.scalar
                def _(a):
                    for c in range(CHUNKS):
                        n = min(CB, NODE_BLOCKS - c * CB)
                        r = stage_r[:, 0:n, 0:width]
                        x = XR[:, c * CB:c * CB + n, :, 0:width]
                        a.wait_ge(staged, STG * c + 2)
                        a.activation(x[:, :, 0, :], r, ACT.Copy).then_inc(split_a, 1)
                        a.wait_ge(split_v, 2 * c + 1)
                        a.activation(x[:, :, 1, :], r, ACT.Copy).then_inc(split_a, 1)

                @block.sync
                def _(sp):
                    for c in range(CHUNKS):
                        n = min(CB, NODE_BLOCKS - c * CB)
                        sp.wait_ge(staged, STG * c + 1)
                        sp.dma_start(rows[:, c * CB:c * CB + n, :], stage[:, 0:n, 0:width]).then_inc(stored, 16)
                    sp.wait_ge(stored, 16 * CHUNKS)

        def gat_edges(name, heads, dram, att, with_weight):
            width = heads * D
            acc = ACC[:, 0:NODE_BLOCKS * width].rearrange("p (b h d) -> p b h d", h=heads, d=D)
            idx_in = [sem(f"{name}_idx_in{s}") for s in range(2)]
            rel_in = [sem(f"{name}_rel_in{s}") for s in range(2)]
            w_in = [sem(f"{name}_w_in{s}") for s in range(2)]
            gathered = [sem(f"{name}_gathered{s}") for s in range(2)]
            cleared, masks, v_ready, v_copied, leaked, s_ready, s_masked, max_step, max_done, p_ready, scl_ready, \
                pt_ready, pt_copied, o_ready, acc_done = (sem(f"{name}_{k}") for k in (
                    "cleared", "masks", "v_ready", "v_copied", "leaked", "s_ready", "s_masked", "max_step",
                    "max_done", "p_ready", "scl_ready", "pt_ready", "pt_copied", "o_ready", "acc_done"))
            V = [psum[:, h, :] for h in range(heads)]
            S = [psum[:, 2 + h, :] for h in range(heads)]
            T = [psum[:, 4 + h, :] for h in range(heads)]
            O = [psum[:, 6 + h, 0:D] for h in range(heads)]

            def block_of(e, i):
                return e.value_load(groups_blocks[0:1, bass.ds(i, 1), 1], min_val=0, max_val=NODE_BLOCKS - 1)

            def walk(e, front, mid, back):
                front(0, 0, 0)
                mid(0, 0, 0)
                with e.Fori(0, PAIRS - 1) as k:
                    for i, s, turn in ((2 * k + 1, 1, k), (2 * k + 2, 0, k + 1)):
                        front(i, s, turn)
                        back(i - 1, 1 - s, turn)
                        mid(i, s, turn)
                i = ITEMS - 1
                front(i, 1, PAIRS - 1)
                back(i - 1, 0, PAIRS - 1)
                mid(i, 1, PAIRS - 1)
                back(i, 1, PAIRS - 1)

            with nc.Block() as block:
                @block.sync
                def _(sp):
                    def item(i, s, k):
                        sp.wait_ge(gathered[s], 16 * SUBS * k)
                        sp.dma_start(idx[:, s, :], idx_all[:, bass.ds(i, 1), :].rearrange("p a j -> p (a j)")).then_inc(idx_in[s], 16)
                        wait(sp, masks, i - 1)
                        sp.dma_start(rel[:, s, :], rel_rows[bass.ds(i, 1), :].broadcast_to([P, GROUP_EDGES])).then_inc(rel_in[s], 16)
                        if with_weight:
                            hold(sp, (v_ready, heads * (i - 1)))
                            sp.dma_start(wrow[:, s, :], weight_rows[bass.ds(i, 1), :]).then_inc(w_in[s], 16)

                    pairs(sp, item)

                @block.gpsimd
                def _(pool):
                    def item(i, s, k):
                        hold(pool, (idx_in[s], 16 * (k + 1)),
                             (o_ready, heads * (i - 1)))
                        for j in range(SUBS):
                            pool.indirect_dma_start(
                                out=gath[:, s, j, 0:width], out_offset=None, in_=dram,
                                in_offset=bass.IndirectOffsetOnAxis(ap=idx[:, s, j:j + 1], axis=0)).then_inc(gathered[s], 16)

                    pairs(pool, item)

                @block.tensor
                def _(e):
                    def front(i, s, turn):
                        b = block_of(e, i)
                        late = [(w_in[s], 16 * (turn + 1))] if with_weight else []
                        hold(e, (masks, i + 1), (gathered[s], 16 * SUBS * (turn + 1)), *late)
                        for h in range(heads):
                            for k in range(SPLIT):
                                e.matmul(V[h], XR[:, bass.ds(b, 1), k, h * D:(h + 1) * D].rearrange("p a d -> p (a d)"), hot_t[:, s, :],
                                         start=(k == 0), stop=False)
                            if with_weight:
                                e.matmul(V[h], we_row[:, :], wrow[:, s, :], start=False, stop=False)
                            for j in range(SUBS):
                                last = e.matmul(V[h][:, j * P:(j + 1) * P], gath[:, s, j, h * D:(h + 1) * D],
                                                ident, start=False, stop=(j == SUBS - 1))
                            last.then_inc(v_ready, 1)

                    def mid(i, s, turn):
                        for h in range(heads):
                            e.wait_ge(leaked, heads * i + h + 1)
                            e.matmul(S[h], att_b[:, att[h], :], lk[:, h, :], start=True, stop=True).then_inc(s_ready, 1)

                    def back(i, s, turn):
                        for h in range(heads):
                            e.wait_ge(p_ready, heads * i + h + 1)
                            for j in range(SUBS):
                                last = e.transpose(T[h][:, j * P:(j + 1) * P], pm[:, h, j * P:(j + 1) * P], ident)
                            last.then_inc(pt_ready, 1)
                        wait(e, acc_done, i)
                        for h in range(heads):
                            e.wait_ge(pt_copied, heads * i + h + 1)
                            for j in range(SUBS):
                                last = e.matmul(O[h], pt[:, h, j, :], gath[:, s, j, h * D:(h + 1) * D],
                                                start=(j == 0), stop=(j == SUBS - 1))
                            last.then_inc(o_ready, 1)

                    walk(e, front, mid, back)

                @block.scalar
                def _(a):
                    def front(i, s, turn):
                        for h in range(heads):
                            wait(a, leaked, heads * (i - 1) + h + 1)
                            a.wait_ge(v_ready, heads * i + h + 1)
                            a.activation(vs[:, h, :], V[h], ACT.Copy).then_inc(v_copied, 1)

                    def mid(i, s, turn):
                        a.wait_ge(max_done, i + 1)
                        wait(a, acc_done, i)
                        for h in range(heads):
                            a.activation(pm[:, h, :], sm[:, h, :], ACT.Exp, bias=NEGM[:, h:h + 1],
                                         accum_out=ZI[:, h:h + 1]).then_inc(p_ready, 1)
                        a.activation(SCL[:, 0:heads], DM[:, 0:heads], ACT.Exp).then_inc(scl_ready, 1)

                    def back(i, s, turn):
                        for h in range(heads):
                            a.wait_ge(pt_ready, heads * i + h + 1)
                            wait(a, acc_done, i)
                            a.activation(pt[:, h, :, :].rearrange("p j n -> p (j n)"), T[h], ACT.Copy).then_inc(pt_copied, 1)

                    walk(a, front, mid, back)

                @block.vector
                def _(v):
                    v.memset(ACC[:, 0:NODE_BLOCKS * width], 0.0)
                    v.memset(zsum[:, :, :], 0.0)
                    v.memset(mmax[:, :, :], FLOOR).then_inc(cleared, 1)
                    v.wait_ge(cleared, 1)

                    def mask(i, s, turn):
                        v.wait_ge(rel_in[s], 16 * (turn + 1))
                        wait(v, v_ready, heads * (i - 1))
                        wait(v, s_masked, heads * (i - 1))
                        v.tensor_scalar(neg[:, s, :], rel[:, s, :], row, MASKED, ALU.not_equal, ALU.mult)
                        v.tensor_scalar(hot_t[:, s, :], rel[:, s, :], row, None, ALU.is_equal).then_inc(masks, 1)

                    def front(i, s, turn):
                        for h in range(heads):
                            wait(v, s_ready, heads * (i - 1) + h + 1)
                            v.wait_ge(v_copied, heads * i + h + 1)
                            v.scalar_tensor_tensor(lk[:, h, :], V[h], 0.2, vs[:, h, :], ALU.mult, ALU.max).then_inc(leaked, 1)

                    def mid(i, s, turn):
                        b = block_of(v, i)
                        for h in range(heads):
                            hold(v, (p_ready, heads * i),
                                 (scl_ready, i), (s_ready, heads * i + h + 1))
                            v.tensor_tensor_reduce(out=sm[:, h, :], in0=S[h], in1=neg[:, s, :], scale=1.0, scalar=MASKED,
                                                   op0=ALU.add, op1=ALU.max, accum_out=MI[:, h:h + 1]).then_inc(s_masked, 1)
                        old = mmax[:, bass.ds(b, 1), 0:heads].rearrange("p a h -> p (a h)")
                        new = MNEW[:, 0:heads]
                        v.wait_ge(s_masked, heads * (i + 1))
                        wait(v, max_done, i)
                        v.tensor_tensor(new, old, MI[:, 0:heads], ALU.max).then_inc(max_step, 1)
                        v.wait_ge(max_step, 2 * i + 1)
                        v.tensor_tensor(DM[:, 0:heads], old, new, ALU.subtract).then_inc(max_step, 1)
                        v.tensor_scalar(NEGM[:, 0:heads], new, -1.0, None, ALU.mult)
                        hold(v, (max_step, 2 * i + 2))
                        v.tensor_copy(old, new).then_inc(max_done, 1)
                        if not (isinstance(i, int) and i == ITEMS - 1):
                            mask(i + 1, 1 - s, turn + s)

                    def back(i, s, turn):
                        b = block_of(v, i)
                        v.wait_ge(scl_ready, i + 1)
                        v.wait_ge(p_ready, heads * (i + 1))
                        wait(v, acc_done, i)
                        for h in range(heads):
                            v.wait_ge(o_ready, heads * i + h + 1)
                            a_h = acc[:, bass.ds(b, 1), h, :].rearrange("p a d -> p (a d)")
                            z_h = zsum[:, bass.ds(b, 1), h:h + 1].rearrange("p a h -> p (a h)")
                            v.scalar_tensor_tensor(a_h, a_h, SCL[:, h:h + 1], O[h], ALU.mult, ALU.add)
                            last = v.scalar_tensor_tensor(z_h, z_h, SCL[:, h:h + 1], ZI[:, h:h + 1], ALU.mult, ALU.add)
                        last.then_inc(acc_done, 1)

                    mask(0, 0, 0)
                    walk(v, front, mid, back)

        gi = {k: sem(f"gine_{k}") for k in (
            "hot_done", "e_ready", "added", "msg", "o_ready", "acc_done", "cleared")}
        gi_idx = [sem(f"gine_idx_in{s}") for s in range(2)]
        gi_ea = [sem(f"gine_ea_in{s}") for s in range(2)]
        gi_gath = [sem(f"gine_gathered{s}") for s in range(2)]
        gine_stored = sem("gine_stored")

        def group_of(e, i):
            return e.value_load(groups_blocks[0:1, bass.ds(i, 1), 0], min_val=0, max_val=GROUPS - 1)

        def block_of(e, i):
            return e.value_load(groups_blocks[0:1, bass.ds(i, 1), 1], min_val=0, max_val=NODE_BLOCKS - 1)

        def gine_edges(layer):
            acc = ACC[:, 0:NPAD]
            done = layer * ITEMS
            turns = layer * PAIRS
            E = [psum[:, s, :] for s in range(2)]
            O = [psum[:, 2 + s, 0:P] for s in range(2)]
            with nc.Block() as block:
                @block.sync
                def _(sp):
                    def item(i, s, k):
                        n, turn = done + i, turns + k
                        g = group_of(sp, i)
                        sp.wait_ge(gi_gath[s], 16 * SUBS * turn)
                        sp.dma_start(idx[:, s, :], idx_all[:, bass.ds(i, 1), :].rearrange("p a j -> p (a j)")).then_inc(gi_idx[s], 16)
                        if not isinstance(k, int):
                            sp.wait_ge(gi["e_ready"], n - 1)
                        sp.dma_start(ea[:, s, :], t["edge_attr"][bass.ds(g, 1), :, :].rearrange("a k e -> (a k) e")).then_inc(gi_ea[s], 16)

                    pairs(sp, item)

                @block.gpsimd
                def _(pool):
                    def item(i, s, k):
                        hold(pool, (gi_idx[s], 16 * (turns + k + 1)), (gine_stored, 16 * (layer + 1)),
                             *([] if isinstance(k, int) else [(gi["added"], done + i - 1)]))
                        for j in range(SUBS):
                            pool.indirect_dma_start(
                                out=gath[:, s, j, 0:D], out_offset=None, in_=table1,
                                in_offset=bass.IndirectOffsetOnAxis(ap=idx[:, s, j:j + 1], axis=0)).then_inc(gi_gath[s], 16)

                    pairs(pool, item)

                def walk(e, front, back):
                    front(0, done, 0, turns)
                    with e.Fori(0, PAIRS - 1) as k:
                        for i, s, turn in ((2 * k + 1, 1, turns + k), (2 * k + 2, 0, turns + k + 1)):
                            front(i, done + i, s, turn)
                            back(i - 1, done + i - 1, 1 - s)
                    i = ITEMS - 1
                    front(i, done + i, 1, turns + PAIRS - 1)
                    back(i - 1, done + i - 1, 0)
                    back(i, done + i, 1)

                @block.tensor
                def _(e):
                    def front(i, n, s, turn):
                        e.wait_ge(gi_ea[s], 16 * (turn + 1))
                        for j in range(SUBS):
                            last = e.matmul(E[s][:, j * D:(j + 1) * D], ea[:, s, j * P:(j + 1) * P], gine_lin[:, :],
                                            start=True, stop=True)
                        last.then_inc(gi["e_ready"], 1)

                    def back(i, n, s):
                        e.wait_ge(gi["msg"], n + 1)
                        e.wait_ge(gi["hot_done"], n + 1)
                        e.wait_ge(gi["acc_done"], n)
                        for j in range(SUBS):
                            last = e.matmul(O[s], pm[:, s, j * P:(j + 1) * P], hot[:, s, j, :], start=(j == 0), stop=(j == SUBS - 1))
                        last.then_inc(gi["o_ready"], 1)

                    walk(e, front, back)

                @block.vector
                def _(v):
                    v.memset(acc, 0.0).then_inc(gi["cleared"], 1)
                    v.wait_ge(gi["cleared"], layer + 1)

                    def front(i, n, s, turn):
                        if not isinstance(i, int) or i >= 2:
                            v.wait_ge(gi["o_ready"], done + i - 1)
                        v.tensor_tensor(hot[:, s, :, :], iota.unsqueeze(1).broadcast_to([P, SUBS, P]),
                                        rel_all[:, bass.ds(i, 1), :].rearrange("p a j -> p (a j)").unsqueeze(2).broadcast_to([P, SUBS, P]),
                                        ALU.is_equal).then_inc(gi["hot_done"], 1)
                        v.wait_ge(gi_gath[s], 16 * SUBS * (turn + 1))
                        if not isinstance(i, int) or i >= 2:
                            v.wait_ge(gi["msg"], done + i - 1)
                        v.wait_ge(gi["e_ready"], n + 1)
                        v.tensor_tensor(vs[:, s, :].rearrange("p (j d) -> p j d", j=SUBS), E[s].rearrange("p (j d) -> p j d", j=SUBS), gath[:, s, :, 0:D], ALU.add).then_inc(gi["added"], 1)

                    def back(i, n, s):
                        b = block_of(v, i)
                        v.wait_ge(gi["acc_done"], n + 1)
                        v.wait_ge(gi["o_ready"], n + 1)
                        a_b = acc[:, bass.ds(b * P, P)]
                        v.tensor_tensor(a_b, a_b, O[s], ALU.add).then_inc(gi["acc_done"], 1)

                    walk(v, front, back)

                @block.scalar
                def _(a):
                    def item(i, s, k):
                        n = done + i
                        if not isinstance(k, int):
                            a.wait_ge(gi["o_ready"], n - 1)
                        a.wait_ge(gi["added"], n + 1)
                        a.activation(pm[:, s, :], vs[:, s, :], ACT.Relu).then_inc(gi["msg"], 1)

                    pairs(a, item)

        def mlp_edges():
            acc = [ACC[:, h * NPAD:(h + 1) * NPAD] for h in range(2)]
            idx_in = [sem(f"mlp_idx_in{s}") for s in range(2)]
            rel_in = [sem(f"mlp_rel_in{s}") for s in range(2)]
            ea_in = [sem(f"mlp_ea_in{s}") for s in range(2)]
            gathered = [sem(f"mlp_gathered{s}") for s in range(2)]
            cleared, hot_done, h1_ready, h1_done, h2_ready, h2_added, h2_done, o_ready, acc_done, deg_step = (
                sem(f"mlp_{k}") for k in ("cleared", "hot_done", "h1_ready", "h1_done", "h2_ready", "h2_added",
                                          "h2_done", "o_ready", "acc_done", "deg_step"))
            H1 = [psum[:, h, :] for h in range(2)]
            H2 = psum[:, 2:4, :].rearrange("p a n -> p (a n)").rearrange("p (j d) -> p j d", d=HID)
            O = psum[:, 4, 0:2 * P].rearrange("p (h n) -> p h n", h=2)
            h1 = pm
            h2a = XT_free = TMP[:, 0:8, :].rearrange("p a d -> p (a d)").rearrange("p (j d) -> p j d", d=HID)
            h2 = TMP[:, 8:16, :].rearrange("p a d -> p (a d)").rearrange("p (j d) -> p j d", d=HID)
            w2 = [weight("L3_gnn_W2a"), weight("L3_gnn_W2b")]

            def walk(e, front, mid, back):
                front(0, 0, 0)
                mid(0, 0)
                with e.Fori(0, PAIRS - 1) as k:
                    for i, s, turn in ((2 * k + 1, 1, k), (2 * k + 2, 0, k + 1)):
                        front(i, s, turn)
                        back(i - 1, 1 - s)
                        mid(i, s)
                i = ITEMS - 1
                front(i, 1, PAIRS - 1)
                back(i - 1, 0)
                mid(i, 1)
                back(i, 1)

            with nc.Block() as block:
                @block.sync
                def _(sp):
                    def item(i, s, k):
                        g = group_of(sp, i)
                        sp.wait_ge(gathered[s], 16 * SUBS * k)
                        sp.dma_start(idx[:, s, :], idx_all[:, bass.ds(i, 1), :].rearrange("p a j -> p (a j)")).then_inc(idx_in[s], 16)
                        wait(sp, hot_done, i - 1)
                        sp.dma_start(rel[:, s, :], rel_rows[bass.ds(i, 1), :].broadcast_to([P, GROUP_EDGES])).then_inc(rel_in[s], 16)
                        wait(sp, h1_ready, 2 * (i - 1))
                        sp.dma_start(ea[:, s, :], t["edge_attr"][bass.ds(g, 1), :, :].rearrange("a k e -> (a k) e")).then_inc(ea_in[s], 16)

                    pairs(sp, item)

                @block.gpsimd
                def _(pool):
                    def item(i, s, k):
                        hold(pool, (idx_in[s], 16 * (k + 1)),
                             (h1_ready, 2 * (i - 1)))
                        for j in range(SUBS):
                            pool.indirect_dma_start(
                                out=gath[:, s, j, :], out_offset=None, in_=table,
                                in_offset=bass.IndirectOffsetOnAxis(ap=idx[:, s, j:j + 1], axis=0)).then_inc(gathered[s], 16)

                    pairs(pool, item)

                @block.tensor
                def _(e):
                    def front(i, s, turn):
                        b = block_of(e, i)
                        hold(e, (ea_in[s], 16 * (turn + 1)),
                             (hot_done, i + 1),
                             (gathered[s], 16 * SUBS * (turn + 1)))
                        for h in range(2):
                            for k in range(SPLIT):
                                e.matmul(H1[h], XR[:, bass.ds(b, 1), k, h * D:(h + 1) * D].rearrange("p a d -> p (a d)"), hot_t[:, s, :],
                                         start=(k == 0), stop=False)
                            e.matmul(H1[h], edge_w1[:, h * D:(h + 1) * D], ea[:, s, :], start=False, stop=False)
                            for j in range(SUBS):
                                last = e.matmul(H1[h][:, j * P:(j + 1) * P], gath[:, s, j, h * D:(h + 1) * D],
                                                ident, start=False, stop=(j == SUBS - 1))
                            last.then_inc(h1_ready, 1)

                    def mid(i, s):
                        e.wait_ge(h1_done, 2 * (i + 1))
                        for j in range(SUBS):
                            for h in range(2):
                                last = e.matmul(H2[:, j, :], h1[:, h, j * P:(j + 1) * P], w2[h], start=(h == 0), stop=(h == 1))
                        last.then_inc(h2_ready, 1)

                    def back(i, s):
                        e.wait_ge(h2_done, i + 1)
                        wait(e, acc_done, i)
                        for h in range(2):
                            for j in range(SUBS):
                                last = e.matmul(O[:, h, :], h2[:, j, h * D:(h + 1) * D], hot[:, s, j, :], start=(j == 0), stop=(j == SUBS - 1))
                        last.then_inc(o_ready, 1)

                    walk(e, front, mid, back)

                @block.scalar
                def _(a):
                    def front(i, s, turn):
                        for h in range(2):
                            wait(a, h2_ready, i)
                            a.wait_ge(h1_ready, 2 * i + h + 1)
                            a.activation(h1[:, h, :], H1[h], ACT.Relu).then_inc(h1_done, 1)

                    def mid(i, s):
                        wait(a, o_ready, i)
                        a.wait_ge(h2_added, i + 1)
                        a.activation(h2, h2a, ACT.Relu).then_inc(h2_done, 1)

                    walk(a, front, mid, lambda i, s: None)

                @block.vector
                def _(v):
                    v.memset(ACC[:, :], 0.0)
                    v.memset(stat[:, 0, :], 0.0).then_inc(cleared, 1)
                    v.wait_ge(cleared, 1)

                    def hots(i, s, turn):
                        wait(v, o_ready, i - 1)
                        v.tensor_tensor(hot[:, s, :, :], iota.unsqueeze(1).broadcast_to([P, SUBS, P]),
                                        rel_all[:, bass.ds(i, 1), :].rearrange("p a j -> p (a j)").unsqueeze(2).broadcast_to([P, SUBS, P]),
                                        ALU.is_equal)
                        v.wait_ge(rel_in[s], 16 * (turn + 1))
                        wait(v, deg_step, 2 * i - 2)
                        wait(v, h1_ready, 2 * i - 2)
                        v.tensor_scalar(hot_t[:, s, :], rel[:, s, :], row, None, ALU.is_equal).then_inc(hot_done, 1)

                    def front(i, s, turn):
                        b = block_of(v, i)
                        v.wait_ge(hot_done, i + 1)
                        wait(v, deg_step, 2 * i)
                        v.tensor_reduce(MI[:, 0:1], hot_t[:, s, :], AX, ALU.add).then_inc(deg_step, 1)
                        v.wait_ge(deg_step, 2 * i + 1)
                        d_b = stat[:, 0, bass.ds(b, 1)]
                        v.tensor_tensor(d_b, d_b, MI[:, 0:1], ALU.add).then_inc(deg_step, 1)

                    def mid(i, s):
                        wait(v, h2_done, i)
                        v.wait_ge(h2_ready, i + 1)
                        b2 = bias("L3_gnn_b2").unsqueeze(1).broadcast_to([P, SUBS, HID])
                        v.tensor_tensor(h2a, H2, b2, ALU.add).then_inc(h2_added, 1)
                        if not (isinstance(i, int) and i == ITEMS - 1):
                            hots(i + 1, 1 - s, mid.turn + s)

                    def back(i, s):
                        b = block_of(v, i)
                        wait(v, acc_done, i)
                        v.wait_ge(o_ready, i + 1)
                        for h in range(2):
                            a_b = acc[h][:, bass.ds(b * P, P)]
                            last = v.tensor_tensor(a_b, a_b, O[:, h, :], ALU.add)
                        last.then_inc(acc_done, 1)

                    def front_turn(i, s, turn):
                        mid.turn = turn
                        front(i, s, turn)

                    hots(0, 0, 0)
                    walk(v, front_turn, mid, back)

        layernorm("ln0", X[:, :, :], Y[:, :, :], gamma=bias("L0_gnn_gamma"), beta=bias("L0_gnn_beta"), relu=True)
        transposes(sem("t0_turned"), sem("t0_taken"), flat(Y), XT)
        tables("tab0", 2 * D, weight("L0_gnn_Wl"), bias("L0_gnn_bl"), weight("L0_gnn_Wr"), bias("L0_gnn_br"), table,
               extra=(weight("L0_gnn_res_W"), bias("L0_gnn_bias")))
        gat_edges("gat0", HEADS, table, (0, 1), with_weight=False)

        def mean_of_heads(v, step):
            acc = ACC[:, :].rearrange("p (b h d) -> p b h d", h=2, d=D)
            step(v.tensor_scalar(zsum[:, :, :], zsum[:, :, :], 1e-16, None, ALU.add))
            step(v.reciprocal(zsum[:, :, :], zsum[:, :, :]))
            for h in range(2):
                z = zsum[:, :, h:h + 1].broadcast_to([P, NODE_BLOCKS, D])
                step(v.tensor_tensor(acc[:, :, h, :], acc[:, :, h, :], z, ALU.mult))
            step(v.tensor_tensor(TMP[:, :, :], acc[:, :, 0, :], acc[:, :, 1, :], ALU.add))
            step(v.scalar_tensor_tensor(flat(Y), flat(TMP), 0.5, flat(Y), ALU.mult, ALU.add))

        layernorm("ln1", Y[:, :, :], X[:, :, :], prep=mean_of_heads, prep_steps=6)

        transposes(sem("t1_turned"), sem("t1_taken"), flat(X), XT)
        tables("tab1", D, weight("L1_gnn_Wl"), bias("L1_gnn_bl"), weight("L1_gnn_Wr"), bias("L1_gnn_br"), table1)
        gat_edges("gat1", 1, table1, (2,), with_weight=True)

        def gat1_sum():
            dve = sem("gat1_sum")
            acc = ACC[:, 0:NPAD].rearrange("p (b d) -> p b d", d=D)
            with nc.Block() as block:
                @block.vector
                def _(v):
                    n = [0]

                    def step(ins):
                        n[0] += 1
                        ins.then_inc(dve, 1)
                        v.wait_ge(dve, n[0])

                    step(v.tensor_scalar(zsum[:, :, :], zsum[:, :, :], 1e-16, None, ALU.add))
                    step(v.reciprocal(zsum[:, :, :], zsum[:, :, :]))
                    step(v.tensor_tensor(Y[:, :, :], acc, zsum[:, :, 0:1].broadcast_to([P, NODE_BLOCKS, D]), ALU.mult))
                    step(v.tensor_tensor(Y[:, :, :], Y[:, :, :], X[:, :, :], ALU.add))
                    step(v.tensor_tensor(Y[:, :, :], Y[:, :, :], over_blocks(bias("L1_gnn_bias_out")), ALU.add))

        def batchnorm(name, h, gamma, beta, func, sems=None, layer=0, scratch_out=None):
            dve, act = sems or (sem(name + "_dve"), sem(name + "_act"))
            base_v, base_a = layer * 7, layer * 3
            m = small[:, 6, 0:1]
            nm = small[:, 6, 1:2]
            va = small[:, 7, 0:1]
            sd = small[:, 7, 1:2]
            sc = small[:, 4, 0:1]
            sh = small[:, 4, 1:2]
            with nc.Block() as block:
                @block.vector
                def _(v):
                    n = [0]

                    def step(ins):
                        n[0] += 1
                        ins.then_inc(dve, 1)
                        v.wait_ge(dve, base_v + n[0])

                    step(v.tensor_reduce(m, h[:, 0:NODES], AX, ALU.add))
                    step(v.tensor_scalar(nm, m, -1.0 / NODES, None, ALU.mult))
                    v.wait_ge(act, base_a + 1)
                    step(v.tensor_scalar(va, va, 1.0 / NODES, 1e-5, ALU.mult, ALU.add))
                    v.wait_ge(act, base_a + 2)
                    step(v.reciprocal(sd, sd))
                    step(v.tensor_tensor(sc, sd, gamma, ALU.mult))
                    step(v.tensor_tensor(sh, sc, nm, ALU.mult))
                    v.tensor_tensor(sh, sh, beta, ALU.add).then_inc(dve, 1)

                @block.scalar
                def _(a):
                    a.wait_ge(dve, base_v + 2)
                    a.activation(flat(TMP)[:, 0:NODES], h[:, 0:NODES], ACT.Square, bias=nm, accum_out=va).then_inc(act, 1)
                    a.wait_ge(dve, base_v + 3)
                    a.activation(sd, va, ACT.Sqrt).then_inc(act, 1)
                    a.wait_ge(dve, base_v + 7)
                    a.activation(h, h, func, bias=sh, scale=sc).then_inc(act, 1)

        gat1_sum()
        HT = ACC[:, 0:NPAD]
        transposes(sem("t2_turned"), sem("t2_taken"), flat(Y), HT)

        def gelu():
            done = sem("gelu_done")
            with nc.Block() as block:
                @block.scalar
                def _(a):
                    a.activation(HT, HT, ACT.Gelu).then_inc(done, 1)
                    a.wait_ge(done, 1)

        gelu()
        batchnorm("bn1", HT, col("bn_gamma"), col("bn_beta"), ACT.Identity)
        transposes(sem("t3_turned"), sem("t3_taken"), HT, flat(Y))

        def add_residual(v, step):
            step(v.tensor_tensor(Y[:, :, :], Y[:, :, :], X[:, :, :], ALU.add))

        layernorm("ln2", Y[:, :, :], X[:, :, :], prep=add_residual, prep_steps=1)

        transposes(sem("t4_turned"), sem("t4_taken"), flat(X), XT)
        gine_loads, gine_tab, gine_h = (sem(f"gine_{k}") for k in ("loads", "tab", "h"))
        mlp1, mlp1_done, mlp2, mlp2_done = (sem(f"gine_{k}") for k in ("mlp1", "mlp1_done", "mlp2", "mlp2_done"))
        bn_sems = (sem("gine_bn_dve"), sem("gine_bn_act"))
        back_sems = (sem("gine_turned"), sem("gine_taken"))
        Z = XR[:, :, :, :].rearrange("p b k d -> p (b k d)").bitcast(F32)[:, 0:NPAD]
        Z3 = Z.rearrange("p (b d) -> p b d", d=D)
        NCOL = 400
        NCH = NPAD // NCOL

        def gine_node_to_table(layer):
            with nc.Block() as block:
                @block.sync
                def _(sp):
                    one = bass.ds(layer, 1)
                    sp.dma_start(gine_w[:, :, :], t["gine_w"][:, one, :, :].rearrange("p a k d -> p (a k) d")).then_inc(gine_loads, 16)
                    sp.dma_start(gine_lin[:, :], t["gine_lin"][one, :, :].rearrange("a k d -> (a k) d")).then_inc(gine_loads, 16)
                    sp.dma_start(gine_blin[:, :], t["gine_blin"][one, :].broadcast_to([P, D])).then_inc(gine_loads, 16)
                    sp.dma_start(gine_cols[:, :], t["gine_cols"][:, one, :].rearrange("p a k -> p (a k)")).then_inc(gine_loads, 16)
                    sp.wait_ge(gine_tab, layer + 1)
                    sp.dma_start(table1.rearrange("(b p) d -> p b d", p=P), TMP[:, :, :]).then_inc(gine_stored, 16)

                @block.vector
                def _(v):
                    v.wait_ge(gine_loads, 64 * (layer + 1))
                    v.tensor_tensor(TMP[:, :, :], Z3, over_blocks(gine_blin[:, :]), ALU.add).then_inc(gine_tab, 1)

        def gine_mlp(layer):
            h = ACC[:, 0:NPAD]
            u = ACC[:, NPAD:2 * NPAD]
            with nc.Block() as block:
                @block.vector
                def _(v):
                    v.tensor_tensor(h, h, XT[:, :], ALU.add).then_inc(gine_h, 1)

                @block.tensor
                def _(e):
                    with e.Fori(0, NCH) as c:
                        e.wait_ge(gine_h, layer + 1)
                        e.wait_ge(mlp1_done, layer * NCH + c)
                        e.matmul(psum[:, 0, 0:NCOL], gine_w[:, 0, :], h[:, bass.ds(c * NCOL, NCOL)], start=True, stop=True).then_inc(mlp1, 1)
                        e.wait_ge(mlp2_done, layer * NCH + c)
                        e.wait_ge(mlp1_done, layer * NCH + c + 1)
                        e.matmul(psum[:, 1, 0:NCOL], gine_w[:, 1, :], u[:, bass.ds(c * NCOL, NCOL)], start=True, stop=True).then_inc(mlp2, 1)

                @block.scalar
                def _(a):
                    with a.Fori(0, NCH) as c:
                        at = bass.ds(c * NCOL, NCOL)
                        hold(a, (mlp1, layer * NCH + c + 1))
                        a.activation(u[:, at], psum[:, 0, 0:NCOL], ACT.Relu, bias=gine_cols[:, 0:1]).then_inc(mlp1_done, 1)
                        hold(a, (gine_h, layer + 1),
                             (mlp2, layer * NCH + c + 1))
                        a.activation(XT[:, at], psum[:, 1, 0:NCOL], ACT.Identity, bias=gine_cols[:, 1:2]).then_inc(mlp2_done, 1)

        def gine_first():
            done = sem("gine_first")
            with nc.Block() as block:
                @block.vector
                def _(v):
                    v.tensor_copy(Z3, X[:, :, :]).then_inc(done, 1)
                    v.memset(small[:, 7, :], 0.0).then_inc(gi["acc_done"], 1)

        gine_first()
        with nc.Fori(0, GINE_LAYERS) as layer:
            gine_node_to_table(layer)
            gine_edges(layer)
            gine_mlp(layer)
            batchnorm("gine_bn", XT[:, :], gine_cols[:, 2:3], gine_cols[:, 3:4], ACT.Relu, sems=bn_sems, layer=layer)
            transposes(*back_sems, XT, Z, base=layer * (NODE_BLOCKS // CH))

        def add_gine(v, step):
            step(v.tensor_tensor(Y[:, :, :], Z3, X[:, :, :], ALU.add))

        layernorm("ln3", Y[:, :, :], X[:, :, :], prep=add_gine, prep_steps=1)

        transposes(sem("t5_turned"), sem("t5_taken"), flat(X), XT)
        zero_bias = stat
        tables("tab3", HID, weight("L3_gnn_W1a"), bias("L3_gnn_b1"), weight("L3_gnn_W1b"), zeros_b(nc, sb, sem), table)
        mlp_edges()

        def node_mlp():
            made, taken, diag, dsum = (sem(f"node_{k}") for k in ("made", "taken", "diag", "dsum"))
            aggr = XR[:, :, :, :].rearrange("p b k d -> p (b k d)").bitcast(F32)[:, 0:NPAD]
            hid = [XR[:, :, :, :].rearrange("p b k d -> p (b k d)").bitcast(F32)[:, NPAD * (1 + h):NPAD * (2 + h)] for h in range(2)]
            sums = [ACC[:, h * NPAD:(h + 1) * NPAD] for h in range(2)]
            b3 = bias("L3_gnn_b3")
            w3 = [weight("L3_gnn_W3a"), weight("L3_gnn_W3b")]
            with nc.Block() as block:
                @block.vector
                def _(v):
                    for b in range(NODE_BLOCKS):
                        wait(v, made, b - 1)
                        v.tensor_scalar(lk[:, b % 2, 0:P], ident, stat[:, 0, b:b + 1], None, ALU.mult).then_inc(diag, 1)

                @block.tensor
                def _(e):
                    for b in range(NODE_BLOCKS):
                        e.wait_ge(diag, b + 1)
                        wait(e, taken, b - 1)
                        o = psum[:, b % 2, 0:P]
                        for h in range(2):
                            e.matmul(o, w3[h], sums[h][:, b * P:(b + 1) * P], start=(h == 0), stop=False)
                        e.matmul(o, b3, lk[:, b % 2, 0:P], start=False, stop=True).then_inc(made, 1)

                @block.scalar
                def _(a):
                    for b in range(NODE_BLOCKS):
                        a.wait_ge(made, b + 1)
                        a.activation(aggr[:, b * P:(b + 1) * P], psum[:, b % 2, 0:P], ACT.Copy).then_inc(taken, 1)

            m1, m1_done, m2, m2_done = (sem(f"node_{k}") for k in ("m1", "m1_done", "m2", "m2_done"))
            wn1a, wn1b = weight("L3_gnn_Wn1a"), weight("L3_gnn_Wn1b")
            wn2 = [weight("L3_gnn_Wn2a"), weight("L3_gnn_Wn2b")]
            with nc.Block() as block:
                @block.tensor
                def _(e):
                    with e.Fori(0, NCH) as c:
                        at = bass.ds(c * NCOL, NCOL)
                        for h in range(2):
                            e.wait_ge(m1_done, 2 * c)
                            o = psum[:, h, 0:NCOL]
                            e.matmul(o, wn1a[:, h * D:(h + 1) * D], XT[:, at], start=True, stop=False)
                            e.matmul(o, wn1b[:, h * D:(h + 1) * D], aggr[:, at], start=False, stop=True).then_inc(m1, 1)
                        e.wait_ge(m2_done, c)
                        for h in range(2):
                            e.wait_ge(m1_done, 2 * c + h + 1)
                            last = e.matmul(psum[:, 2, 0:NCOL], wn2[h], hid[h][:, at], start=(h == 0), stop=(h == 1))
                        last.then_inc(m2, 1)

                @block.scalar
                def _(a):
                    with a.Fori(0, NCH) as c:
                        at = bass.ds(c * NCOL, NCOL)
                        for h in range(2):
                            hold(a, (m1, 2 * c + h + 1))
                            a.activation(hid[h][:, at], psum[:, h, 0:NCOL], ACT.Relu, bias=col("bn1a" if h == 0 else "bn1b")).then_inc(m1_done, 1)
                        hold(a, (m2, c + 1))
                        a.activation(HT[:, at], psum[:, 2, 0:NCOL], ACT.Identity, bias=col("bn2")).then_inc(m2_done, 1)

        node_mlp()
        transposes(sem("t6_turned"), sem("t6_taken"), HT, flat(Y))
        layernorm("ln4", Y[:, :, :], Y[:, :, :], gamma=bias("L3_gnn_gamma"), beta=bias("L3_gnn_beta"), prep=add_residual, prep_steps=1)
        layernorm("ln5", Y[:, :, :], Y[:, :, :], prep=add_residual, prep_steps=1)

        out_done = sem("out_done")
        with nc.Block() as block:
            @block.sync
            def _(sp):
                full = NODES // P
                sp.dma_start(t["out"][0:full * P, :].rearrange("(b p) d -> p b d", p=P), Y[:, 0:full, :]).then_inc(out_done, 16)
                sp.dma_start(t["out"][full * P:NODES, :], Y[0:NODES - full * P, full, :]).then_inc(out_done, 16)
                sp.wait_ge(out_done, 32)


def zeros_b(nc, sb, sem):
    z = sb("zeros", [P, HID])
    done = sem("zeros_done")
    with nc.Block() as block:
        @block.vector
        def _(v):
            v.memset(z[:, :], 0.0).then_inc(done, 1)
    return z[:, :]


def kernel(**inputs):
    import concourse.bacc as bacc
    from concourse.bass_utils import run_bass_kernel_spmd

    a = {k: np.asarray(v) for k, v in inputs.items()}
    pad = GROUPS * GROUP_EDGES - EDGES

    def padded(x, fill):
        return np.concatenate([x, np.full((pad,) + x.shape[1:], fill, x.dtype)])

    def spread(v):
        return np.broadcast_to(v.reshape(1, -1), (P, v.size))

    consts = np.zeros((P, C_WIDTH), np.float32)
    consts[:, C_IDENT:C_IDENT + P] = np.eye(P)
    consts[:, C_IOTA:C_IOTA + P] = np.arange(P)
    consts[:, C_ROW] = np.arange(P)
    w1, w2, w3 = a["L3_gnn_W1"], a["L3_gnn_W2"], a["L3_gnn_W3"]
    wn1, wn2 = a["L3_gnn_Wn1"], a["L3_gnn_Wn2"]
    a.update({"L3_gnn_W1a": w1[0:D], "L3_gnn_W1b": w1[D:2 * D], "L3_gnn_W2a": w2[0:D], "L3_gnn_W2b": w2[D:],
              "L3_gnn_W3a": w3[0:D], "L3_gnn_W3b": w3[D:], "L3_gnn_Wn1a": wn1[0:D], "L3_gnn_Wn1b": wn1[D:],
              "L3_gnn_Wn2a": wn2[0:D], "L3_gnn_Wn2b": wn2[D:]})
    dst = padded(a["dst"].astype(np.int32), NPAD).reshape(GROUPS, GROUP_EDGES)
    src = padded(a["src"].astype(np.int32), 0).reshape(GROUPS, GROUP_EDGES)
    bn1 = a["L3_gnn_bn1"]
    arrays = {
        "consts": consts,
        "x": np.concatenate([a["x"], np.zeros((NPAD - NODES, D), np.float32)]),
        "dst": dst,
        "dst_last": np.ascontiguousarray(dst[:, -1]).reshape(1, GROUPS),
        "src": src,
        "edge_weight": padded(a["edge_weight1"][:, 0], 0).reshape(GROUPS, GROUP_EDGES),
        "edge_attr": np.ascontiguousarray(padded(a["edge_attr_32"], 0).reshape(GROUPS, GROUP_EDGES, EDGE_D).transpose(0, 2, 1)),
        "biases": np.concatenate([spread(a[n]) for n, _ in BIASES], axis=1),
        "weights": np.concatenate([a[n] for n, _ in WEIGHTS], axis=1),
        "cols": np.stack([a["L0_gnn_att"][0], a["L0_gnn_att"][1], a["L1_gnn_att"], a["L1_gnn_bn_gamma"],
                          a["L1_gnn_bn_beta"], bn1[0:D], bn1[D:], a["L3_gnn_bn2"]], axis=1),
        "edge_w1": w1[2 * D:],
        "we": a["L1_gnn_We"],
        "gine_w": np.stack([a["L2_gnn_W1"], a["L2_gnn_W2"]]).transpose(2, 1, 0, 3),
        "gine_lin": a["L2_gnn_W_lin"],
        "gine_blin": a["L2_gnn_b_lin"],
        "gine_cols": np.stack([a["L2_gnn_b1"], a["L2_gnn_b2"], a["L2_gnn_gamma"], a["L2_gnn_beta"]]).transpose(2, 1, 0),
    }
    arrays = {k: np.ascontiguousarray(v) for k, v in arrays.items()}
    nc = bacc.Bacc("TRN2", target_bir_lowering=False, num_devices=1)
    t = {k: nc.dram_tensor(f"in_{k}", v.shape, mybir.dt.from_np(v.dtype), kind="ExternalInput").ap()
         for k, v in arrays.items()}
    t["out"] = nc.dram_tensor("out", (NODES, D), F32, kind="ExternalOutput").ap()
    build(nc, t)
    r = run_bass_kernel_spmd(nc, [{f"in_{k}": v for k, v in arrays.items()}], core_ids=[0])
    return r.results[0]["out"]
```

```python
from contextlib import ExitStack

import numpy as np
import concourse.bass as bass
from concourse import mybir

F32 = mybir.dt.float32
BF16 = mybir.dt.bfloat16
I32 = mybir.dt.int32
ALU = mybir.AluOpType
ACT = mybir.ActivationFunctionType
AX = mybir.AxisListType.X

P = 128
NODES, EDGES, D = 3125, 50000, 128
EDGE_D, HID, HEADS, GINE_LAYERS = 32, 256, 2, 3
NODE_BLOCKS = -(-NODES // P)
NPAD = NODE_BLOCKS * P
SUBS = 4
GROUP_EDGES = SUBS * P
GROUPS = -(-EDGES // GROUP_EDGES)
ITEMS = GROUPS + NODE_BLOCKS - 1
PAIRS = ITEMS // 2
assert ITEMS % 2 == 0 and ITEMS <= P
SPLIT = 3
MASKED = -1e30
FLOOR = -1e20

C_IDENT, C_IOTA, C_ROW = 0, P, 2 * P
C_WIDTH = 2 * P + 1
BIASES = [("L0_gnn_gamma", D), ("L0_gnn_beta", D), ("L0_gnn_bl", 2 * D), ("L0_gnn_br", 2 * D),
          ("L0_gnn_bias", D), ("L1_gnn_bl", D), ("L1_gnn_br", D), ("L1_gnn_bias_out", D),
          ("L3_gnn_b1", HID), ("L3_gnn_b2", HID), ("L3_gnn_b3", D), ("L3_gnn_gamma", D),
          ("L3_gnn_beta", D)]
BIAS_AT, at = {}, 0
for _name, _n in BIASES:
    BIAS_AT[_name] = (at, _n)
    at += _n
BIAS_WIDTH = at
COLS = ["att0", "att1", "att2", "bn_gamma", "bn_beta", "bn1a", "bn1b", "bn2"]
GINE_COLS = 4
WEIGHTS = [("L0_gnn_Wl", 2 * D), ("L0_gnn_Wr", 2 * D), ("L0_gnn_res_W", D), ("L1_gnn_Wl", D),
           ("L1_gnn_Wr", D), ("L3_gnn_W1a", HID), ("L3_gnn_W1b", HID), ("L3_gnn_W2a", HID),
           ("L3_gnn_W2b", HID), ("L3_gnn_W3a", D), ("L3_gnn_W3b", D), ("L3_gnn_Wn1a", HID),
           ("L3_gnn_Wn1b", HID), ("L3_gnn_Wn2a", D), ("L3_gnn_Wn2b", D)]
WEIGHT_AT, at = {}, 0
for _name, _n in WEIGHTS:
    WEIGHT_AT[_name] = (at, _n)
    at += _n
WEIGHT_WIDTH = at


def build(nc, t):
    with ExitStack() as ctx:
        def sb(name, shape, dt=F32):
            return ctx.enter_context(nc.sbuf_tensor(name, shape, dt))

        def sem(name):
            return ctx.enter_context(nc.semaphore(name))

        def scratch(name, shape, dt=F32):
            return nc.dram_tensor(name, shape, dt, kind="Internal").ap()

        table = scratch("source_rows", (NPAD, 2 * D))
        table1 = scratch("source_rows_narrow", (NPAD, D))
        rel_rows = scratch("rel_rows", (ITEMS, GROUP_EDGES), BF16)
        weight_rows = scratch("weight_rows", (ITEMS, GROUP_EDGES))
        group_block = scratch("group_block", (ITEMS, 3), I32)

        consts = sb("consts", [P, C_WIDTH])
        ident = consts[:, C_IDENT:C_IDENT + P]
        iota = consts[:, C_IOTA:C_IOTA + P]
        row = consts[:, C_ROW:C_ROW + 1]
        bias_all = sb("bias_all", [P, BIAS_WIDTH])
        weight_all = sb("weight_all", [P, WEIGHT_WIDTH])
        cols = sb("cols", [P, len(COLS)])
        gine_cols = sb("gine_cols", [P, GINE_COLS])
        gine_w = sb("gine_w", [P, 2, D])
        gine_lin = sb("gine_lin", [EDGE_D, D])
        gine_blin = sb("gine_blin", [P, D])
        edge_w1 = sb("edge_w1", [EDGE_D, HID])
        we_row = sb("we_row", [1, D])
        att_b = sb("att_b", [P, 3, P])
        X = sb("X", [P, NODE_BLOCKS, D])
        Y = sb("Y", [P, NODE_BLOCKS, D])
        XT = sb("XT", [P, NPAD])
        TMP = sb("TMP", [P, NODE_BLOCKS, D])
        ACC = sb("ACC", [P, NODE_BLOCKS * 2 * D])
        XR = sb("XR", [P, NODE_BLOCKS, SPLIT, 2 * D], BF16)
        stage = sb("stage", [P, 4, 2 * D])
        stage_r = sb("stage_r", [P, 4, 2 * D])
        zsum = sb("zsum", [P, NODE_BLOCKS, 2])
        mmax = sb("mmax", [P, NODE_BLOCKS, 2])
        stat = sb("stat", [P, 4, NODE_BLOCKS])
        groups_blocks = sb("groups_blocks", [1, ITEMS, 3], I32)
        group_end = sb("group_end", [1, GROUPS], I32)
        idx_all = sb("idx_all", [P, ITEMS, SUBS], I32)
        rel_all = sb("rel_all", [P, ITEMS, SUBS])
        idx = sb("idx", [P, 4, SUBS], I32)
        rel = sb("rel", [P, 2, GROUP_EDGES], BF16)
        wrow = sb("wrow", [1, 2, GROUP_EDGES])
        gath = sb("gath", [P, 4, SUBS, 2 * D])
        hot_t = sb("hot_t", [P, 2, GROUP_EDGES], BF16)
        hot = sb("hot", [P, 2, SUBS, P])
        neg = sb("neg", [P, 2, GROUP_EDGES], BF16)
        ea = sb("ea", [EDGE_D, 2, GROUP_EDGES])
        vs = sb("vs", [P, 2, GROUP_EDGES])
        lk = sb("lk", [P, 2, GROUP_EDGES])
        sm = sb("sm", [P, 2, GROUP_EDGES])
        pm = sb("pm", [P, 2, GROUP_EDGES])
        pt = sb("pt", [P, 2, SUBS, P])
        small = sb("small", [P, 8, 2])
        MI, MNEW, NEGM, DM = (small[:, k, :] for k in range(4))
        factors = sb("factors", [P, 2, 2, 2])
        SCL = [factors[:, s, 0, :] for s in range(2)]
        ZI = [factors[:, s, 1, :] for s in range(2)]

        psum = ctx.enter_context(nc.psum_tensor("psum", [P, 8, 512], F32))

        consts_in = sem("consts_in")

        def wait(e, s, value):
            if not (isinstance(value, int) and value <= 0):
                e.wait_ge(s, value)

        def hold(e, *waits):
            waits = [(s, v if isinstance(v, int) else e.snap(e.to_reg(v))) for s, v in waits]
            e.wait_ge(consts_in, 16)
            for s, v in waits:
                wait(e, s, v)

        def place(quad, m, layer):
            return m % 2, layer * PAIRS + 2 * quad + m // 2, m, layer * -(-(ITEMS - m) // 4) + quad

        def in_order(e, body, layer=0):
            for i in range(5):
                body(i, *place(i // 4, i % 4, layer))
            with e.Fori(0, (ITEMS - 6) // 4) as k:
                for q in range(4):
                    body(4 * k + 5 + q, *place(k + (5 + q) // 4, (5 + q) % 4, layer))
            body(ITEMS - 1, *place((ITEMS - 1) // 4, (ITEMS - 1) % 4, layer))

        def nothing(*_):
            pass

        def walk(e, front, back=nothing, mid=nothing, tail=nothing, layer=0):
            def step(i, *places):
                front(i, *places[0])
                if len(places) > 2:
                    tail(i - 2, *places[2])
                if len(places) > 1:
                    back(i - 1, *places[1])
                mid(i, *places[0])

            def place_of(i):
                return place(i // 4, i % 4, layer)

            for i in range(5):
                step(i, *(place_of(i - lag) for lag in range(min(i, 2) + 1)))
            with e.Fori(0, (ITEMS - 6) // 4) as k:
                for q in range(5, 9):
                    step(4 * k + q, *(place(k + (q - lag) // 4, (q - lag) % 4, layer) for lag in range(3)))
            last = ITEMS - 1
            step(last, *(place_of(last - lag) for lag in range(3)))
            tail(last - 1, *place_of(last - 1))
            back(last, *place_of(last))
            tail(last, *place_of(last))

        def bias(name):
            a, n = BIAS_AT[name]
            return bias_all[:, a:a + n]

        def weight(name):
            a, n = WEIGHT_AT[name]
            return weight_all[:, a:a + n]

        def col(name):
            k = COLS.index(name)
            return cols[:, k:k + 1]

        def over_blocks(v):
            return v.unsqueeze(1).broadcast_to([P, NODE_BLOCKS, v.shape[1]])

        def over_features(v):
            return v.unsqueeze(2).broadcast_to([P, NODE_BLOCKS, D])

        def setup():
            loads = sem("setup_loads")
            last_in = sem("last_in")
            dve = sem("setup_dve")
            tables_out = sem("tables_out")
            rows_in = sem("rows_in")
            pe = sem("setup_pe")
            copied = sem("setup_copied")
            with ExitStack() as mine:
                last_i = mine.enter_context(nc.sbuf_tensor("last_i", [ITEMS, GROUPS], I32))
                gb_f = mine.enter_context(nc.sbuf_tensor("gb_f", [ITEMS, 4], F32))
                gb_i = mine.enter_context(nc.sbuf_tensor("gb_i", [ITEMS, 3], I32))
                last_f = vs[0:ITEMS, 0, 0:GROUPS]
                ew_i = vs[0:ITEMS, 1, :]
                dst_i = lk[0:ITEMS, 0, :].bitcast(I32)
                src_i = lk[0:ITEMS, 1, :].bitcast(I32)
                dst_f = sm[0:ITEMS, 0, :]
                src_f = sm[0:ITEMS, 1, :]
                rel_b = rel[0:ITEMS, 0, :]
                with nc.Block() as block:
                    @block.sync
                    def _(sp):
                        sp.dma_start(consts[:, :], t["consts"]).then_inc(consts_in, 16)
                        sp.dma_start(last_i[:, :], t["dst_last"].broadcast_to([ITEMS, GROUPS])).then_inc(last_in, 16)
                        sp.dma_start(X[:, :, :], t["x"].rearrange("(b p) d -> p b d", p=P)).then_inc(loads, 16)
                        sp.dma_start(bias_all[:, :], t["biases"]).then_inc(loads, 16)
                        sp.dma_start(weight_all[:, :], t["weights"]).then_inc(loads, 16)
                        sp.dma_start(cols[:, :], t["cols"]).then_inc(loads, 16)
                        sp.dma_start(edge_w1[:, :], t["edge_w1"]).then_inc(loads, 16)
                        sp.dma_start(we_row[:, :], t["we"]).then_inc(loads, 16)
                        sp.wait_ge(dve, 10)
                        sp.dma_start(group_block, gb_i[:, :]).then_inc(tables_out, 16)
                        sp.wait_ge(tables_out, 16)
                        sp.dma_start(groups_blocks[:, :, :], group_block.unsqueeze(0)).then_inc(loads, 16)
                        sp.wait_ge(dve, 14)
                        sp.dma_start(rel_rows, rel_b).then_inc(tables_out, 16)
                        sp.wait_ge(rows_in, 48)
                        sp.dma_start(weight_rows, ew_i).then_inc(tables_out, 16)
                        sp.wait_ge(tables_out, 48)
                        sp.wait_ge(loads, 7 * 16)

                    @block.gpsimd
                    def _(pool):
                        pool.wait_ge(dve, 10)
                        for rows, out in ((t["dst"], dst_i), (t["src"], src_i), (t["edge_weight"], ew_i)):
                            pool.indirect_dma_start(
                                out=out, out_offset=None, in_=rows,
                                in_offset=bass.IndirectOffsetOnAxis(ap=gb_i[:, 0:1], axis=0)).then_inc(rows_in, 16)
                        pool.wait_ge(rows_in, 48)

                    @block.vector
                    def _(v):
                        n = [0]

                        def step(ins):
                            n[0] += 1
                            ins.then_inc(dve, 1)
                            v.wait_ge(dve, n[0])

                        v.wait_ge(last_in, 16)
                        v.wait_ge(consts_in, 16)
                        step(v.tensor_scalar(last_i[:, :], last_i[:, :], 7, None, ALU.arith_shift_right))
                        step(v.tensor_copy(last_f, last_i[:, :]))
                        step(v.scalar_tensor_tensor(last_f, last_f, float(NODE_BLOCKS - 1),
                                                    iota[0:ITEMS, 0:GROUPS], ALU.min, ALU.add))
                        step(v.tensor_scalar(group_end[:, :], last_f[0:1, :], 1.0, None, ALU.add))
                        step(v.tensor_scalar(last_f, last_f, row[0:ITEMS, :], None, ALU.is_lt))
                        step(v.tensor_reduce(gb_f[:, 0:1], last_f, AX, ALU.add))
                        step(v.tensor_tensor(gb_f[:, 1:2], row[0:ITEMS, :], gb_f[:, 0:1], ALU.subtract))
                        step(v.tensor_copy(gb_i[:, 0:2], gb_f[:, 0:2]))
                        step(v.tensor_scalar(gb_i[:, 2:3], gb_i[:, 0:1], 3, None, ALU.bitwise_and))
                        step(v.tensor_scalar(gb_f[:, 2:3], gb_f[:, 1:2], float(P), None, ALU.mult))
                        v.wait_ge(rows_in, 48)
                        step(v.tensor_copy(dst_f, dst_i))
                        step(v.tensor_scalar(dst_f, dst_f, gb_f[:, 2:3], -1.0, ALU.subtract, ALU.max))
                        step(v.tensor_scalar(dst_f, dst_f, float(P), None, ALU.min))
                        step(v.tensor_copy(rel_b, dst_f))
                        step(v.tensor_copy(src_f, src_i))
                        v.wait_ge(pe, 1)
                        v.tensor_copy(rel_all[:, :, :].rearrange("p i j -> p j i"), psum[:, 0, :].rearrange("p (j i) -> p j i", j=SUBS)[:, :, 0:ITEMS])
                        v.tensor_copy(idx_all[:, :, :].rearrange("p i j -> p j i"), psum[:, 1, :].rearrange("p (j i) -> p j i", j=SUBS)[:, :, 0:ITEMS])
                        v.wait_ge(loads, 7 * 16)
                        for k in range(3):
                            v.tensor_copy(att_b[:, k, :], cols[:, k:k + 1].broadcast_to([P, P]))

                    @block.tensor
                    def _(e):
                        e.wait_ge(consts_in, 16)
                        e.wait_ge(dve, 15)
                        for k, rows in enumerate((dst_f, src_f)):
                            for j in range(SUBS):
                                last = e.transpose(psum[:, k, j * P:j * P + ITEMS], rows[:, j * P:(j + 1) * P],
                                                   ident[0:ITEMS, 0:ITEMS])
                        last.then_inc(pe, 1)

        setup()

        ln_dve, ln_act, ln_steps, ln_calls = sem("layernorm_dve"), sem("layernorm_act"), [0], [0]

        def layernorm(src, dst, gamma=None, beta=None, relu=False, prep=None, prep_steps=0):
            base_v, base_a = ln_steps[0], 2 * ln_calls[0]
            ln_calls[0] += 1
            with nc.Block() as block:
                @block.vector
                def _(v):
                    def step(ins):
                        ln_steps[0] += 1
                        ins.then_inc(ln_dve, 1)
                        v.wait_ge(ln_dve, ln_steps[0])

                    if prep is not None:
                        prep(v, step)
                    assert ln_steps[0] == base_v + prep_steps
                    step(v.tensor_reduce(stat[:, 0, :], src, AX, ALU.add))
                    step(v.tensor_scalar(stat[:, 0, :], stat[:, 0, :], 1.0 / D, None, ALU.mult))
                    step(v.tensor_tensor(dst, src, over_features(stat[:, 0, :]), ALU.subtract))
                    v.wait_ge(ln_act, base_a + 1)
                    step(v.tensor_reduce(stat[:, 1, :], TMP[:, :, :], AX, ALU.add))
                    step(v.tensor_scalar(stat[:, 1, :], stat[:, 1, :], 1.0 / D, 1e-5, ALU.mult, ALU.add))
                    v.wait_ge(ln_act, base_a + 2)
                    step(v.reciprocal(stat[:, 3, :], stat[:, 2, :]))
                    step(v.tensor_tensor(dst, dst, over_features(stat[:, 3, :]), ALU.mult))
                    if gamma is not None:
                        step(v.tensor_tensor(dst, dst, over_blocks(gamma), ALU.mult))
                        step(v.tensor_tensor(dst, dst, over_blocks(beta), ALU.add))
                    if relu:
                        step(v.tensor_scalar(dst, dst, 0.0, None, ALU.max))

                @block.scalar
                def _(a):
                    a.wait_ge(ln_dve, base_v + prep_steps + 3)
                    a.activation(TMP[:, :, :], dst, ACT.Square).then_inc(ln_act, 1)
                    a.wait_ge(ln_dve, base_v + prep_steps + 5)
                    a.activation(stat[:, 2, :], stat[:, 1, :], ACT.Sqrt).then_inc(ln_act, 1)

        CH = 5
        turned_, taken_, moves = sem("turned"), sem("taken"), [0]

        def transposes(src, dst, turned=turned_, taken=taken_, base=None):
            if base is None:
                base = moves[0]
                moves[0] += NODE_BLOCKS // CH
            with nc.Block() as block:
                @block.tensor
                def _(e):
                    for c in range(NODE_BLOCKS // CH):
                        if c >= 2:
                            hold(e, (taken, base + c - 1))
                        for k in range(CH):
                            b = c * CH + k
                            o = psum[:, 2 * (c % 2) + k // 4, (k % 4) * P:(k % 4 + 1) * P]
                            last = e.transpose(o, src[:, b * P:(b + 1) * P], ident)
                        last.then_inc(turned, 1)

                @block.scalar
                def _(a):
                    for c in range(NODE_BLOCKS // CH):
                        wait(a, turned, base + c + 1)
                        half = psum[:, 2 * (c % 2):2 * (c % 2) + 2, :].rearrange("p a n -> p (a n)")
                        a.activation(dst[:, c * CH * P:(c + 1) * CH * P], half[:, 0:CH * P], ACT.Copy).then_inc(taken, 1)

        def flat(buf):
            return buf[:, :, :].rearrange("p b d -> p (b d)")

        CB = 4
        CHUNKS = -(-NODE_BLOCKS // CB)

        def tables(name, width, w_src, b_src, w_dst, b_dst, dram, extra=None):
            made, staged, split_a, split_v, stored, eb = (sem(f"{name}_{k}") for k in (
                "made", "staged", "split_a", "split_v", "stored", "extra"))
            rows = dram.rearrange("(b p) d -> p b d", p=P)
            per = 512 // width
            STG = 2 if extra is None else 3

            def place(bank0, k):
                return psum[:, bank0 + k // per, (k % per) * width:(k % per + 1) * width]

            def banks(bank0, n):
                v = psum[:, bank0:bank0 + CB // per, :].rearrange("p a (k w) -> p (a k) w", w=width)
                return v[:, 0:n, :]

            def bias_of(b, n):
                return b.unsqueeze(1).broadcast_to([P, n, b.shape[1]])

            with nc.Block() as block:
                @block.tensor
                def _(e):
                    for c in range(CHUNKS):
                        wait(e, staged, STG * c)
                        for k in range(min(CB, NODE_BLOCKS - c * CB)):
                            b = c * CB + k
                            xt = XT[:, b * P:(b + 1) * P]
                            e.matmul(place(0, k), xt, w_src, start=True, stop=True)
                            last = e.matmul(place(2, k), xt, w_dst, start=True, stop=True)
                            if extra is not None:
                                last = e.matmul(psum[:, 4, k * D:(k + 1) * D], xt, extra[0], start=True, stop=True)
                        last.then_inc(made, 1)

                @block.vector
                def _(v):
                    for c in range(CHUNKS):
                        n = min(CB, NODE_BLOCKS - c * CB)
                        v.wait_ge(made, c + 1)
                        wait(v, stored, 16 * c)
                        v.tensor_tensor(stage[:, 0:n, 0:width], banks(0, n), bias_of(b_src, n), ALU.add).then_inc(staged, 1)
                        wait(v, split_v, 2 * c)
                        if b_dst is None:
                            v.tensor_copy(stage_r[:, 0:n, 0:width], banks(2, n)).then_inc(staged, 1)
                        else:
                            v.tensor_tensor(stage_r[:, 0:n, 0:width], banks(2, n), bias_of(b_dst, n), ALU.add).then_inc(staged, 1)
                        if extra is not None:
                            y = Y[:, c * CB:c * CB + n, :]
                            v.tensor_tensor(y, psum[:, 4, 0:n * D].rearrange("p (k d) -> p k d", d=D), bias_of(extra[1], n), ALU.add).then_inc(eb, 1)
                            v.wait_ge(eb, c + 1)
                            v.scalar_tensor_tensor(y, X[:, c * CB:c * CB + n, :], 2.0, y, ALU.mult, ALU.add).then_inc(staged, 1)
                        r = stage_r[:, 0:n, 0:width]
                        x = XR[:, c * CB:c * CB + n, :, 0:width]
                        v.wait_ge(split_a, 2 * c + 1)
                        v.tensor_tensor(r, r, x[:, :, 0, :], ALU.subtract).then_inc(split_v, 1)
                        v.wait_ge(split_a, 2 * c + 2)
                        v.wait_ge(split_v, 2 * c + 1)
                        v.tensor_tensor(x[:, :, 2, :], r, x[:, :, 1, :], ALU.subtract).then_inc(split_v, 1)

                @block.scalar
                def _(a):
                    for c in range(CHUNKS):
                        n = min(CB, NODE_BLOCKS - c * CB)
                        r = stage_r[:, 0:n, 0:width]
                        x = XR[:, c * CB:c * CB + n, :, 0:width]
                        a.wait_ge(staged, STG * c + 2)
                        a.activation(x[:, :, 0, :], r, ACT.Copy).then_inc(split_a, 1)
                        a.wait_ge(split_v, 2 * c + 1)
                        a.activation(x[:, :, 1, :], r, ACT.Copy).then_inc(split_a, 1)

                @block.sync
                def _(sp):
                    for c in range(CHUNKS):
                        n = min(CB, NODE_BLOCKS - c * CB)
                        sp.wait_ge(staged, STG * c + 1)
                        sp.dma_start(rows[:, c * CB:c * CB + n, :], stage[:, 0:n, 0:width]).then_inc(stored, 16)
                    sp.wait_ge(stored, 16 * CHUNKS)

        def gat_edges(name, heads, dram, att, with_weight):
            width = heads * D
            acc = ACC[:, 0:NODE_BLOCKS * width].rearrange("p (b h d) -> p b h d", h=heads, d=D)
            idx_in = [sem(f"{name}_idx_in{s}") for s in range(4)]
            rel_in = [sem(f"{name}_rel_in{s}") for s in range(2)]
            w_in = [sem(f"{name}_w_in{s}") for s in range(2)]
            gathered = [sem(f"{name}_gathered{s}") for s in range(4)]
            cleared, masks, v_ready, v_copied, leaked, s_ready, s_masked, max_step, max_done, p_ready, scl_ready, \
                pt_ready, pt_copied, o_ready, acc_done = (sem(f"{name}_{k}") for k in (
                    "cleared", "masks", "v_ready", "v_copied", "leaked", "s_ready", "s_masked", "max_step",
                    "max_done", "p_ready", "scl_ready", "pt_ready", "pt_copied", "o_ready", "acc_done"))
            V = [psum[:, h, :] for h in range(heads)]
            S = [psum[:, 2 + h, :] for h in range(heads)]
            T = [psum[:, 4 + h, :] for h in range(heads)]
            O = [psum[:, 6 + h, 0:D] for h in range(heads)]

            def block_of(e, i):
                return e.value_load(groups_blocks[0:1, bass.ds(i, 1), 1], min_val=0, max_val=NODE_BLOCKS - 1)

            with nc.Block() as block:
                @block.sync
                def _(sp):
                    def item(i, s, turn, s4, turn4):
                        wait(sp, gathered[s4], 16 * SUBS * turn4)
                        sp.dma_start(idx[:, s4, :], idx_all[:, bass.ds(i, 1), :].rearrange("p a j -> p (a j)")).then_inc(idx_in[s4], 16)
                        wait(sp, masks, i - 1)
                        sp.dma_start(rel[:, s, :], rel_rows[bass.ds(i, 1), :].broadcast_to([P, GROUP_EDGES])).then_inc(rel_in[s], 16)
                        if with_weight:
                            hold(sp, (v_ready, heads * (i - 1)))
                            sp.dma_start(wrow[:, s, :], weight_rows[bass.ds(i, 1), :]).then_inc(w_in[s], 16)

                    in_order(sp, item)

                @block.gpsimd
                def _(pool):
                    def item(i, s, turn, s4, turn4):
                        hold(pool, (idx_in[s4], 16 * (turn4 + 1)),
                             (o_ready, heads * (i - 3)))
                        for j in range(SUBS):
                            pool.indirect_dma_start(
                                out=gath[:, s4, j, 0:width], out_offset=None, in_=dram,
                                in_offset=bass.IndirectOffsetOnAxis(ap=idx[:, s4, j:j + 1], axis=0)).then_inc(gathered[s4], 16)

                    in_order(pool, item)

                @block.tensor
                def _(e):
                    def front(i, s, turn, s4, turn4):
                        b = block_of(e, i)
                        late = [(w_in[s], 16 * (turn + 1))] if with_weight else []
                        hold(e, (masks, i + 1), (gathered[s4], 16 * SUBS * (turn4 + 1)), *late)
                        for h in range(heads):
                            for k in range(SPLIT):
                                e.matmul(V[h], XR[:, bass.ds(b, 1), k, h * D:(h + 1) * D].rearrange("p a d -> p (a d)"), hot_t[:, s, :],
                                         start=(k == 0), stop=False)
                            if with_weight:
                                e.matmul(V[h], we_row[:, :], wrow[:, s, :], start=False, stop=False)
                            for j in range(SUBS):
                                last = e.matmul(V[h][:, j * P:(j + 1) * P], gath[:, s4, j, h * D:(h + 1) * D],
                                                ident, start=False, stop=(j == SUBS - 1))
                            last.then_inc(v_ready, 1)

                    def mid(i, s, turn, s4, turn4):
                        for h in range(heads):
                            e.wait_ge(leaked, heads * i + h + 1)
                            e.matmul(S[h], att_b[:, att[h], :], lk[:, h, :], start=True, stop=True).then_inc(s_ready, 1)

                    def back(i, s, turn, s4, turn4):
                        for h in range(heads):
                            e.wait_ge(p_ready, heads * i + h + 1)
                            for j in range(SUBS):
                                last = e.transpose(T[h][:, j * P:(j + 1) * P], pm[:, h, j * P:(j + 1) * P], ident)
                            last.then_inc(pt_ready, 1)

                    def tail(i, s, turn, s4, turn4):
                        wait(e, acc_done, i)
                        for h in range(heads):
                            e.wait_ge(pt_copied, heads * i + h + 1)
                            for j in range(SUBS):
                                last = e.matmul(O[h], pt[:, h, j, :], gath[:, s4, j, h * D:(h + 1) * D],
                                                start=(j == 0), stop=(j == SUBS - 1))
                            last.then_inc(o_ready, 1)

                    walk(e, front, back, mid, tail)

                @block.scalar
                def _(a):
                    def front(i, s, turn, s4, turn4):
                        for h in range(heads):
                            wait(a, leaked, heads * (i - 1) + h + 1)
                            a.wait_ge(v_ready, heads * i + h + 1)
                            a.activation(vs[:, h, :], V[h], ACT.Copy).then_inc(v_copied, 1)

                    def mid(i, s, turn, s4, turn4):
                        a.wait_ge(max_done, i + 1)
                        wait(a, acc_done, i - 1)
                        for h in range(heads):
                            a.activation(pm[:, h, :], sm[:, h, :], ACT.Exp, bias=NEGM[:, h:h + 1],
                                         accum_out=ZI[s][:, h:h + 1]).then_inc(p_ready, 1)
                        a.activation(SCL[s][:, 0:heads], DM[:, 0:heads], ACT.Exp).then_inc(scl_ready, 1)

                    def back(i, s, turn, s4, turn4):
                        for h in range(heads):
                            a.wait_ge(pt_ready, heads * i + h + 1)
                            wait(a, o_ready, heads * i)
                            a.activation(pt[:, h, :, :].rearrange("p j n -> p (j n)"), T[h], ACT.Copy).then_inc(pt_copied, 1)

                    walk(a, front, back, mid)

                @block.vector
                def _(v):
                    v.memset(ACC[:, 0:NODE_BLOCKS * width], 0.0)
                    v.memset(zsum[:, :, :], 0.0)
                    v.memset(mmax[:, :, :], FLOOR).then_inc(cleared, 1)
                    v.wait_ge(cleared, 1)

                    def mask(i, s, turn):
                        v.wait_ge(rel_in[s], 16 * (turn + 1))
                        wait(v, v_ready, heads * (i - 1))
                        wait(v, s_masked, heads * (i - 1))
                        v.tensor_scalar(neg[:, s, :], rel[:, s, :], row, MASKED, ALU.not_equal, ALU.mult)
                        v.tensor_scalar(hot_t[:, s, :], rel[:, s, :], row, None, ALU.is_equal).then_inc(masks, 1)

                    def front(i, s, turn, s4, turn4):
                        blocks["item"] = block_of(v, i)
                        if not isinstance(i, int) or i >= 2:
                            blocks["tail"] = block_of(v, i - 2)
                        for h in range(heads):
                            wait(v, s_ready, heads * (i - 1) + h + 1)
                            v.wait_ge(v_copied, heads * i + h + 1)
                            v.scalar_tensor_tensor(lk[:, h, :], V[h], 0.2, vs[:, h, :], ALU.mult, ALU.max).then_inc(leaked, 1)
                        if not (isinstance(i, int) and i == ITEMS - 1):
                            mask(i + 1, 1 - s, turn + s)

                    def mid(i, s, turn, s4, turn4):
                        b = blocks["item"]
                        for h in range(heads):
                            hold(v, (p_ready, heads * i),
                                 (scl_ready, i), (s_ready, heads * i + h + 1))
                            v.tensor_tensor_reduce(out=sm[:, h, :], in0=S[h], in1=neg[:, s, :], scale=1.0, scalar=MASKED,
                                                   op0=ALU.add, op1=ALU.max, accum_out=MI[:, h:h + 1]).then_inc(s_masked, 1)
                        old = mmax[:, bass.ds(b, 1), 0:heads].rearrange("p a h -> p (a h)")
                        new = MNEW[:, 0:heads]
                        v.wait_ge(s_masked, heads * (i + 1))
                        wait(v, max_done, i)
                        v.tensor_tensor(new, old, MI[:, 0:heads], ALU.max).then_inc(max_step, 1)
                        v.wait_ge(max_step, 2 * i + 1)
                        v.tensor_tensor(DM[:, 0:heads], old, new, ALU.subtract).then_inc(max_step, 1)
                        v.tensor_scalar(NEGM[:, 0:heads], new, -1.0, None, ALU.mult)
                        hold(v, (max_step, 2 * i + 2))
                        v.tensor_copy(old, new).then_inc(max_done, 1)

                    def tail(i, s, turn, s4, turn4):
                        b = blocks.pop("tail") if "tail" in blocks else block_of(v, i)
                        v.wait_ge(scl_ready, i + 1)
                        v.wait_ge(p_ready, heads * (i + 1))
                        wait(v, acc_done, i)
                        for h in range(heads):
                            v.wait_ge(o_ready, heads * i + h + 1)
                            a_h = acc[:, bass.ds(b, 1), h, :].rearrange("p a d -> p (a d)")
                            z_h = zsum[:, bass.ds(b, 1), h:h + 1].rearrange("p a h -> p (a h)")
                            v.scalar_tensor_tensor(a_h, a_h, SCL[s][:, h:h + 1], O[h], ALU.mult, ALU.add)
                            last = v.scalar_tensor_tensor(z_h, z_h, SCL[s][:, h:h + 1], ZI[s][:, h:h + 1], ALU.mult, ALU.add)
                        last.then_inc(acc_done, 1)

                    blocks = {}
                    mask(0, 0, 0)
                    walk(v, front, mid=mid, tail=tail)

        gi = {k: sem(f"gine_{k}") for k in (
            "hot_done", "e_ready", "added", "msg", "o_ready", "acc_done", "cleared")}
        gi_idx = [sem(f"gine_idx_in{s}") for s in range(4)]
        gi_ea = [sem(f"gine_ea_in{s}") for s in range(2)]
        gi_gath = [sem(f"gine_gathered{s}") for s in range(4)]
        gi_landed = sem("gine_landed")
        gine_stored = sem("gine_stored")

        def group_of(e, i):
            return e.value_load(groups_blocks[0:1, bass.ds(i, 1), 0], min_val=0, max_val=GROUPS - 1)

        def block_of(e, i):
            return e.value_load(groups_blocks[0:1, bass.ds(i, 1), 1], min_val=0, max_val=NODE_BLOCKS - 1)

        def gine_edges(layer):
            acc = ACC[:, 0:NPAD]
            done = layer * ITEMS
            turns = layer * PAIRS
            E = [psum[:, s, :] for s in range(2)]
            O = [psum[:, 2 + s, 0:P] for s in range(2)]
            with nc.Block() as block:
                def turn_of(slot, round):
                    return layer * -(-(GROUPS - slot) // 4) + round

                def by_group(e, body):
                    for g in range(4):
                        body(g, g, 0)
                    with e.Fori(0, (GROUPS - 4) // 4) as k:
                        for q in range(4):
                            body(4 * k + 4 + q, q, k + 1)
                    for g in range(GROUPS - GROUPS % 4, GROUPS):
                        body(g, g % 4, g // 4)

                @block.sync
                def _(sp):
                    def group(g, slot, round):
                        if not isinstance(g, int) or g >= 4:
                            end = sp.value_load(group_end[0:1, bass.ds(g - 4, 1)], min_val=1, max_val=ITEMS)
                            sp.wait_ge(gi["added"], done + end)
                        sp.wait_ge(gi_gath[slot], 16 * SUBS * turn_of(slot, round))
                        sp.dma_start(idx[:, slot, :], t["src_by_group"][bass.ds(g, 1), :, :].rearrange("a p j -> (a p) j")).then_inc(gi_idx[slot], 16)

                    by_group(sp, group)

                @block.gpsimd
                def _(pool):
                    def landed(slot, round):
                        pool.wait_ge(gi_gath[slot], 16 * SUBS * (turn_of(slot, round) + 1))
                        pool.nop().then_inc(gi_landed, 1)

                    def group(g, slot, round):
                        hold(pool, (gi_idx[slot], 16 * (turn_of(slot, round) + 1)), (gine_stored, 16 * (layer + 1)))
                        for j in range(SUBS):
                            pool.indirect_dma_start(
                                out=gath[:, slot, j, 0:D], out_offset=None, in_=table1,
                                in_offset=bass.IndirectOffsetOnAxis(ap=idx[:, slot, j:j + 1], axis=0)).then_inc(gi_gath[slot], 16)
                        if not (isinstance(g, int) and g == 0):
                            landed((slot - 1) % 4, round - (1 if slot == 0 else 0))
                        if isinstance(g, int) and g == GROUPS - 1:
                            landed(slot, round)

                    by_group(pool, group)

                @block.tensor
                def _(e):
                    def front(i, s, turn, s4, turn4):
                        n = done + i
                        e.wait_ge(gi_ea[s], 16 * (turn + 1))
                        for j in range(SUBS):
                            last = e.matmul(E[s][:, j * D:(j + 1) * D], ea[:, s, j * P:(j + 1) * P], gine_lin[:, :],
                                            start=True, stop=True)
                        last.then_inc(gi["e_ready"], 1)

                    def back(i, s, turn, s4, turn4):
                        n = done + i
                        e.wait_ge(gi["msg"], n + 1)
                        e.wait_ge(gi["hot_done"], n + 1)
                        e.wait_ge(gi["acc_done"], n)
                        for j in range(SUBS):
                            last = e.matmul(O[s], pm[:, s, j * P:(j + 1) * P], hot[:, s, j, :], start=(j == 0), stop=(j == SUBS - 1))
                        last.then_inc(gi["o_ready"], 1)

                    walk(e, front, back, layer=layer)

                @block.vector
                def _(v):
                    v.memset(acc, 0.0).then_inc(gi["cleared"], 1)
                    v.wait_ge(gi["cleared"], layer + 1)

                    def front(i, s, turn, s4, turn4):
                        n = done + i
                        if not isinstance(i, int) or i >= 2:
                            v.wait_ge(gi["o_ready"], done + i - 1)
                        v.tensor_tensor(hot[:, s, :, :], iota.unsqueeze(1).broadcast_to([P, SUBS, P]),
                                        rel_all[:, bass.ds(i, 1), :].rearrange("p a j -> p (a j)").unsqueeze(2).broadcast_to([P, SUBS, P]),
                                        ALU.is_equal).then_inc(gi["hot_done"], 1)
                        g = group_of(v, i)
                        slot = v.value_load(groups_blocks[0:1, bass.ds(i, 1), 2], min_val=0, max_val=3)
                        v.wait_ge(gi_landed, layer * GROUPS + g + 1)
                        if not isinstance(i, int) or i >= 2:
                            v.wait_ge(gi["msg"], done + i - 1)
                        v.wait_ge(gi["e_ready"], n + 1)
                        v.tensor_tensor(vs[:, s, :].rearrange("p (j d) -> p j d", j=SUBS), E[s].rearrange("p (j d) -> p j d", j=SUBS),
                                        gath[:, bass.ds(slot, 1), :, 0:D].rearrange("p a j d -> p (a j) d"), ALU.add).then_inc(gi["added"], 1)

                    def back(i, s, turn, s4, turn4):
                        n = done + i
                        b = block_of(v, i)
                        v.wait_ge(gi["acc_done"], n + 1)
                        v.wait_ge(gi["o_ready"], n + 1)
                        a_b = acc[:, bass.ds(b * P, P)]
                        v.tensor_tensor(a_b, a_b, O[s], ALU.add).then_inc(gi["acc_done"], 1)

                    walk(v, front, back, layer=layer)

                @block.scalar
                def _(a):
                    def load(i, s):
                        g = group_of(a, i)
                        if not isinstance(i, int) or i >= 2:
                            a.wait_ge(gi["e_ready"], done + i - 1)
                        a.dma_start(ea[:, s, :], t["edge_attr"][bass.ds(g, 1), :, :].rearrange("a k e -> (a k) e")).then_inc(gi_ea[s], 16)

                    load(0, 0)

                    def item(i, s, turn, s4, turn4):
                        n = done + i
                        if not (isinstance(i, int) and i == ITEMS - 1):
                            load(i + 1, 1 - s)
                        if not isinstance(i, int) or i >= 2:
                            a.wait_ge(gi["o_ready"], n - 1)
                        a.wait_ge(gi["added"], n + 1)
                        a.activation(pm[:, s, :], vs[:, s, :], ACT.Relu).then_inc(gi["msg"], 1)

                    in_order(a, item, layer)

        def mlp_edges():
            acc = [ACC[:, h * NPAD:(h + 1) * NPAD] for h in range(2)]
            idx_in = [sem(f"mlp_idx_in{s}") for s in range(4)]
            rel_in = [sem(f"mlp_rel_in{s}") for s in range(2)]
            ea_in = [sem(f"mlp_ea_in{s}") for s in range(2)]
            gathered = [sem(f"mlp_gathered{s}") for s in range(4)]
            cleared, hot_t_done, hot_done, h1_ready, h1_done, h2_ready, h2_added, h2_done, o_ready, acc_done, deg_step = (
                sem(f"mlp_{k}") for k in ("cleared", "hot_t_done", "hot_done", "h1_ready", "h1_done", "h2_ready", "h2_added",
                                          "h2_done", "o_ready", "acc_done", "deg_step"))
            H1 = [psum[:, h, :] for h in range(2)]
            H2 = psum[:, 2:4, :].rearrange("p a n -> p (a n)").rearrange("p (j d) -> p j d", d=HID)
            O = psum[:, 4, 0:2 * P].rearrange("p (h n) -> p h n", h=2)
            h1 = pm
            h2a = TMP[:, 0:8, :].rearrange("p a d -> p (a d)").rearrange("p (j d) -> p j d", d=HID)
            h2 = TMP[:, 8:16, :].rearrange("p a d -> p (a d)").rearrange("p (j d) -> p j d", d=HID)
            w2 = [weight("L3_gnn_W2a"), weight("L3_gnn_W2b")]

            with nc.Block() as block:
                @block.sync
                def _(sp):
                    def item(i, s, turn, s4, turn4):
                        g = group_of(sp, i)
                        wait(sp, gathered[s4], 16 * SUBS * turn4)
                        sp.dma_start(idx[:, s4, :], idx_all[:, bass.ds(i, 1), :].rearrange("p a j -> p (a j)")).then_inc(idx_in[s4], 16)
                        wait(sp, hot_t_done, i - 1)
                        sp.dma_start(rel[:, s, :], rel_rows[bass.ds(i, 1), :].broadcast_to([P, GROUP_EDGES])).then_inc(rel_in[s], 16)
                        wait(sp, h1_ready, 2 * (i - 1))
                        sp.dma_start(ea[:, s, :], t["edge_attr"][bass.ds(g, 1), :, :].rearrange("a k e -> (a k) e")).then_inc(ea_in[s], 16)

                    in_order(sp, item)

                @block.gpsimd
                def _(pool):
                    def item(i, s, turn, s4, turn4):
                        hold(pool, (idx_in[s4], 16 * (turn4 + 1)),
                             (h1_ready, 2 * (i - 3)))
                        for j in range(SUBS):
                            pool.indirect_dma_start(
                                out=gath[:, s4, j, :], out_offset=None, in_=table,
                                in_offset=bass.IndirectOffsetOnAxis(ap=idx[:, s4, j:j + 1], axis=0)).then_inc(gathered[s4], 16)

                    in_order(pool, item)

                @block.tensor
                def _(e):
                    def front(i, s, turn, s4, turn4):
                        b = block_of(e, i)
                        hold(e, (ea_in[s], 16 * (turn + 1)),
                             (hot_t_done, i + 1),
                             (gathered[s4], 16 * SUBS * (turn4 + 1)))
                        for h in range(2):
                            for k in range(SPLIT):
                                e.matmul(H1[h], XR[:, bass.ds(b, 1), k, h * D:(h + 1) * D].rearrange("p a d -> p (a d)"), hot_t[:, s, :],
                                         start=(k == 0), stop=False)
                            e.matmul(H1[h], edge_w1[:, h * D:(h + 1) * D], ea[:, s, :], start=False, stop=False)
                            for j in range(SUBS):
                                last = e.matmul(H1[h][:, j * P:(j + 1) * P], gath[:, s4, j, h * D:(h + 1) * D],
                                                ident, start=False, stop=(j == SUBS - 1))
                            last.then_inc(h1_ready, 1)

                    def mid(i, s, turn, s4, turn4):
                        e.wait_ge(h1_done, 2 * (i + 1))
                        for j in range(SUBS):
                            for h in range(2):
                                last = e.matmul(H2[:, j, :], h1[:, h, j * P:(j + 1) * P], w2[h], start=(h == 0), stop=(h == 1))
                        last.then_inc(h2_ready, 1)

                    def back(i, s, turn, s4, turn4):
                        e.wait_ge(h2_done, i + 1)
                        e.wait_ge(hot_done, i + 1)
                        wait(e, acc_done, i)
                        for h in range(2):
                            for j in range(SUBS):
                                last = e.matmul(O[:, h, :], h2[:, j, h * D:(h + 1) * D], hot[:, s, j, :], start=(j == 0), stop=(j == SUBS - 1))
                        last.then_inc(o_ready, 1)

                    walk(e, front, back, mid)

                @block.scalar
                def _(a):
                    def front(i, s, turn, s4, turn4):
                        for h in range(2):
                            wait(a, h2_ready, i)
                            a.wait_ge(h1_ready, 2 * i + h + 1)
                            a.activation(h1[:, h, :], H1[h], ACT.Relu).then_inc(h1_done, 1)

                    def mid(i, s, turn, s4, turn4):
                        wait(a, o_ready, i)
                        a.wait_ge(h2_added, i + 1)
                        a.activation(h2, h2a, ACT.Relu).then_inc(h2_done, 1)

                    walk(a, front, mid=mid)

                @block.vector
                def _(v):
                    v.memset(ACC[:, :], 0.0)
                    v.memset(stat[:, 0, :], 0.0).then_inc(cleared, 1)
                    v.wait_ge(cleared, 1)

                    def make_hot_t(i, s, turn):
                        v.wait_ge(rel_in[s], 16 * (turn + 1))
                        wait(v, deg_step, 2 * i - 2)
                        wait(v, h1_ready, 2 * i - 2)
                        v.tensor_scalar(hot_t[:, s, :], rel[:, s, :], row, None, ALU.is_equal).then_inc(hot_t_done, 1)

                    def front(i, s, turn, s4, turn4):
                        b = block_of(v, i)
                        v.wait_ge(hot_t_done, i + 1)
                        wait(v, deg_step, 2 * i)
                        v.tensor_reduce(MI[:, 0:1], hot_t[:, s, :], AX, ALU.add).then_inc(deg_step, 1)
                        v.wait_ge(deg_step, 2 * i + 1)
                        d_b = stat[:, 0, bass.ds(b, 1)]
                        v.tensor_tensor(d_b, d_b, MI[:, 0:1], ALU.add).then_inc(deg_step, 1)
                        if not (isinstance(i, int) and i == ITEMS - 1):
                            make_hot_t(i + 1, 1 - s, turn + s)
                        wait(v, o_ready, i - 1)
                        v.tensor_tensor(hot[:, s, :, :], iota.unsqueeze(1).broadcast_to([P, SUBS, P]),
                                        rel_all[:, bass.ds(i, 1), :].rearrange("p a j -> p (a j)").unsqueeze(2).broadcast_to([P, SUBS, P]),
                                        ALU.is_equal).then_inc(hot_done, 1)

                    def mid(i, s, turn, s4, turn4):
                        wait(v, h2_done, i)
                        v.wait_ge(h2_ready, i + 1)
                        b2 = bias("L3_gnn_b2").unsqueeze(1).broadcast_to([P, SUBS, HID])
                        v.tensor_tensor(h2a, H2, b2, ALU.add).then_inc(h2_added, 1)

                    def back(i, s, turn, s4, turn4):
                        b = block_of(v, i)
                        wait(v, acc_done, i)
                        v.wait_ge(o_ready, i + 1)
                        for h in range(2):
                            a_b = acc[h][:, bass.ds(b * P, P)]
                            last = v.tensor_tensor(a_b, a_b, O[:, h, :], ALU.add)
                        last.then_inc(acc_done, 1)

                    make_hot_t(0, 0, 0)
                    walk(v, front, back, mid)

        layernorm(X[:, :, :], Y[:, :, :], gamma=bias("L0_gnn_gamma"), beta=bias("L0_gnn_beta"), relu=True)
        transposes(flat(Y), XT)
        tables("tab0", 2 * D, weight("L0_gnn_Wl"), bias("L0_gnn_bl"), weight("L0_gnn_Wr"), bias("L0_gnn_br"), table,
               extra=(weight("L0_gnn_res_W"), bias("L0_gnn_bias")))
        gat_edges("gat0", HEADS, table, (0, 1), with_weight=False)

        def mean_of_heads(v, step):
            acc = ACC[:, :].rearrange("p (b h d) -> p b h d", h=2, d=D)
            step(v.tensor_scalar(zsum[:, :, :], zsum[:, :, :], 1e-16, None, ALU.add))
            step(v.reciprocal(zsum[:, :, :], zsum[:, :, :]))
            for h in range(2):
                z = zsum[:, :, h:h + 1].broadcast_to([P, NODE_BLOCKS, D])
                step(v.tensor_tensor(acc[:, :, h, :], acc[:, :, h, :], z, ALU.mult))
            step(v.tensor_tensor(TMP[:, :, :], acc[:, :, 0, :], acc[:, :, 1, :], ALU.add))
            step(v.scalar_tensor_tensor(flat(Y), flat(TMP), 0.5, flat(Y), ALU.mult, ALU.add))

        layernorm(Y[:, :, :], X[:, :, :], prep=mean_of_heads, prep_steps=6)

        transposes(flat(X), XT)
        tables("tab1", D, weight("L1_gnn_Wl"), bias("L1_gnn_bl"), weight("L1_gnn_Wr"), bias("L1_gnn_br"), table1)
        gat_edges("gat1", 1, table1, (2,), with_weight=True)

        def gat1_sum():
            dve = sem("gat1_sum")
            acc = ACC[:, 0:NPAD].rearrange("p (b d) -> p b d", d=D)
            with nc.Block() as block:
                @block.vector
                def _(v):
                    n = [0]

                    def step(ins):
                        n[0] += 1
                        ins.then_inc(dve, 1)
                        v.wait_ge(dve, n[0])

                    step(v.tensor_scalar(zsum[:, :, :], zsum[:, :, :], 1e-16, None, ALU.add))
                    step(v.reciprocal(zsum[:, :, :], zsum[:, :, :]))
                    step(v.tensor_tensor(Y[:, :, :], acc, zsum[:, :, 0:1].broadcast_to([P, NODE_BLOCKS, D]), ALU.mult))
                    step(v.tensor_tensor(Y[:, :, :], Y[:, :, :], X[:, :, :], ALU.add))
                    step(v.tensor_tensor(Y[:, :, :], Y[:, :, :], over_blocks(bias("L1_gnn_bias_out")), ALU.add))

        def batchnorm(name, h, gamma, beta, func, sems=None, layer=0, scratch_out=None):
            dve, act = sems or (sem(name + "_dve"), sem(name + "_act"))
            base_v, base_a = layer * 7, layer * 3
            m = small[:, 6, 0:1]
            nm = small[:, 6, 1:2]
            va = small[:, 7, 0:1]
            sd = small[:, 7, 1:2]
            sc = small[:, 4, 0:1]
            sh = small[:, 4, 1:2]
            with nc.Block() as block:
                @block.vector
                def _(v):
                    n = [0]

                    def step(ins):
                        n[0] += 1
                        ins.then_inc(dve, 1)
                        v.wait_ge(dve, base_v + n[0])

                    step(v.tensor_reduce(m, h[:, 0:NODES], AX, ALU.add))
                    step(v.tensor_scalar(nm, m, -1.0 / NODES, None, ALU.mult))
                    v.wait_ge(act, base_a + 1)
                    step(v.tensor_scalar(va, va, 1.0 / NODES, 1e-5, ALU.mult, ALU.add))
                    v.wait_ge(act, base_a + 2)
                    step(v.reciprocal(sd, sd))
                    step(v.tensor_tensor(sc, sd, gamma, ALU.mult))
                    step(v.tensor_tensor(sh, sc, nm, ALU.mult))
                    v.tensor_tensor(sh, sh, beta, ALU.add).then_inc(dve, 1)

                @block.scalar
                def _(a):
                    a.wait_ge(dve, base_v + 2)
                    a.activation(flat(TMP)[:, 0:NODES], h[:, 0:NODES], ACT.Square, bias=nm, accum_out=va).then_inc(act, 1)
                    a.wait_ge(dve, base_v + 3)
                    a.activation(sd, va, ACT.Sqrt).then_inc(act, 1)
                    a.wait_ge(dve, base_v + 7)
                    a.activation(h, h, func, bias=sh, scale=sc).then_inc(act, 1)

        gat1_sum()
        HT = ACC[:, 0:NPAD]
        transposes(flat(Y), HT)

        def gelu():
            done = sem("gelu_done")
            with nc.Block() as block:
                @block.scalar
                def _(a):
                    a.activation(HT, HT, ACT.Gelu).then_inc(done, 1)
                    a.wait_ge(done, 1)

        gelu()
        batchnorm("bn1", HT, col("bn_gamma"), col("bn_beta"), ACT.Identity)
        transposes(HT, flat(Y))

        def add_residual(v, step):
            step(v.tensor_tensor(Y[:, :, :], Y[:, :, :], X[:, :, :], ALU.add))

        layernorm(Y[:, :, :], X[:, :, :], prep=add_residual, prep_steps=1)

        transposes(flat(X), XT)
        gine_loads, gine_tab, gine_h = (sem(f"gine_{k}") for k in ("loads", "tab", "h"))
        mlp1, mlp1_done, mlp2, mlp2_done = (sem(f"gine_{k}") for k in ("mlp1", "mlp1_done", "mlp2", "mlp2_done"))
        bn_sems = (sem("gine_bn_dve"), sem("gine_bn_act"))
        back_sems = (sem("gine_turned"), sem("gine_taken"))
        Z = XR[:, :, :, :].rearrange("p b k d -> p (b k d)").bitcast(F32)[:, 0:NPAD]
        Z3 = Z.rearrange("p (b d) -> p b d", d=D)
        NCOL = 400
        NCH = NPAD // NCOL

        def gine_node_to_table(layer):
            with nc.Block() as block:
                @block.sync
                def _(sp):
                    one = bass.ds(layer, 1)
                    sp.dma_start(gine_w[:, :, :], t["gine_w"][:, one, :, :].rearrange("p a k d -> p (a k) d")).then_inc(gine_loads, 16)
                    sp.dma_start(gine_lin[:, :], t["gine_lin"][one, :, :].rearrange("a k d -> (a k) d")).then_inc(gine_loads, 16)
                    sp.dma_start(gine_blin[:, :], t["gine_blin"][one, :].broadcast_to([P, D])).then_inc(gine_loads, 16)
                    sp.dma_start(gine_cols[:, :], t["gine_cols"][:, one, :].rearrange("p a k -> p (a k)")).then_inc(gine_loads, 16)
                    sp.wait_ge(gine_tab, layer + 1)
                    sp.dma_start(table1.rearrange("(b p) d -> p b d", p=P), TMP[:, :, :]).then_inc(gine_stored, 16)

                @block.vector
                def _(v):
                    v.wait_ge(gine_loads, 64 * (layer + 1))
                    v.tensor_tensor(TMP[:, :, :], Z3, over_blocks(gine_blin[:, :]), ALU.add).then_inc(gine_tab, 1)

        def gine_mlp(layer):
            h = ACC[:, 0:NPAD]
            u = ACC[:, NPAD:2 * NPAD]
            with nc.Block() as block:
                @block.vector
                def _(v):
                    v.tensor_tensor(h, h, XT[:, :], ALU.add).then_inc(gine_h, 1)

                @block.tensor
                def _(e):
                    with e.Fori(0, NCH) as c:
                        e.wait_ge(gine_h, layer + 1)
                        e.wait_ge(mlp1_done, layer * NCH + c)
                        e.matmul(psum[:, 0, 0:NCOL], gine_w[:, 0, :], h[:, bass.ds(c * NCOL, NCOL)], start=True, stop=True).then_inc(mlp1, 1)
                        e.wait_ge(mlp2_done, layer * NCH + c)
                        e.wait_ge(mlp1_done, layer * NCH + c + 1)
                        e.matmul(psum[:, 1, 0:NCOL], gine_w[:, 1, :], u[:, bass.ds(c * NCOL, NCOL)], start=True, stop=True).then_inc(mlp2, 1)

                @block.scalar
                def _(a):
                    with a.Fori(0, NCH) as c:
                        at = bass.ds(c * NCOL, NCOL)
                        hold(a, (mlp1, layer * NCH + c + 1))
                        a.activation(u[:, at], psum[:, 0, 0:NCOL], ACT.Relu, bias=gine_cols[:, 0:1]).then_inc(mlp1_done, 1)
                        hold(a, (gine_h, layer + 1),
                             (mlp2, layer * NCH + c + 1))
                        a.activation(XT[:, at], psum[:, 1, 0:NCOL], ACT.Identity, bias=gine_cols[:, 1:2]).then_inc(mlp2_done, 1)

        def gine_first():
            done = sem("gine_first")
            with nc.Block() as block:
                @block.vector
                def _(v):
                    v.tensor_copy(Z3, X[:, :, :]).then_inc(done, 1)
                    v.memset(small[:, 7, :], 0.0).then_inc(gi["acc_done"], 1)

        gine_first()
        with nc.Fori(0, GINE_LAYERS) as layer:
            gine_node_to_table(layer)
            gine_edges(layer)
            gine_mlp(layer)
            batchnorm("gine_bn", XT[:, :], gine_cols[:, 2:3], gine_cols[:, 3:4], ACT.Relu, sems=bn_sems, layer=layer)
            transposes(XT, Z, *back_sems, base=layer * (NODE_BLOCKS // CH))

        def add_gine(v, step):
            step(v.tensor_tensor(Y[:, :, :], Z3, X[:, :, :], ALU.add))

        layernorm(Y[:, :, :], X[:, :, :], prep=add_gine, prep_steps=1)

        transposes(flat(X), XT)
        tables("tab3", HID, weight("L3_gnn_W1a"), bias("L3_gnn_b1"), weight("L3_gnn_W1b"), None, table)
        mlp_edges()

        def node_mlp():
            made, taken, diag, dsum = (sem(f"node_{k}") for k in ("made", "taken", "diag", "dsum"))
            aggr = XR[:, :, :, :].rearrange("p b k d -> p (b k d)").bitcast(F32)[:, 0:NPAD]
            hid = [XR[:, :, :, :].rearrange("p b k d -> p (b k d)").bitcast(F32)[:, NPAD * (1 + h):NPAD * (2 + h)] for h in range(2)]
            sums = [ACC[:, h * NPAD:(h + 1) * NPAD] for h in range(2)]
            b3 = bias("L3_gnn_b3")
            w3 = [weight("L3_gnn_W3a"), weight("L3_gnn_W3b")]
            with nc.Block() as block:
                @block.vector
                def _(v):
                    for b in range(NODE_BLOCKS):
                        wait(v, made, b - 1)
                        v.tensor_scalar(lk[:, b % 2, 0:P], ident, stat[:, 0, b:b + 1], None, ALU.mult).then_inc(diag, 1)

                @block.tensor
                def _(e):
                    for b in range(NODE_BLOCKS):
                        e.wait_ge(diag, b + 1)
                        wait(e, taken, b - 1)
                        o = psum[:, b % 2, 0:P]
                        for h in range(2):
                            e.matmul(o, w3[h], sums[h][:, b * P:(b + 1) * P], start=(h == 0), stop=False)
                        e.matmul(o, b3, lk[:, b % 2, 0:P], start=False, stop=True).then_inc(made, 1)

                @block.scalar
                def _(a):
                    for b in range(NODE_BLOCKS):
                        a.wait_ge(made, b + 1)
                        a.activation(aggr[:, b * P:(b + 1) * P], psum[:, b % 2, 0:P], ACT.Copy).then_inc(taken, 1)

            m1, m1_done, m2, m2_done = (sem(f"node_{k}") for k in ("m1", "m1_done", "m2", "m2_done"))
            wn1a, wn1b = weight("L3_gnn_Wn1a"), weight("L3_gnn_Wn1b")
            wn2 = [weight("L3_gnn_Wn2a"), weight("L3_gnn_Wn2b")]
            with nc.Block() as block:
                @block.tensor
                def _(e):
                    with e.Fori(0, NCH) as c:
                        at = bass.ds(c * NCOL, NCOL)
                        for h in range(2):
                            e.wait_ge(m1_done, 2 * c)
                            o = psum[:, h, 0:NCOL]
                            e.matmul(o, wn1a[:, h * D:(h + 1) * D], XT[:, at], start=True, stop=False)
                            e.matmul(o, wn1b[:, h * D:(h + 1) * D], aggr[:, at], start=False, stop=True).then_inc(m1, 1)
                        e.wait_ge(m2_done, c)
                        for h in range(2):
                            e.wait_ge(m1_done, 2 * c + h + 1)
                            last = e.matmul(psum[:, 2, 0:NCOL], wn2[h], hid[h][:, at], start=(h == 0), stop=(h == 1))
                        last.then_inc(m2, 1)

                @block.scalar
                def _(a):
                    with a.Fori(0, NCH) as c:
                        at = bass.ds(c * NCOL, NCOL)
                        for h in range(2):
                            hold(a, (m1, 2 * c + h + 1))
                            a.activation(hid[h][:, at], psum[:, h, 0:NCOL], ACT.Relu, bias=col("bn1a" if h == 0 else "bn1b")).then_inc(m1_done, 1)
                        hold(a, (m2, c + 1))
                        a.activation(HT[:, at], psum[:, 2, 0:NCOL], ACT.Identity, bias=col("bn2")).then_inc(m2_done, 1)

        node_mlp()
        transposes(HT, flat(Y))
        layernorm(Y[:, :, :], Y[:, :, :], gamma=bias("L3_gnn_gamma"), beta=bias("L3_gnn_beta"), prep=add_residual, prep_steps=1)
        layernorm(Y[:, :, :], Y[:, :, :], prep=add_residual, prep_steps=1)

        out_done = sem("out_done")
        with nc.Block() as block:
            @block.sync
            def _(sp):
                full = NODES // P
                sp.dma_start(t["out"][0:full * P, :].rearrange("(b p) d -> p b d", p=P), Y[:, 0:full, :]).then_inc(out_done, 16)
                sp.dma_start(t["out"][full * P:NODES, :], Y[0:NODES - full * P, full, :]).then_inc(out_done, 16)
                sp.wait_ge(out_done, 32)


def kernel(**inputs):
    import concourse.bacc as bacc
    from concourse.bass_utils import run_bass_kernel_spmd

    a = {k: np.asarray(v) for k, v in inputs.items()}
    pad = GROUPS * GROUP_EDGES - EDGES

    def padded(x, fill):
        return np.concatenate([x, np.full((pad,) + x.shape[1:], fill, x.dtype)])

    def spread(v):
        return np.broadcast_to(v.reshape(1, -1), (P, v.size))

    consts = np.zeros((P, C_WIDTH), np.float32)
    consts[:, C_IDENT:C_IDENT + P] = np.eye(P)
    consts[:, C_IOTA:C_IOTA + P] = np.arange(P)
    consts[:, C_ROW] = np.arange(P)
    w1, w2, w3 = a["L3_gnn_W1"], a["L3_gnn_W2"], a["L3_gnn_W3"]
    wn1, wn2 = a["L3_gnn_Wn1"], a["L3_gnn_Wn2"]
    a.update({"L3_gnn_W1a": w1[0:D], "L3_gnn_W1b": w1[D:2 * D], "L3_gnn_W2a": w2[0:D], "L3_gnn_W2b": w2[D:],
              "L3_gnn_W3a": w3[0:D], "L3_gnn_W3b": w3[D:], "L3_gnn_Wn1a": wn1[0:D], "L3_gnn_Wn1b": wn1[D:],
              "L3_gnn_Wn2a": wn2[0:D], "L3_gnn_Wn2b": wn2[D:]})
    dst = padded(a["dst"].astype(np.int32), NPAD).reshape(GROUPS, GROUP_EDGES)
    src = padded(a["src"].astype(np.int32), 0).reshape(GROUPS, GROUP_EDGES)
    bn1 = a["L3_gnn_bn1"]
    arrays = {
        "consts": consts,
        "x": np.concatenate([a["x"], np.zeros((NPAD - NODES, D), np.float32)]),
        "dst": dst,
        "dst_last": np.ascontiguousarray(dst[:, -1]).reshape(1, GROUPS),
        "src": src,
        "src_by_group": src.reshape(GROUPS, SUBS, P).transpose(0, 2, 1),
        "edge_weight": padded(a["edge_weight1"][:, 0], 0).reshape(GROUPS, GROUP_EDGES),
        "edge_attr": np.ascontiguousarray(padded(a["edge_attr_32"], 0).reshape(GROUPS, GROUP_EDGES, EDGE_D).transpose(0, 2, 1)),
        "biases": np.concatenate([spread(a[n]) for n, _ in BIASES], axis=1),
        "weights": np.concatenate([a[n] for n, _ in WEIGHTS], axis=1),
        "cols": np.stack([a["L0_gnn_att"][0], a["L0_gnn_att"][1], a["L1_gnn_att"], a["L1_gnn_bn_gamma"],
                          a["L1_gnn_bn_beta"], bn1[0:D], bn1[D:], a["L3_gnn_bn2"]], axis=1),
        "edge_w1": w1[2 * D:],
        "we": a["L1_gnn_We"],
        "gine_w": np.stack([a["L2_gnn_W1"], a["L2_gnn_W2"]]).transpose(2, 1, 0, 3),
        "gine_lin": a["L2_gnn_W_lin"],
        "gine_blin": a["L2_gnn_b_lin"],
        "gine_cols": np.stack([a["L2_gnn_b1"], a["L2_gnn_b2"], a["L2_gnn_gamma"], a["L2_gnn_beta"]]).transpose(2, 1, 0),
    }
    arrays = {k: np.ascontiguousarray(v) for k, v in arrays.items()}
    nc = bacc.Bacc("TRN2", target_bir_lowering=False, num_devices=1)
    t = {k: nc.dram_tensor(f"in_{k}", v.shape, mybir.dt.from_np(v.dtype), kind="ExternalInput").ap()
         for k, v in arrays.items()}
    t["out"] = nc.dram_tensor("out", (NODES, D), F32, kind="ExternalOutput").ap()
    build(nc, t)
    r = run_bass_kernel_spmd(nc, [{f"in_{k}": v for k, v in arrays.items()}], core_ids=[0])
    return r.results[0]["out"]
```

```python
from contextlib import ExitStack

import numpy as np
import concourse.bass as bass
from concourse import mybir

F32 = mybir.dt.float32
BF16 = mybir.dt.bfloat16
I32 = mybir.dt.int32
ALU = mybir.AluOpType
ACT = mybir.ActivationFunctionType
AX = mybir.AxisListType.X

P = 128
NODES, EDGES, D = 3125, 50000, 128
EDGE_D, HID, HEADS, GINE_LAYERS = 32, 256, 2, 3
NODE_BLOCKS = -(-NODES // P)
NPAD = NODE_BLOCKS * P
SUBS = 4
GROUP_EDGES = SUBS * P
GROUPS = -(-EDGES // GROUP_EDGES)
ITEMS = GROUPS + NODE_BLOCKS - 1
PAIRS = ITEMS // 2
assert ITEMS % 2 == 0 and ITEMS <= P
MASK = 2.0 ** 100
FLOOR = -1e20

SPLIT = 3

C_IDENT, C_IOTA, C_ROW = 0, P, 2 * P
C_PICK = 2 * P + 1
C_WIDTH = C_PICK + SPLIT
BIASES = [("L0_gnn_gamma", D), ("L0_gnn_beta", D), ("L0_gnn_bl", 2 * D), ("L0_gnn_br", 2 * D),
          ("L0_gnn_bias", D), ("L1_gnn_bl", D), ("L1_gnn_br", D), ("L1_gnn_bias_out", D),
          ("L3_gnn_b1", HID), ("L3_gnn_b2", HID), ("L3_gnn_b3", D), ("L3_gnn_gamma", D),
          ("L3_gnn_beta", D)]
BIAS_AT, at = {}, 0
for _name, _n in BIASES:
    BIAS_AT[_name] = (at, _n)
    at += _n
BIAS_WIDTH = at
COLS = ["att0", "att1", "att2", "bn_gamma", "bn_beta", "bn1a", "bn1b", "bn2"]
GINE_COLS = 4
WEIGHTS = [("L0_gnn_Wl", 2 * D), ("L0_gnn_Wr", 2 * D), ("L0_gnn_res_W", D), ("L1_gnn_Wl", D),
           ("L1_gnn_Wr", D), ("L3_gnn_W1a", HID), ("L3_gnn_W1b", HID), ("L3_gnn_W2a", HID),
           ("L3_gnn_W2b", HID), ("L3_gnn_W3a", D), ("L3_gnn_W3b", D), ("L3_gnn_Wn1a", HID),
           ("L3_gnn_Wn1b", HID), ("L3_gnn_Wn2a", D), ("L3_gnn_Wn2b", D)]
WEIGHT_AT, at = {}, 0
for _name, _n in WEIGHTS:
    WEIGHT_AT[_name] = (at, _n)
    at += _n
WEIGHT_WIDTH = at


def build(nc, t):
    with ExitStack() as ctx:
        def sb(name, shape, dt=F32):
            return ctx.enter_context(nc.sbuf_tensor(name, shape, dt))

        def sem(name):
            return ctx.enter_context(nc.semaphore(name))

        def scratch(name, shape, dt=F32):
            return nc.dram_tensor(name, shape, dt, kind="Internal").ap()

        table = scratch("source_rows", (NPAD, 2 * D))
        table1 = scratch("source_rows_narrow", (NPAD, D))
        rel_rows = scratch("rel_rows", (ITEMS, GROUP_EDGES), BF16)
        weight_rows = scratch("weight_rows", (ITEMS, SPLIT * SPLIT, GROUP_EDGES), BF16)
        group_block = scratch("group_block", (ITEMS, 4), I32)

        consts = sb("consts", [P, C_WIDTH])
        ident = consts[:, C_IDENT:C_IDENT + P]
        iota = consts[:, C_IOTA:C_IOTA + P]
        row = consts[:, C_ROW:C_ROW + 1]
        bias_all = sb("bias_all", [P, BIAS_WIDTH])
        weight_all = sb("weight_all", [P, WEIGHT_WIDTH])
        cols = sb("cols", [P, len(COLS)])
        gine_cols = sb("gine_cols", [P, GINE_COLS])
        gine_w = sb("gine_w", [P, 2, D])
        gine_lin = sb("gine_lin", [EDGE_D, D])
        gine_blin = sb("gine_blin", [P, D])
        edge_w1 = sb("edge_w1", [EDGE_D, HID])
        we_parts = sb("we_parts", [SPLIT * SPLIT, D], BF16)
        att_b = sb("att_b", [P, 3, P])
        X = sb("X", [P, NODE_BLOCKS, D])
        Y = sb("Y", [P, NODE_BLOCKS, D])
        XT = sb("XT", [P, NPAD])
        TMP = sb("TMP", [P, NODE_BLOCKS, D])
        ACC = sb("ACC", [P, NODE_BLOCKS * 2 * D])
        XR = sb("XR", [P, NODE_BLOCKS, SPLIT, 2 * D], BF16)
        stage = sb("stage", [P, 4, 2 * D])
        stage_r = sb("stage_r", [P, 4, 2 * D])
        zsum = sb("zsum", [P, NODE_BLOCKS, 2])
        neg_max = sb("neg_max", [P, NODE_BLOCKS, 2])
        stat = sb("stat", [P, 4, NODE_BLOCKS])
        groups_blocks = sb("groups_blocks", [1, ITEMS, 4], I32)
        group_end = sb("group_end", [1, GROUPS], I32)
        idx_all = sb("idx_all", [P, ITEMS, SUBS], I32)
        rel_all = sb("rel_all", [P, ITEMS, SUBS])
        idx = sb("idx", [P, 4, SUBS], I32)
        rel = sb("rel", [P, 2, GROUP_EDGES], BF16)
        wrow = sb("wrow", [SPLIT * SPLIT, 2, GROUP_EDGES], BF16)
        gath = sb("gath", [P, 4, SUBS, 2 * D])
        hot_t = sb("hot_t", [P, 2, GROUP_EDGES], BF16)
        hot = sb("hot", [P, 2, SUBS, P])
        neg = sb("neg", [P, 2, GROUP_EDGES], BF16)
        ea = sb("ea", [EDGE_D, 2, GROUP_EDGES])
        vs = sb("vs", [P, 2, GROUP_EDGES])
        lk = sb("lk", [P, 2, GROUP_EDGES])
        sm = sb("sm", [P, 2, GROUP_EDGES])
        pm = sb("pm", [P, 2, GROUP_EDGES])
        pt = sb("pt", [P, 2, SUBS, P])
        small = sb("small", [P, 8, 2])
        MI, NEGM, DM = (small[:, k, :] for k in range(3))
        row_mask = sb("row_mask", [P, 1])
        factors = sb("factors", [P, 2, 2, 2])
        SCL = [factors[:, s, 0, :] for s in range(2)]
        ZI = [factors[:, s, 1, :] for s in range(2)]

        psum = ctx.enter_context(nc.psum_tensor("psum", [P, 8, 512], F32))

        consts_in = sem("consts_in")

        def wait(e, s, value):
            if not (isinstance(value, int) and value <= 0):
                e.wait_ge(s, value)

        def hold(e, *waits):
            waits = [(s, v if isinstance(v, int) else e.snap(e.to_reg(v))) for s, v in waits]
            e.wait_ge(consts_in, 16)
            for s, v in waits:
                wait(e, s, v)

        def place(quad, m, layer):
            return m % 2, layer * PAIRS + 2 * quad + m // 2, m, layer * -(-(ITEMS - m) // 4) + quad

        def in_order(e, body, layer=0):
            for i in range(5):
                body(i, *place(i // 4, i % 4, layer))
            with e.Fori(0, (ITEMS - 6) // 4) as k:
                for q in range(4):
                    body(4 * k + 5 + q, *place(k + (5 + q) // 4, (5 + q) % 4, layer))
            body(ITEMS - 1, *place((ITEMS - 1) // 4, (ITEMS - 1) % 4, layer))

        def nothing(*_):
            pass

        def walk(e, front, back=nothing, mid=nothing, tail=nothing, layer=0):
            def step(i, *places):
                front(i, *places[0])
                if len(places) > 2:
                    tail(i - 2, *places[2])
                if len(places) > 1:
                    back(i - 1, *places[1])
                mid(i, *places[0])

            def place_of(i):
                return place(i // 4, i % 4, layer)

            for i in range(5):
                step(i, *(place_of(i - lag) for lag in range(min(i, 2) + 1)))
            with e.Fori(0, (ITEMS - 6) // 4) as k:
                for q in range(5, 9):
                    step(4 * k + q, *(place(k + (q - lag) // 4, (q - lag) % 4, layer) for lag in range(3)))
            last = ITEMS - 1
            step(last, *(place_of(last - lag) for lag in range(3)))
            tail(last - 1, *place_of(last - 1))
            back(last, *place_of(last))
            tail(last, *place_of(last))

        def bias(name):
            a, n = BIAS_AT[name]
            return bias_all[:, a:a + n]

        def weight(name):
            a, n = WEIGHT_AT[name]
            return weight_all[:, a:a + n]

        def col(name):
            k = COLS.index(name)
            return cols[:, k:k + 1]

        def over_blocks(v):
            return v.unsqueeze(1).broadcast_to([P, NODE_BLOCKS, v.shape[1]])

        def over_features(v):
            return v.unsqueeze(2).broadcast_to([P, NODE_BLOCKS, D])

        def setup():
            loads = sem("setup_loads")
            last_in = sem("last_in")
            dve = sem("setup_dve")
            tables_out = sem("tables_out")
            rows_in = sem("rows_in")
            pe = sem("setup_pe")
            copied = sem("setup_copied")
            with ExitStack() as mine:
                last_i = mine.enter_context(nc.sbuf_tensor("last_i", [ITEMS, GROUPS], I32))
                gb_f = mine.enter_context(nc.sbuf_tensor("gb_f", [ITEMS, 4], F32))
                gb_i = mine.enter_context(nc.sbuf_tensor("gb_i", [ITEMS, 4], I32))
                last_f = vs[0:ITEMS, 0, 0:GROUPS]
                ew_i = vs[0:ITEMS, 1, :]
                dst_i = lk[0:ITEMS, 0, :].bitcast(I32)
                src_i = lk[0:ITEMS, 1, :].bitcast(I32)
                dst_f = sm[0:ITEMS, 0, :]
                src_f = sm[0:ITEMS, 1, :]
                rel_b = rel[0:ITEMS, 0, :]
                ew_parts = [hot_t[0:ITEMS, 0, :], hot_t[0:ITEMS, 1, :], neg[0:ITEMS, 0, :]]
                we_f = pm[0:SPLIT * SPLIT, 0, 0:D]
                we_p = [neg[0:SPLIT * SPLIT, 1, k * D:(k + 1) * D] for k in range(SPLIT)]
                ew_split = sem("weight_split")
                with nc.Block() as block:
                    @block.sync
                    def _(sp):
                        sp.dma_start(consts[:, :], t["consts"]).then_inc(consts_in, 16)
                        sp.dma_start(last_i[:, :], t["dst_last"].broadcast_to([ITEMS, GROUPS])).then_inc(last_in, 16)
                        sp.dma_start(X[:, :, :], t["x"].rearrange("(b p) d -> p b d", p=P)).then_inc(loads, 16)
                        sp.dma_start(bias_all[:, :], t["biases"]).then_inc(loads, 16)
                        sp.dma_start(weight_all[:, :], t["weights"]).then_inc(loads, 16)
                        sp.dma_start(cols[:, :], t["cols"]).then_inc(loads, 16)
                        sp.dma_start(edge_w1[:, :], t["edge_w1"]).then_inc(loads, 16)
                        sp.dma_start(we_f, t["we"].broadcast_to([SPLIT * SPLIT, D])).then_inc(loads, 16)
                        sp.wait_ge(dve, 10)
                        sp.dma_start(group_block, gb_i[:, :]).then_inc(tables_out, 16)
                        sp.wait_ge(tables_out, 16)
                        sp.dma_start(groups_blocks[:, :, :], group_block.unsqueeze(0)).then_inc(loads, 16)
                        sp.wait_ge(dve, 14)
                        sp.dma_start(rel_rows, rel_b).then_inc(tables_out, 16)
                        sp.wait_ge(ew_split, 5)
                        for a in range(SPLIT):
                            for b in range(SPLIT):
                                sp.dma_start(weight_rows[:, SPLIT * a + b, :], ew_parts[a]).then_inc(tables_out, 16)
                        sp.wait_ge(tables_out, 16 * (2 + SPLIT * SPLIT))
                        sp.wait_ge(loads, 7 * 16)

                    @block.gpsimd
                    def _(pool):
                        pool.wait_ge(dve, 10)
                        for rows, out in ((t["dst"], dst_i), (t["src"], src_i), (t["edge_weight"], ew_i)):
                            pool.indirect_dma_start(
                                out=out, out_offset=None, in_=rows,
                                in_offset=bass.IndirectOffsetOnAxis(ap=gb_i[:, 0:1], axis=0)).then_inc(rows_in, 16)
                        pool.wait_ge(rows_in, 48)

                    @block.vector
                    def _(v):
                        n = [0]

                        def step(ins):
                            n[0] += 1
                            ins.then_inc(dve, 1)
                            v.wait_ge(dve, n[0])

                        v.wait_ge(last_in, 16)
                        v.wait_ge(consts_in, 16)
                        v.tensor_scalar(row_mask[:, :], row, -MASK, None, ALU.mult)
                        step(v.tensor_scalar(last_i[:, :], last_i[:, :], 7, None, ALU.arith_shift_right))
                        step(v.tensor_copy(last_f, last_i[:, :]))
                        step(v.scalar_tensor_tensor(last_f, last_f, float(NODE_BLOCKS - 1),
                                                    iota[0:ITEMS, 0:GROUPS], ALU.min, ALU.add))
                        step(v.tensor_scalar(group_end[:, :], last_f[0:1, :], 1.0, None, ALU.add))
                        step(v.tensor_scalar(last_f, last_f, row[0:ITEMS, :], None, ALU.is_lt))
                        step(v.tensor_reduce(gb_f[:, 0:1], last_f, AX, ALU.add))
                        step(v.tensor_tensor(gb_f[:, 1:2], row[0:ITEMS, :], gb_f[:, 0:1], ALU.subtract))
                        v.memset(gb_i[:, 3:4], 0)
                        v.tensor_copy(gb_i[:, 2:3], gb_f[:, 1:2])
                        step(v.tensor_copy(gb_i[:, 0:1], gb_f[:, 0:1]))
                        step(v.tensor_scalar(gb_i[:, 1:2], gb_i[:, 0:1], 3, None, ALU.bitwise_and))
                        step(v.tensor_scalar(gb_f[:, 2:3], gb_f[:, 1:2], float(P), None, ALU.mult))
                        v.wait_ge(rows_in, 48)
                        step(v.tensor_copy(dst_f, dst_i))
                        step(v.tensor_scalar(dst_f, dst_f, gb_f[:, 2:3], -1.0, ALU.subtract, ALU.max))
                        step(v.tensor_scalar(dst_f, dst_f, float(P), None, ALU.min))
                        step(v.tensor_copy(rel_b, dst_f))
                        step(v.tensor_copy(src_f, src_i))
                        v.wait_ge(pe, 1)
                        v.tensor_copy(rel_all[:, :, :].rearrange("p i j -> p j i"), psum[:, 0, :].rearrange("p (j i) -> p j i", j=SUBS)[:, :, 0:ITEMS])
                        v.tensor_copy(idx_all[:, :, :].rearrange("p i j -> p j i"), psum[:, 1, :].rearrange("p (j i) -> p j i", j=SUBS)[:, :, 0:ITEMS])
                        v.wait_ge(loads, 7 * 16)
                        for k in range(3):
                            v.tensor_copy(att_b[:, k, :], cols[:, k:k + 1].broadcast_to([P, P]))
                        v.tensor_copy(groups_blocks[:, 2:ITEMS, 3], groups_blocks[:, 0:ITEMS - 2, 2])
                        m = 0
                        for x, parts in ((ew_i, ew_parts), (we_f, we_p)):
                            for k, part in enumerate(parts):
                                v.tensor_copy(part, x).then_inc(ew_split, 1)
                                m += 1
                                v.wait_ge(ew_split, m)
                                if k < SPLIT - 1:
                                    v.tensor_tensor(x, x, part, ALU.subtract).then_inc(ew_split, 1)
                                    m += 1
                                    v.wait_ge(ew_split, m)
                        pick = consts[0:SPLIT * SPLIT, C_PICK:C_PICK + SPLIT]
                        v.tensor_scalar(we_parts[:, :], we_p[0], pick[:, 0:1], None, ALU.mult).then_inc(ew_split, 1)
                        for k in range(1, SPLIT):
                            m += 1
                            v.wait_ge(ew_split, m)
                            v.scalar_tensor_tensor(we_parts[:, :], we_p[k], pick[:, k:k + 1], we_parts[:, :], ALU.mult, ALU.add).then_inc(ew_split, 1)

                    @block.tensor
                    def _(e):
                        e.wait_ge(consts_in, 16)
                        e.wait_ge(dve, 15)
                        for k, rows in enumerate((dst_f, src_f)):
                            for j in range(SUBS):
                                last = e.transpose(psum[:, k, j * P:j * P + ITEMS], rows[:, j * P:(j + 1) * P],
                                                   ident[0:ITEMS, 0:ITEMS])
                        last.then_inc(pe, 1)

        setup()

        ln_dve, ln_act, ln_steps, ln_calls = sem("layernorm_dve"), sem("layernorm_act"), [0], [0]

        def layernorm(src, dst, gamma=None, beta=None, relu=False, prep=None, prep_steps=0):
            base_v, base_a = ln_steps[0], 2 * ln_calls[0]
            ln_calls[0] += 1
            with nc.Block() as block:
                @block.vector
                def _(v):
                    def step(ins):
                        ln_steps[0] += 1
                        ins.then_inc(ln_dve, 1)
                        v.wait_ge(ln_dve, ln_steps[0])

                    if prep is not None:
                        prep(v, step)
                    assert ln_steps[0] == base_v + prep_steps
                    step(v.tensor_reduce(stat[:, 0, :], src, AX, ALU.add))
                    step(v.tensor_scalar(stat[:, 0, :], stat[:, 0, :], 1.0 / D, None, ALU.mult))
                    step(v.tensor_tensor(dst, src, over_features(stat[:, 0, :]), ALU.subtract))
                    v.wait_ge(ln_act, base_a + 1)
                    step(v.tensor_reduce(stat[:, 1, :], TMP[:, :, :], AX, ALU.add))
                    step(v.tensor_scalar(stat[:, 1, :], stat[:, 1, :], 1.0 / D, 1e-5, ALU.mult, ALU.add))
                    v.wait_ge(ln_act, base_a + 2)
                    step(v.reciprocal(stat[:, 3, :], stat[:, 2, :]))
                    step(v.tensor_tensor(dst, dst, over_features(stat[:, 3, :]), ALU.mult))
                    if gamma is not None:
                        step(v.tensor_tensor(dst, dst, over_blocks(gamma), ALU.mult))
                        step(v.tensor_tensor(dst, dst, over_blocks(beta), ALU.add))
                    if relu:
                        step(v.tensor_scalar(dst, dst, 0.0, None, ALU.max))

                @block.scalar
                def _(a):
                    a.wait_ge(ln_dve, base_v + prep_steps + 3)
                    a.activation(TMP[:, :, :], dst, ACT.Square).then_inc(ln_act, 1)
                    a.wait_ge(ln_dve, base_v + prep_steps + 5)
                    a.activation(stat[:, 2, :], stat[:, 1, :], ACT.Sqrt).then_inc(ln_act, 1)

        CH = 5
        turned_, taken_, moves = sem("turned"), sem("taken"), [0]

        def transposes(src, dst, turned=turned_, taken=taken_, base=None):
            if base is None:
                base = moves[0]
                moves[0] += NODE_BLOCKS // CH
            with nc.Block() as block:
                @block.tensor
                def _(e):
                    for c in range(NODE_BLOCKS // CH):
                        if c >= 2:
                            hold(e, (taken, base + c - 1))
                        for k in range(CH):
                            b = c * CH + k
                            o = psum[:, 2 * (c % 2) + k // 4, (k % 4) * P:(k % 4 + 1) * P]
                            last = e.transpose(o, src[:, b * P:(b + 1) * P], ident)
                        last.then_inc(turned, 1)

                @block.scalar
                def _(a):
                    for c in range(NODE_BLOCKS // CH):
                        wait(a, turned, base + c + 1)
                        half = psum[:, 2 * (c % 2):2 * (c % 2) + 2, :].rearrange("p a n -> p (a n)")
                        a.activation(dst[:, c * CH * P:(c + 1) * CH * P], half[:, 0:CH * P], ACT.Copy).then_inc(taken, 1)

        def flat(buf):
            return buf[:, :, :].rearrange("p b d -> p (b d)")

        CB = 4
        CHUNKS = -(-NODE_BLOCKS // CB)

        def tables(name, width, w_src, b_src, w_dst, b_dst, dram, extra=None):
            made, staged, split_a, split_v, stored, eb = (sem(f"{name}_{k}") for k in (
                "made", "staged", "split_a", "split_v", "stored", "extra"))
            rows = dram.rearrange("(b p) d -> p b d", p=P)
            per = 512 // width
            STG = 2 if extra is None else 3

            def place(bank0, k):
                return psum[:, bank0 + k // per, (k % per) * width:(k % per + 1) * width]

            def banks(bank0, n):
                v = psum[:, bank0:bank0 + CB // per, :].rearrange("p a (k w) -> p (a k) w", w=width)
                return v[:, 0:n, :]

            def bias_of(b, n):
                return b.unsqueeze(1).broadcast_to([P, n, b.shape[1]])

            with nc.Block() as block:
                @block.tensor
                def _(e):
                    for c in range(CHUNKS):
                        wait(e, staged, STG * c)
                        for k in range(min(CB, NODE_BLOCKS - c * CB)):
                            b = c * CB + k
                            xt = XT[:, b * P:(b + 1) * P]
                            e.matmul(place(0, k), xt, w_src, start=True, stop=True)
                            last = e.matmul(place(2, k), xt, w_dst, start=True, stop=True)
                            if extra is not None:
                                last = e.matmul(psum[:, 4, k * D:(k + 1) * D], xt, extra[0], start=True, stop=True)
                        last.then_inc(made, 1)

                @block.vector
                def _(v):
                    for c in range(CHUNKS):
                        n = min(CB, NODE_BLOCKS - c * CB)
                        v.wait_ge(made, c + 1)
                        wait(v, stored, 16 * c)
                        v.tensor_tensor(stage[:, 0:n, 0:width], banks(0, n), bias_of(b_src, n), ALU.add).then_inc(staged, 1)
                        wait(v, split_v, 2 * c)
                        if b_dst is None:
                            v.tensor_copy(stage_r[:, 0:n, 0:width], banks(2, n)).then_inc(staged, 1)
                        else:
                            v.tensor_tensor(stage_r[:, 0:n, 0:width], banks(2, n), bias_of(b_dst, n), ALU.add).then_inc(staged, 1)
                        if extra is not None:
                            y = Y[:, c * CB:c * CB + n, :]
                            v.tensor_tensor(y, psum[:, 4, 0:n * D].rearrange("p (k d) -> p k d", d=D), bias_of(extra[1], n), ALU.add).then_inc(eb, 1)
                            v.wait_ge(eb, c + 1)
                            v.scalar_tensor_tensor(y, X[:, c * CB:c * CB + n, :], 2.0, y, ALU.mult, ALU.add).then_inc(staged, 1)
                        r = stage_r[:, 0:n, 0:width]
                        x = XR[:, c * CB:c * CB + n, :, 0:width]
                        v.wait_ge(split_a, 2 * c + 1)
                        v.tensor_tensor(r, r, x[:, :, 0, :], ALU.subtract).then_inc(split_v, 1)
                        v.wait_ge(split_a, 2 * c + 2)
                        v.wait_ge(split_v, 2 * c + 1)
                        v.tensor_tensor(x[:, :, 2, :], r, x[:, :, 1, :], ALU.subtract).then_inc(split_v, 1)

                @block.scalar
                def _(a):
                    for c in range(CHUNKS):
                        n = min(CB, NODE_BLOCKS - c * CB)
                        r = stage_r[:, 0:n, 0:width]
                        x = XR[:, c * CB:c * CB + n, :, 0:width]
                        a.wait_ge(staged, STG * c + 2)
                        a.activation(x[:, :, 0, :], r, ACT.Copy).then_inc(split_a, 1)
                        a.wait_ge(split_v, 2 * c + 1)
                        a.activation(x[:, :, 1, :], r, ACT.Copy).then_inc(split_a, 1)

                @block.sync
                def _(sp):
                    for c in range(CHUNKS):
                        n = min(CB, NODE_BLOCKS - c * CB)
                        sp.wait_ge(staged, STG * c + 1)
                        sp.dma_start(rows[:, c * CB:c * CB + n, :], stage[:, 0:n, 0:width]).then_inc(stored, 16)
                    sp.wait_ge(stored, 16 * CHUNKS)

        idx_in = [sem(f"idx_in{s}") for s in range(4)]
        rel_in = [sem(f"rel_in{s}") for s in range(2)]
        gathered = [sem(f"gathered{s}") for s in range(4)]

        def gat_edges(number, heads, dram, att, with_weight):
            width = heads * D
            acc = ACC[:, 0:NODE_BLOCKS * width].rearrange("p (b h d) -> p b h d", h=heads, d=D)
            name = f"gat{number}"
            w_in = [sem(f"{name}_w_in{s}") for s in range(2)] if with_weight else []
            cleared, hot_t_done, negs, g_ready, g_copied, v_ready, v_added, leaked, s_ready, s_masked, neg_max_new, max_step, max_done, p_ready, scl_ready, \
                pt_ready, pt_copied, o_ready, acc_done = (sem(f"{name}_{k}") for k in (
                    "cleared", "hot_t_done", "negs", "g_ready", "g_copied", "v_ready", "v_added", "leaked", "s_ready", "s_masked", "neg_max_new", "max_step",
                    "max_done", "p_ready", "scl_ready", "pt_ready", "pt_copied", "o_ready", "acc_done"))
            V = [psum[:, h, :] for h in range(heads)]
            S = [psum[:, 2 + h, :] for h in range(heads)]
            T = [psum[:, 4 + h, :] for h in range(heads)]
            O = [psum[:, 6 + h, 0:D] for h in range(heads)]

            def block_of(e, i):
                return e.value_load(groups_blocks[0:1, bass.ds(i, 1), 2], min_val=0, max_val=NODE_BLOCKS - 1)

            with nc.Block() as block:
                @block.sync
                def _(sp):
                    def item(i, s, turn, s4, turn4):
                        hold(sp, (gathered[s4], 16 * SUBS * turn4))
                        sp.dma_start(idx[:, s4, :], idx_all[:, bass.ds(i, 1), :].rearrange("p a j -> p (a j)")).then_inc(idx_in[s4], 16)
                        hold(sp, (hot_t_done, i - 1), (negs, i - 1))
                        sp.dma_start(rel[:, s, :], rel_rows[bass.ds(i, 1), :].broadcast_to([P, GROUP_EDGES])).then_inc(rel_in[s], 16)
                        if with_weight:
                            hold(sp, (v_ready, heads * (i - 1)))
                            sp.dma_start(wrow[:, s, :], weight_rows[bass.ds(i, 1), :]).then_inc(w_in[s], 16)

                    in_order(sp, item, number)

                @block.gpsimd
                def _(pool):
                    def item(i, s, turn, s4, turn4):
                        hold(pool, (idx_in[s4], 16 * (turn4 + 1)),
                             (o_ready, heads * (i - 3)))
                        for j in range(SUBS):
                            pool.indirect_dma_start(
                                out=gath[:, s4, j, 0:width], out_offset=None, in_=dram,
                                in_offset=bass.IndirectOffsetOnAxis(ap=idx[:, s4, j:j + 1], axis=0)).then_inc(gathered[s4], 16)

                    in_order(pool, item, number)

                @block.tensor
                def _(e):
                    def front(i, s, turn, s4, turn4):
                        e.wait_ge(gathered[s4], 16 * SUBS * (turn4 + 1))
                        for h in range(heads):
                            wait(e, pt_copied, heads * (i - 2) + h + 1)
                            for j in range(SUBS):
                                last = e.transpose(T[h][:, j * P:(j + 1) * P], gath[:, s4, j, h * D:(h + 1) * D], ident)
                            last.then_inc(g_ready, 1)
                        b = block_of(e, i)
                        late = [(w_in[s], 16 * (turn + 1 - number * PAIRS))] if with_weight else []
                        hold(e, (hot_t_done, i + 1), *late)
                        for h in range(heads):
                            if with_weight:
                                e.matmul(V[h], we_parts[:, :], wrow[:, s, :], start=True, stop=False)
                            for k in range(SPLIT):
                                last = e.matmul(V[h], XR[:, bass.ds(b, 1), k, h * D:(h + 1) * D].rearrange("p a d -> p (a d)"), hot_t[:, s, :],
                                                start=(k == 0 and not with_weight), stop=(k == SPLIT - 1))
                            last.then_inc(v_ready, 1)

                    def mid(i, s, turn, s4, turn4):
                        for h in range(heads):
                            e.wait_ge(leaked, heads * i + h + 1)
                            e.matmul(S[h], att_b[:, att[h], :], lk[:, h, :], start=True, stop=True).then_inc(s_ready, 1)

                    def back(i, s, turn, s4, turn4):
                        for h in range(heads):
                            e.wait_ge(p_ready, heads * i + h + 1)
                            g_out = heads * (i + 2) if not (isinstance(i, int) and i == ITEMS - 1) else heads * ITEMS
                            e.wait_ge(g_copied, g_out)
                            for j in range(SUBS):
                                last = e.transpose(T[h][:, j * P:(j + 1) * P], pm[:, h, j * P:(j + 1) * P], ident)
                            last.then_inc(pt_ready, 1)

                    def tail(i, s, turn, s4, turn4):
                        wait(e, acc_done, i)
                        for h in range(heads):
                            e.wait_ge(pt_copied, heads * i + h + 1)
                            for j in range(SUBS):
                                last = e.matmul(O[h], pt[:, h, j, :], gath[:, s4, j, h * D:(h + 1) * D],
                                                start=(j == 0), stop=(j == SUBS - 1))
                            last.then_inc(o_ready, 1)

                    walk(e, front, back, mid, tail, number)

                @block.scalar
                def _(a):
                    def front(i, s, turn, s4, turn4):
                        for h in range(heads):
                            wait(a, leaked, heads * (i - 1) + h + 1)
                            a.wait_ge(g_ready, heads * i + h + 1)
                            a.activation(vs[:, h, :], T[h], ACT.Copy).then_inc(g_copied, 1)

                    def mask(i, s, turn):
                        a.wait_ge(rel_in[s], 16 * (turn + 1))
                        wait(a, s_masked, heads * (i - 1))
                        a.activation(neg[:, s, :], rel[:, s, :], ACT.Abs, bias=row_mask[:, :], scale=MASK).then_inc(negs, 1)

                    def mid(i, s, turn, s4, turn4):
                        if not (isinstance(i, int) and i == ITEMS - 1):
                            mask(i + 1, 1 - s, turn + s)

                    def back(i, s, turn, s4, turn4):
                        a.wait_ge(neg_max_new, i + 1)
                        wait(a, acc_done, i - 1)
                        for h in range(heads):
                            a.activation(pm[:, h, :], sm[:, h, :], ACT.Exp, bias=NEGM[:, h:h + 1],
                                         accum_out=ZI[s][:, h:h + 1]).then_inc(p_ready, 1)
                        a.wait_ge(max_step, i + 1)
                        a.activation(SCL[s][:, 0:heads], DM[:, 0:heads], ACT.Exp).then_inc(scl_ready, 1)
                        for h in range(heads):
                            a.wait_ge(pt_ready, heads * i + h + 1)
                            wait(a, o_ready, heads * i)
                            a.activation(pt[:, h, :, :].rearrange("p j n -> p (j n)"), T[h], ACT.Copy).then_inc(pt_copied, 1)

                    mask(0, 0, number * PAIRS)
                    walk(a, front, back, mid, layer=number)

                @block.vector
                def _(v):
                    v.memset(ACC[:, 0:NODE_BLOCKS * width], 0.0)
                    v.memset(zsum[:, :, :], 0.0)
                    v.memset(neg_max[:, :, :], -FLOOR).then_inc(cleared, 1)
                    v.wait_ge(cleared, 1)

                    def make_hot_t(i, s, turn):
                        v.wait_ge(rel_in[s], 16 * (turn + 1))
                        wait(v, v_ready, heads * (i - 1))
                        v.tensor_scalar(hot_t[:, s, :], rel[:, s, :], row, None, ALU.is_equal).then_inc(hot_t_done, 1)

                    def read_blocks(i):
                        if isinstance(i, int) and i < 2:
                            blocks["item"] = block_of(v, i)
                        else:
                            _, (blocks["item"], blocks["tail"]) = nc.values_load_multi_w_load_instructions(
                                groups_blocks[0:1, bass.ds(i, 1), 2:4], engines=(mybir.EngineType.DVE,),
                                min_val=0, max_val=NODE_BLOCKS - 1)

                    def front(i, s, turn, s4, turn4):
                        for h in range(heads):
                            wait(v, s_ready, heads * (i - 1) + h + 1)
                            v.wait_ge(v_ready, heads * i + h + 1)
                            v.wait_ge(g_copied, heads * i + h + 1)
                            v.tensor_tensor(vs[:, h, :], V[h], vs[:, h, :], ALU.add).then_inc(v_added, 1)
                            if h == 0:
                                read_blocks(i)
                            v.wait_ge(v_added, heads * i + h + 1)
                            v.scalar_tensor_tensor(lk[:, h, :], vs[:, h, :], 0.2, vs[:, h, :], ALU.mult, ALU.max).then_inc(leaked, 1)
                        if not (isinstance(i, int) and i == ITEMS - 1):
                            make_hot_t(i + 1, 1 - s, turn + s)

                    def mid(i, s, turn, s4, turn4):
                        b = blocks["item"]
                        for h in range(heads):
                            hold(v, (negs, i + 1), (p_ready, heads * i),
                                 (s_ready, heads * i + h + 1))
                            v.tensor_tensor_reduce(out=sm[:, h, :], in0=S[h], in1=neg[:, s, :], scale=1.0, scalar=-4 * MASK,
                                                   op0=ALU.subtract, op1=ALU.max, accum_out=MI[:, h:h + 1]).then_inc(s_masked, 1)
                        old = neg_max[:, bass.ds(b, 1), 0:heads].rearrange("p a h -> p (a h)")
                        new = NEGM[:, 0:heads]
                        v.wait_ge(s_masked, heads * (i + 1))
                        wait(v, max_done, i)
                        v.scalar_tensor_tensor(new, MI[:, 0:heads], -1.0, old, ALU.mult, ALU.min).then_inc(neg_max_new, 1)
                        v.wait_ge(neg_max_new, i + 1)
                        wait(v, scl_ready, i)
                        v.tensor_tensor(DM[:, 0:heads], new, old, ALU.subtract).then_inc(max_step, 1)
                        hold(v, (max_step, i + 1))
                        v.tensor_copy(old, new).then_inc(max_done, 1)

                    def tail(i, s, turn, s4, turn4):
                        b = blocks.pop("tail") if "tail" in blocks else block_of(v, i)
                        v.wait_ge(scl_ready, i + 1)
                        v.wait_ge(p_ready, heads * (i + 1))
                        wait(v, acc_done, i)
                        for h in range(heads):
                            v.wait_ge(o_ready, heads * i + h + 1)
                            a_h = acc[:, bass.ds(b, 1), h, :].rearrange("p a d -> p (a d)")
                            z_h = zsum[:, bass.ds(b, 1), h:h + 1].rearrange("p a h -> p (a h)")
                            v.scalar_tensor_tensor(a_h, a_h, SCL[s][:, h:h + 1], O[h], ALU.mult, ALU.add)
                            last = v.scalar_tensor_tensor(z_h, z_h, SCL[s][:, h:h + 1], ZI[s][:, h:h + 1], ALU.mult, ALU.add)
                        last.then_inc(acc_done, 1)

                    blocks = {}
                    make_hot_t(0, 0, number * PAIRS)
                    walk(v, front, mid=mid, tail=tail, layer=number)

        gi = {k: sem(f"gine_{k}") for k in (
            "hot_done", "e_ready", "added", "msg", "o_ready", "acc_done", "cleared")}
        gi_idx = [sem(f"gine_idx_in{s}") for s in range(4)]
        gi_ea = [sem(f"gine_ea_in{s}") for s in range(2)]
        gi_gath = [sem(f"gine_gathered{s}") for s in range(4)]
        gi_landed = sem("gine_landed")
        gine_stored = sem("gine_stored")

        def group_of(e, i):
            return e.value_load(groups_blocks[0:1, bass.ds(i, 1), 0], min_val=0, max_val=GROUPS - 1)

        def block_of(e, i):
            return e.value_load(groups_blocks[0:1, bass.ds(i, 1), 2], min_val=0, max_val=NODE_BLOCKS - 1)

        def gine_edges(layer):
            acc = ACC[:, 0:NPAD]
            done = layer * ITEMS
            turns = layer * PAIRS
            E = [psum[:, s, :] for s in range(2)]
            O = [psum[:, 2 + s, 0:P] for s in range(2)]
            with nc.Block() as block:
                def turn_of(slot, round):
                    return layer * -(-(GROUPS - slot) // 4) + round

                def by_group(e, body):
                    for g in range(4):
                        body(g, g, 0)
                    with e.Fori(0, (GROUPS - 4) // 4) as k:
                        for q in range(4):
                            body(4 * k + 4 + q, q, k + 1)
                    for g in range(GROUPS - GROUPS % 4, GROUPS):
                        body(g, g % 4, g // 4)

                @block.sync
                def _(sp):
                    def group(g, slot, round):
                        if not isinstance(g, int) or g >= 4:
                            end = sp.value_load(group_end[0:1, bass.ds(g - 4, 1)], min_val=1, max_val=ITEMS)
                            sp.wait_ge(gi["added"], done + end)
                        sp.wait_ge(gi_gath[slot], 16 * SUBS * turn_of(slot, round))
                        sp.dma_start(idx[:, slot, :], t["src_by_group"][bass.ds(g, 1), :, :].rearrange("a p j -> (a p) j")).then_inc(gi_idx[slot], 16)

                    by_group(sp, group)

                @block.gpsimd
                def _(pool):
                    def landed(slot, round):
                        pool.wait_ge(gi_gath[slot], 16 * SUBS * (turn_of(slot, round) + 1))
                        pool.nop().then_inc(gi_landed, 1)

                    def group(g, slot, round):
                        hold(pool, (gi_idx[slot], 16 * (turn_of(slot, round) + 1)), (gine_stored, 16 * (layer + 1)))
                        for j in range(SUBS):
                            pool.indirect_dma_start(
                                out=gath[:, slot, j, 0:D], out_offset=None, in_=table1,
                                in_offset=bass.IndirectOffsetOnAxis(ap=idx[:, slot, j:j + 1], axis=0)).then_inc(gi_gath[slot], 16)
                        if not (isinstance(g, int) and g == 0):
                            landed((slot - 1) % 4, round - (1 if slot == 0 else 0))
                        if isinstance(g, int) and g == GROUPS - 1:
                            landed(slot, round)

                    by_group(pool, group)

                @block.tensor
                def _(e):
                    def front(i, s, turn, s4, turn4):
                        n = done + i
                        e.wait_ge(gi_ea[s], 16 * (turn + 1))
                        for j in range(SUBS):
                            last = e.matmul(E[s][:, j * D:(j + 1) * D], ea[:, s, j * P:(j + 1) * P], gine_lin[:, :],
                                            start=True, stop=True)
                        last.then_inc(gi["e_ready"], 1)

                    def back(i, s, turn, s4, turn4):
                        n = done + i
                        e.wait_ge(gi["msg"], n + 1)
                        e.wait_ge(gi["hot_done"], n + 1)
                        e.wait_ge(gi["acc_done"], n)
                        for j in range(SUBS):
                            last = e.matmul(O[s], pm[:, s, j * P:(j + 1) * P], hot[:, s, j, :], start=(j == 0), stop=(j == SUBS - 1))
                        last.then_inc(gi["o_ready"], 1)

                    walk(e, front, back, layer=layer)

                @block.vector
                def _(v):
                    v.memset(acc, 0.0).then_inc(gi["cleared"], 1)
                    v.wait_ge(gi["cleared"], layer + 1)

                    def front(i, s, turn, s4, turn4):
                        n = done + i
                        if not isinstance(i, int) or i >= 2:
                            v.wait_ge(gi["o_ready"], done + i - 1)
                        v.tensor_tensor(hot[:, s, :, :], iota.unsqueeze(1).broadcast_to([P, SUBS, P]),
                                        rel_all[:, bass.ds(i, 1), :].rearrange("p a j -> p (a j)").unsqueeze(2).broadcast_to([P, SUBS, P]),
                                        ALU.is_equal).then_inc(gi["hot_done"], 1)
                        _, (g, slot) = nc.values_load_multi_w_load_instructions(
                            groups_blocks[0:1, bass.ds(i, 1), 0:2], engines=(mybir.EngineType.DVE,),
                            min_val=0, max_val=GROUPS - 1)
                        slot = nc.s_assert_within(slot, 0, 3)
                        v.wait_ge(gi_landed, layer * GROUPS + g + 1)
                        if not isinstance(i, int) or i >= 2:
                            v.wait_ge(gi["msg"], done + i - 1)
                        v.wait_ge(gi["e_ready"], n + 1)
                        v.tensor_tensor(vs[:, s, :].rearrange("p (j d) -> p j d", j=SUBS), E[s].rearrange("p (j d) -> p j d", j=SUBS),
                                        gath[:, bass.ds(slot, 1), :, 0:D].rearrange("p a j d -> p (a j) d"), ALU.add).then_inc(gi["added"], 1)

                    def back(i, s, turn, s4, turn4):
                        n = done + i
                        b = block_of(v, i)
                        v.wait_ge(gi["acc_done"], n + 1)
                        v.wait_ge(gi["o_ready"], n + 1)
                        a_b = acc[:, bass.ds(b * P, P)]
                        v.tensor_tensor(a_b, a_b, O[s], ALU.add).then_inc(gi["acc_done"], 1)

                    walk(v, front, back, layer=layer)

                @block.scalar
                def _(a):
                    def load(i, s):
                        g = group_of(a, i)
                        if not isinstance(i, int) or i >= 2:
                            a.wait_ge(gi["e_ready"], done + i - 1)
                        a.dma_start(ea[:, s, :], t["edge_attr"][bass.ds(g, 1), :, :].rearrange("a k e -> (a k) e")).then_inc(gi_ea[s], 16)

                    load(0, 0)

                    def item(i, s, turn, s4, turn4):
                        n = done + i
                        if not (isinstance(i, int) and i == ITEMS - 1):
                            load(i + 1, 1 - s)
                        if not isinstance(i, int) or i >= 2:
                            a.wait_ge(gi["o_ready"], n - 1)
                        a.wait_ge(gi["added"], n + 1)
                        a.activation(pm[:, s, :], vs[:, s, :], ACT.Relu).then_inc(gi["msg"], 1)

                    in_order(a, item, layer)

        def mlp_edges():
            acc = [ACC[:, h * NPAD:(h + 1) * NPAD] for h in range(2)]
            number = 2
            ea_in = [sem(f"mlp_ea_in{s}") for s in range(2)]
            cleared, hot_t_done, hot_done, g_ready, g_copied, h1_ready, h1_added, h1_done, h2_ready, h2_added, h2_done, o_ready, acc_done, deg_step = (
                sem(f"mlp_{k}") for k in ("cleared", "hot_t_done", "hot_done", "g_ready", "g_copied", "h1_ready", "h1_added", "h1_done", "h2_ready", "h2_added",
                                          "h2_done", "o_ready", "acc_done", "deg_step"))
            H1 = [psum[:, h, :] for h in range(2)]
            H2 = psum[:, 2:4, :].rearrange("p a n -> p (a n)").rearrange("p (j d) -> p j d", d=HID)
            O = psum[:, 4, 0:2 * P].rearrange("p (h n) -> p h n", h=2)
            G = [psum[:, 5 + h, :] for h in range(2)]
            h1 = pm
            h2a = TMP[:, 0:8, :].rearrange("p a d -> p (a d)").rearrange("p (j d) -> p j d", d=HID)
            h2 = TMP[:, 8:16, :].rearrange("p a d -> p (a d)").rearrange("p (j d) -> p j d", d=HID)
            w2 = [weight("L3_gnn_W2a"), weight("L3_gnn_W2b")]

            with nc.Block() as block:
                @block.sync
                def _(sp):
                    def item(i, s, turn, s4, turn4):
                        g = group_of(sp, i)
                        hold(sp, (gathered[s4], 16 * SUBS * turn4))
                        sp.dma_start(idx[:, s4, :], idx_all[:, bass.ds(i, 1), :].rearrange("p a j -> p (a j)")).then_inc(idx_in[s4], 16)
                        hold(sp, (hot_t_done, i - 1))
                        sp.dma_start(rel[:, s, :], rel_rows[bass.ds(i, 1), :].broadcast_to([P, GROUP_EDGES])).then_inc(rel_in[s], 16)
                        hold(sp, (h1_ready, 2 * (i - 1)))
                        sp.dma_start(ea[:, s, :], t["edge_attr"][bass.ds(g, 1), :, :].rearrange("a k e -> (a k) e")).then_inc(ea_in[s], 16)

                    in_order(sp, item, number)

                @block.gpsimd
                def _(pool):
                    def item(i, s, turn, s4, turn4):
                        hold(pool, (idx_in[s4], 16 * (turn4 + 1)),
                             (h1_ready, 2 * (i - 3)))
                        for j in range(SUBS):
                            pool.indirect_dma_start(
                                out=gath[:, s4, j, :], out_offset=None, in_=table,
                                in_offset=bass.IndirectOffsetOnAxis(ap=idx[:, s4, j:j + 1], axis=0)).then_inc(gathered[s4], 16)

                    in_order(pool, item, number)

                @block.tensor
                def _(e):
                    def front(i, s, turn, s4, turn4):
                        e.wait_ge(gathered[s4], 16 * SUBS * (turn4 + 1))
                        for h in range(2):
                            for j in range(SUBS):
                                last = e.transpose(G[h][:, j * P:(j + 1) * P], gath[:, s4, j, h * D:(h + 1) * D], ident)
                            last.then_inc(g_ready, 1)
                        b = block_of(e, i)
                        hold(e, (ea_in[s], 16 * (turn + 1 - number * PAIRS)),
                             (hot_t_done, i + 1))
                        for h in range(2):
                            for k in range(SPLIT):
                                e.matmul(H1[h], XR[:, bass.ds(b, 1), k, h * D:(h + 1) * D].rearrange("p a d -> p (a d)"), hot_t[:, s, :],
                                         start=(k == 0), stop=False)
                            e.matmul(H1[h], edge_w1[:, h * D:(h + 1) * D], ea[:, s, :], start=False, stop=True).then_inc(h1_ready, 1)

                    def mid(i, s, turn, s4, turn4):
                        e.wait_ge(h1_done, 2 * (i + 1))
                        for j in range(SUBS):
                            for h in range(2):
                                last = e.matmul(H2[:, j, :], h1[:, h, j * P:(j + 1) * P], w2[h], start=(h == 0), stop=(h == 1))
                        last.then_inc(h2_ready, 1)

                    def back(i, s, turn, s4, turn4):
                        e.wait_ge(h2_done, i + 1)
                        e.wait_ge(hot_done, i + 1)
                        wait(e, acc_done, i)
                        for h in range(2):
                            for j in range(SUBS):
                                last = e.matmul(O[:, h, :], h2[:, j, h * D:(h + 1) * D], hot[:, s, j, :], start=(j == 0), stop=(j == SUBS - 1))
                        last.then_inc(o_ready, 1)

                    walk(e, front, back, mid, layer=number)

                @block.scalar
                def _(a):
                    def front(i, s, turn, s4, turn4):
                        for h in range(2):
                            wait(a, h1_done, 2 * (i - 1) + h + 1)
                            a.wait_ge(g_ready, 2 * i + h + 1)
                            a.activation(vs[:, h, :], G[h], ACT.Copy).then_inc(g_copied, 1)
                        for h in range(2):
                            wait(a, h2_ready, i)
                            a.wait_ge(h1_added, 2 * i + h + 1)
                            a.activation(h1[:, h, :], vs[:, h, :], ACT.Relu).then_inc(h1_done, 1)

                    def mid(i, s, turn, s4, turn4):
                        wait(a, o_ready, i)
                        a.wait_ge(h2_added, i + 1)
                        a.activation(h2, h2a, ACT.Relu).then_inc(h2_done, 1)

                    walk(a, front, mid=mid, layer=number)

                @block.vector
                def _(v):
                    v.memset(ACC[:, :], 0.0)
                    v.memset(stat[:, 0, :], 0.0).then_inc(cleared, 1)
                    v.wait_ge(cleared, 1)

                    def make_hot_t(i, s, turn):
                        v.wait_ge(rel_in[s], 16 * (turn + 1))
                        wait(v, deg_step, 2 * i - 2)
                        wait(v, h1_ready, 2 * i - 2)
                        v.tensor_scalar(hot_t[:, s, :], rel[:, s, :], row, None, ALU.is_equal).then_inc(hot_t_done, 1)

                    def front(i, s, turn, s4, turn4):
                        for h in range(2):
                            v.wait_ge(g_copied, 2 * i + h + 1)
                            v.wait_ge(h1_ready, 2 * i + h + 1)
                            v.tensor_tensor(vs[:, h, :], H1[h], vs[:, h, :], ALU.add).then_inc(h1_added, 1)
                        b = block_of(v, i)
                        v.wait_ge(hot_t_done, i + 1)
                        wait(v, deg_step, 2 * i)
                        v.tensor_reduce(MI[:, 0:1], hot_t[:, s, :], AX, ALU.add).then_inc(deg_step, 1)
                        v.wait_ge(deg_step, 2 * i + 1)
                        d_b = stat[:, 0, bass.ds(b, 1)]
                        v.tensor_tensor(d_b, d_b, MI[:, 0:1], ALU.add).then_inc(deg_step, 1)
                        if not (isinstance(i, int) and i == ITEMS - 1):
                            make_hot_t(i + 1, 1 - s, turn + s)
                        wait(v, o_ready, i - 1)
                        v.tensor_tensor(hot[:, s, :, :], iota.unsqueeze(1).broadcast_to([P, SUBS, P]),
                                        rel_all[:, bass.ds(i, 1), :].rearrange("p a j -> p (a j)").unsqueeze(2).broadcast_to([P, SUBS, P]),
                                        ALU.is_equal).then_inc(hot_done, 1)

                    def mid(i, s, turn, s4, turn4):
                        wait(v, h2_done, i)
                        v.wait_ge(h2_ready, i + 1)
                        b2 = bias("L3_gnn_b2").unsqueeze(1).broadcast_to([P, SUBS, HID])
                        v.tensor_tensor(h2a, H2, b2, ALU.add).then_inc(h2_added, 1)

                    def back(i, s, turn, s4, turn4):
                        b = block_of(v, i)
                        wait(v, acc_done, i)
                        v.wait_ge(o_ready, i + 1)
                        for h in range(2):
                            a_b = acc[h][:, bass.ds(b * P, P)]
                            last = v.tensor_tensor(a_b, a_b, O[:, h, :], ALU.add)
                        last.then_inc(acc_done, 1)

                    make_hot_t(0, 0, number * PAIRS)
                    walk(v, front, back, mid, layer=number)

        layernorm(X[:, :, :], Y[:, :, :], gamma=bias("L0_gnn_gamma"), beta=bias("L0_gnn_beta"), relu=True)
        transposes(flat(Y), XT)
        tables("tab0", 2 * D, weight("L0_gnn_Wl"), bias("L0_gnn_bl"), weight("L0_gnn_Wr"), bias("L0_gnn_br"), table,
               extra=(weight("L0_gnn_res_W"), bias("L0_gnn_bias")))
        gat_edges(0, HEADS, table, (0, 1), with_weight=False)

        def mean_of_heads(v, step):
            acc = ACC[:, :].rearrange("p (b h d) -> p b h d", h=2, d=D)
            step(v.tensor_scalar(zsum[:, :, :], zsum[:, :, :], 1e-16, None, ALU.add))
            step(v.reciprocal(zsum[:, :, :], zsum[:, :, :]))
            for h in range(2):
                z = zsum[:, :, h:h + 1].broadcast_to([P, NODE_BLOCKS, D])
                step(v.tensor_tensor(acc[:, :, h, :], acc[:, :, h, :], z, ALU.mult))
            step(v.tensor_tensor(TMP[:, :, :], acc[:, :, 0, :], acc[:, :, 1, :], ALU.add))
            step(v.scalar_tensor_tensor(flat(Y), flat(TMP), 0.5, flat(Y), ALU.mult, ALU.add))

        layernorm(Y[:, :, :], X[:, :, :], prep=mean_of_heads, prep_steps=6)

        transposes(flat(X), XT)
        tables("tab1", D, weight("L1_gnn_Wl"), bias("L1_gnn_bl"), weight("L1_gnn_Wr"), bias("L1_gnn_br"), table1)
        gat_edges(1, 1, table1, (2,), with_weight=True)

        def gat1_sum():
            dve = sem("gat1_sum")
            acc = ACC[:, 0:NPAD].rearrange("p (b d) -> p b d", d=D)
            with nc.Block() as block:
                @block.vector
                def _(v):
                    n = [0]

                    def step(ins):
                        n[0] += 1
                        ins.then_inc(dve, 1)
                        v.wait_ge(dve, n[0])

                    step(v.tensor_scalar(zsum[:, :, :], zsum[:, :, :], 1e-16, None, ALU.add))
                    step(v.reciprocal(zsum[:, :, :], zsum[:, :, :]))
                    step(v.tensor_tensor(Y[:, :, :], acc, zsum[:, :, 0:1].broadcast_to([P, NODE_BLOCKS, D]), ALU.mult))
                    step(v.tensor_tensor(Y[:, :, :], Y[:, :, :], X[:, :, :], ALU.add))
                    step(v.tensor_tensor(Y[:, :, :], Y[:, :, :], over_blocks(bias("L1_gnn_bias_out")), ALU.add))

        def batchnorm(name, h, gamma, beta, func, sems=None, layer=0, scratch_out=None):
            dve, act = sems or (sem(name + "_dve"), sem(name + "_act"))
            base_v, base_a = layer * 7, layer * 3
            m = small[:, 6, 0:1]
            nm = small[:, 6, 1:2]
            va = small[:, 7, 0:1]
            sd = small[:, 7, 1:2]
            sc = small[:, 4, 0:1]
            sh = small[:, 4, 1:2]
            with nc.Block() as block:
                @block.vector
                def _(v):
                    n = [0]

                    def step(ins):
                        n[0] += 1
                        ins.then_inc(dve, 1)
                        v.wait_ge(dve, base_v + n[0])

                    step(v.tensor_reduce(m, h[:, 0:NODES], AX, ALU.add))
                    step(v.tensor_scalar(nm, m, -1.0 / NODES, None, ALU.mult))
                    v.wait_ge(act, base_a + 1)
                    step(v.tensor_scalar(va, va, 1.0 / NODES, 1e-5, ALU.mult, ALU.add))
                    v.wait_ge(act, base_a + 2)
                    step(v.reciprocal(sd, sd))
                    step(v.tensor_tensor(sc, sd, gamma, ALU.mult))
                    step(v.tensor_tensor(sh, sc, nm, ALU.mult))
                    v.tensor_tensor(sh, sh, beta, ALU.add).then_inc(dve, 1)

                @block.scalar
                def _(a):
                    a.wait_ge(dve, base_v + 2)
                    a.activation(flat(TMP)[:, 0:NODES], h[:, 0:NODES], ACT.Square, bias=nm, accum_out=va).then_inc(act, 1)
                    a.wait_ge(dve, base_v + 3)
                    a.activation(sd, va, ACT.Sqrt).then_inc(act, 1)
                    a.wait_ge(dve, base_v + 7)
                    a.activation(h, h, func, bias=sh, scale=sc).then_inc(act, 1)

        gat1_sum()
        HT = ACC[:, 0:NPAD]
        transposes(flat(Y), HT)

        def gelu():
            done = sem("gelu_done")
            with nc.Block() as block:
                @block.scalar
                def _(a):
                    a.activation(HT, HT, ACT.Gelu).then_inc(done, 1)
                    a.wait_ge(done, 1)

        gelu()
        batchnorm("bn1", HT, col("bn_gamma"), col("bn_beta"), ACT.Identity)
        transposes(HT, flat(Y))

        def add_residual(v, step):
            step(v.tensor_tensor(Y[:, :, :], Y[:, :, :], X[:, :, :], ALU.add))

        layernorm(Y[:, :, :], X[:, :, :], prep=add_residual, prep_steps=1)

        transposes(flat(X), XT)
        gine_loads, gine_tab, gine_h = (sem(f"gine_{k}") for k in ("loads", "tab", "h"))
        mlp1, mlp1_done, mlp2, mlp2_done = (sem(f"gine_{k}") for k in ("mlp1", "mlp1_done", "mlp2", "mlp2_done"))
        bn_sems = (sem("gine_bn_dve"), sem("gine_bn_act"))
        back_sems = (sem("gine_turned"), sem("gine_taken"))
        Z = XR[:, :, :, :].rearrange("p b k d -> p (b k d)").bitcast(F32)[:, 0:NPAD]
        Z3 = Z.rearrange("p (b d) -> p b d", d=D)
        NCOL = 400
        NCH = NPAD // NCOL

        def gine_node_to_table(layer):
            with nc.Block() as block:
                @block.sync
                def _(sp):
                    one = bass.ds(layer, 1)
                    sp.dma_start(gine_w[:, :, :], t["gine_w"][:, one, :, :].rearrange("p a k d -> p (a k) d")).then_inc(gine_loads, 16)
                    sp.dma_start(gine_lin[:, :], t["gine_lin"][one, :, :].rearrange("a k d -> (a k) d")).then_inc(gine_loads, 16)
                    sp.dma_start(gine_blin[:, :], t["gine_blin"][one, :].broadcast_to([P, D])).then_inc(gine_loads, 16)
                    sp.dma_start(gine_cols[:, :], t["gine_cols"][:, one, :].rearrange("p a k -> p (a k)")).then_inc(gine_loads, 16)
                    sp.wait_ge(gine_tab, layer + 1)
                    sp.dma_start(table1.rearrange("(b p) d -> p b d", p=P), TMP[:, :, :]).then_inc(gine_stored, 16)

                @block.vector
                def _(v):
                    v.wait_ge(gine_loads, 64 * (layer + 1))
                    v.tensor_tensor(TMP[:, :, :], Z3, over_blocks(gine_blin[:, :]), ALU.add).then_inc(gine_tab, 1)

        def gine_mlp(layer):
            h = ACC[:, 0:NPAD]
            u = ACC[:, NPAD:2 * NPAD]
            with nc.Block() as block:
                @block.vector
                def _(v):
                    v.tensor_tensor(h, h, XT[:, :], ALU.add).then_inc(gine_h, 1)

                @block.tensor
                def _(e):
                    with e.Fori(0, NCH) as c:
                        e.wait_ge(gine_h, layer + 1)
                        e.wait_ge(mlp1_done, layer * NCH + c)
                        e.matmul(psum[:, 0, 0:NCOL], gine_w[:, 0, :], h[:, bass.ds(c * NCOL, NCOL)], start=True, stop=True).then_inc(mlp1, 1)
                        e.wait_ge(mlp2_done, layer * NCH + c)
                        e.wait_ge(mlp1_done, layer * NCH + c + 1)
                        e.matmul(psum[:, 1, 0:NCOL], gine_w[:, 1, :], u[:, bass.ds(c * NCOL, NCOL)], start=True, stop=True).then_inc(mlp2, 1)

                @block.scalar
                def _(a):
                    with a.Fori(0, NCH) as c:
                        at = bass.ds(c * NCOL, NCOL)
                        hold(a, (mlp1, layer * NCH + c + 1))
                        a.activation(u[:, at], psum[:, 0, 0:NCOL], ACT.Relu, bias=gine_cols[:, 0:1]).then_inc(mlp1_done, 1)
                        hold(a, (gine_h, layer + 1),
                             (mlp2, layer * NCH + c + 1))
                        a.activation(XT[:, at], psum[:, 1, 0:NCOL], ACT.Identity, bias=gine_cols[:, 1:2]).then_inc(mlp2_done, 1)

        def gine_first():
            done = sem("gine_first")
            with nc.Block() as block:
                @block.vector
                def _(v):
                    v.tensor_copy(Z3, X[:, :, :]).then_inc(done, 1)
                    v.memset(small[:, 7, :], 0.0).then_inc(gi["acc_done"], 1)

        gine_first()
        with nc.Fori(0, GINE_LAYERS) as layer:
            gine_node_to_table(layer)
            gine_edges(layer)
            gine_mlp(layer)
            batchnorm("gine_bn", XT[:, :], gine_cols[:, 2:3], gine_cols[:, 3:4], ACT.Relu, sems=bn_sems, layer=layer)
            transposes(XT, Z, *back_sems, base=layer * (NODE_BLOCKS // CH))

        def add_gine(v, step):
            step(v.tensor_tensor(Y[:, :, :], Z3, X[:, :, :], ALU.add))

        layernorm(Y[:, :, :], X[:, :, :], prep=add_gine, prep_steps=1)

        transposes(flat(X), XT)
        tables("tab3", HID, weight("L3_gnn_W1a"), bias("L3_gnn_b1"), weight("L3_gnn_W1b"), None, table)
        mlp_edges()

        def node_mlp():
            made, taken, diag, dsum = (sem(f"node_{k}") for k in ("made", "taken", "diag", "dsum"))
            aggr = XR[:, :, :, :].rearrange("p b k d -> p (b k d)").bitcast(F32)[:, 0:NPAD]
            hid = [XR[:, :, :, :].rearrange("p b k d -> p (b k d)").bitcast(F32)[:, NPAD * (1 + h):NPAD * (2 + h)] for h in range(2)]
            sums = [ACC[:, h * NPAD:(h + 1) * NPAD] for h in range(2)]
            b3 = bias("L3_gnn_b3")
            w3 = [weight("L3_gnn_W3a"), weight("L3_gnn_W3b")]
            with nc.Block() as block:
                @block.vector
                def _(v):
                    for b in range(NODE_BLOCKS):
                        wait(v, made, b - 1)
                        v.tensor_scalar(lk[:, b % 2, 0:P], ident, stat[:, 0, b:b + 1], None, ALU.mult).then_inc(diag, 1)

                @block.tensor
                def _(e):
                    for b in range(NODE_BLOCKS):
                        e.wait_ge(diag, b + 1)
                        wait(e, taken, b - 1)
                        o = psum[:, b % 2, 0:P]
                        for h in range(2):
                            e.matmul(o, w3[h], sums[h][:, b * P:(b + 1) * P], start=(h == 0), stop=False)
                        e.matmul(o, b3, lk[:, b % 2, 0:P], start=False, stop=True).then_inc(made, 1)

                @block.scalar
                def _(a):
                    for b in range(NODE_BLOCKS):
                        a.wait_ge(made, b + 1)
                        a.activation(aggr[:, b * P:(b + 1) * P], psum[:, b % 2, 0:P], ACT.Copy).then_inc(taken, 1)

            m1, m1_done, m2, m2_done = (sem(f"node_{k}") for k in ("m1", "m1_done", "m2", "m2_done"))
            wn1a, wn1b = weight("L3_gnn_Wn1a"), weight("L3_gnn_Wn1b")
            wn2 = [weight("L3_gnn_Wn2a"), weight("L3_gnn_Wn2b")]
            with nc.Block() as block:
                @block.tensor
                def _(e):
                    with e.Fori(0, NCH) as c:
                        at = bass.ds(c * NCOL, NCOL)
                        for h in range(2):
                            e.wait_ge(m1_done, 2 * c)
                            o = psum[:, h, 0:NCOL]
                            e.matmul(o, wn1a[:, h * D:(h + 1) * D], XT[:, at], start=True, stop=False)
                            e.matmul(o, wn1b[:, h * D:(h + 1) * D], aggr[:, at], start=False, stop=True).then_inc(m1, 1)
                        e.wait_ge(m2_done, c)
                        for h in range(2):
                            e.wait_ge(m1_done, 2 * c + h + 1)
                            last = e.matmul(psum[:, 2, 0:NCOL], wn2[h], hid[h][:, at], start=(h == 0), stop=(h == 1))
                        last.then_inc(m2, 1)

                @block.scalar
                def _(a):
                    with a.Fori(0, NCH) as c:
                        at = bass.ds(c * NCOL, NCOL)
                        for h in range(2):
                            hold(a, (m1, 2 * c + h + 1))
                            a.activation(hid[h][:, at], psum[:, h, 0:NCOL], ACT.Relu, bias=col("bn1a" if h == 0 else "bn1b")).then_inc(m1_done, 1)
                        hold(a, (m2, c + 1))
                        a.activation(HT[:, at], psum[:, 2, 0:NCOL], ACT.Identity, bias=col("bn2")).then_inc(m2_done, 1)

        node_mlp()
        transposes(HT, flat(Y))
        layernorm(Y[:, :, :], Y[:, :, :], gamma=bias("L3_gnn_gamma"), beta=bias("L3_gnn_beta"), prep=add_residual, prep_steps=1)
        layernorm(Y[:, :, :], Y[:, :, :], prep=add_residual, prep_steps=1)

        out_done = sem("out_done")
        with nc.Block() as block:
            @block.sync
            def _(sp):
                full = NODES // P
                sp.dma_start(t["out"][0:full * P, :].rearrange("(b p) d -> p b d", p=P), Y[:, 0:full, :]).then_inc(out_done, 16)
                sp.dma_start(t["out"][full * P:NODES, :], Y[0:NODES - full * P, full, :]).then_inc(out_done, 16)
                sp.wait_ge(out_done, 32)


def kernel(**inputs):
    import concourse.bacc as bacc
    from concourse.bass_utils import run_bass_kernel_spmd

    a = {k: np.asarray(v) for k, v in inputs.items()}
    pad = GROUPS * GROUP_EDGES - EDGES

    def padded(x, fill):
        return np.concatenate([x, np.full((pad,) + x.shape[1:], fill, x.dtype)])

    def spread(v):
        return np.broadcast_to(v.reshape(1, -1), (P, v.size))

    consts = np.zeros((P, C_WIDTH), np.float32)
    consts[:, C_IDENT:C_IDENT + P] = np.eye(P)
    consts[:, C_IOTA:C_IOTA + P] = np.arange(P)
    consts[:, C_ROW] = np.arange(P)
    consts[:, C_PICK:] = np.arange(P)[:, None] % SPLIT == np.arange(SPLIT)
    w1, w2, w3 = a["L3_gnn_W1"], a["L3_gnn_W2"], a["L3_gnn_W3"]
    wn1, wn2 = a["L3_gnn_Wn1"], a["L3_gnn_Wn2"]
    a.update({"L3_gnn_W1a": w1[0:D], "L3_gnn_W1b": w1[D:2 * D], "L3_gnn_W2a": w2[0:D], "L3_gnn_W2b": w2[D:],
              "L3_gnn_W3a": w3[0:D], "L3_gnn_W3b": w3[D:], "L3_gnn_Wn1a": wn1[0:D], "L3_gnn_Wn1b": wn1[D:],
              "L3_gnn_Wn2a": wn2[0:D], "L3_gnn_Wn2b": wn2[D:]})
    dst = padded(a["dst"].astype(np.int32), NPAD).reshape(GROUPS, GROUP_EDGES)
    src = padded(a["src"].astype(np.int32), 0).reshape(GROUPS, GROUP_EDGES)
    bn1 = a["L3_gnn_bn1"]
    arrays = {
        "consts": consts,
        "x": np.concatenate([a["x"], np.zeros((NPAD - NODES, D), np.float32)]),
        "dst": dst,
        "dst_last": np.ascontiguousarray(dst[:, -1]).reshape(1, GROUPS),
        "src": src,
        "src_by_group": src.reshape(GROUPS, SUBS, P).transpose(0, 2, 1),
        "edge_weight": padded(a["edge_weight1"][:, 0], 0).reshape(GROUPS, GROUP_EDGES),
        "edge_attr": np.ascontiguousarray(padded(a["edge_attr_32"], 0).reshape(GROUPS, GROUP_EDGES, EDGE_D).transpose(0, 2, 1)),
        "biases": np.concatenate([spread(a[n]) for n, _ in BIASES], axis=1),
        "weights": np.concatenate([a[n] for n, _ in WEIGHTS], axis=1),
        "cols": np.stack([a["L0_gnn_att"][0], a["L0_gnn_att"][1], a["L1_gnn_att"], a["L1_gnn_bn_gamma"],
                          a["L1_gnn_bn_beta"], bn1[0:D], bn1[D:], a["L3_gnn_bn2"]], axis=1),
        "edge_w1": w1[2 * D:],
        "we": a["L1_gnn_We"],
        "gine_w": np.stack([a["L2_gnn_W1"], a["L2_gnn_W2"]]).transpose(2, 1, 0, 3),
        "gine_lin": a["L2_gnn_W_lin"],
        "gine_blin": a["L2_gnn_b_lin"],
        "gine_cols": np.stack([a["L2_gnn_b1"], a["L2_gnn_b2"], a["L2_gnn_gamma"], a["L2_gnn_beta"]]).transpose(2, 1, 0),
    }
    arrays = {k: np.ascontiguousarray(v) for k, v in arrays.items()}
    nc = bacc.Bacc("TRN2", target_bir_lowering=False, num_devices=1)
    t = {k: nc.dram_tensor(f"in_{k}", v.shape, mybir.dt.from_np(v.dtype), kind="ExternalInput").ap()
         for k, v in arrays.items()}
    t["out"] = nc.dram_tensor("out", (NODES, D), F32, kind="ExternalOutput").ap()
    build(nc, t)
    r = run_bass_kernel_spmd(nc, [{f"in_{k}": v for k, v in arrays.items()}], core_ids=[0])
    return r.results[0]["out"]
```
